# Optimizing a Trainium2 kernel written in Bass

```python
import numpy as np
import jax
import jax.numpy as jnp

def _softmax(x, axis=-1):
    return jax.nn.softmax(x, axis=axis)

def _gelu(x):
    return jax.nn.gelu(x, approximate=True)

def _silu(x):
    return jax.nn.silu(x)

def _sigmoid(x):
    return jax.nn.sigmoid(x)

def _layernorm(x, axis=-1, eps=1e-05):
    m = jnp.mean(x, axis=axis, keepdims=True)
    v = jnp.var(x, axis=axis, keepdims=True)
    return (x - m) / jnp.sqrt(v + eps)

def _scatter_add(tgt, idx, src, axis=0):
    return tgt.at[idx].add(src)

def _segment_sum(src, seg, n):
    return jax.ops.segment_sum(src, seg, n)
kernel_name = 'mk_cond_resid_d2_seqx_r8_2b165e'

def setup_inputs(seed: int=0):
    np.random.seed(seed)
    _w = jnp.asarray

    def _rec_inputs():
        import jax
        import jax.numpy as jnp
        _rk = jax.random.key(seed)
        x = -0.000125 + 0.9999 * jax.random.normal(jax.random.fold_in(_rk, 1), (8, 256, 128), jnp.float32)
        _lenS = 256 - jax.random.randint(jax.random.fold_in(_rk, 7), (8,), 0, max(1, 256 // 4) + 1, jnp.int32)
        _lenS2 = 256 - jax.random.randint(jax.random.fold_in(_rk, 8), (8,), 0, max(1, 256 // 4) + 1, jnp.int32)
        cond_1024 = -0.00493535 + 1.00056 * jax.random.normal(jax.random.fold_in(_rk, 11), (8, 128), jnp.float32)
        return (x, cond_1024)
    x, cond_1024 = _rec_inputs()

    def _L0_cond_setup():
        import jax, jax.numpy as jnp
        from jax import lax
        import numpy as np
        B, T, U = (64, 64, 128)
        key = jax.random.key(seed)
        k1, k2, k3 = jax.random.split(key, 3)
        x = jax.random.normal(k1, (B, T, U), dtype=jnp.float32)
        h0 = jax.random.normal(k2, (B, U), dtype=jnp.float32)
        limit = float(np.sqrt(6.0 / (2 * U + 2 * U)))
        weight = jax.random.uniform(k3, (2 * U, 2 * U), minval=-limit, maxval=limit, dtype=jnp.float32)
        bias = jnp.zeros((2 * U,), dtype=jnp.float32)
        return {'x': x, 'h0': h0, 'weight': weight, 'bias': bias}
    _L0_cond_all = _L0_cond_setup()
    _L0_cond_in = {k: v for k, v in _L0_cond_all.items() if k in ('weight', 'bias')}
    del _L0_cond_all

    def _L1_cond_setup():
        import math
        import jax, jax.numpy as jnp
        import numpy as np
        EPS = 1e-07
        MAX_TANH_ARG = 1.0 - 1e-05

        def _norm(x):
            return jnp.sqrt(jnp.sum(x * x, axis=-1, keepdims=True)).clip(EPS)

        def logmap0(x):
            n = _norm(x)
            return jnp.arctanh(jnp.clip(n, EPS, MAX_TANH_ARG)) * x / n

        def expmap0(v):
            n = _norm(v)
            return jnp.tanh(n) * v / n

        def mobius_add(x, y):
            x2 = jnp.sum(x * x, -1, keepdims=True)
            y2 = jnp.sum(y * y, -1, keepdims=True)
            xy = jnp.sum(x * y, -1, keepdims=True)
            num = (1 + 2 * xy + y2) * x + (1 - x2) * y
            den = (1 + 2 * xy + x2 * y2).clip(EPS)
            return num / den

        def plin(x, w, b):
            return expmap0(logmap0(x) @ w + b)

        def layer_norm(x, eps=1e-06):
            m = x.mean(-1, keepdims=True)
            v = ((x - m) ** 2).mean(-1, keepdims=True)
            return (x - m) / jnp.sqrt(v + eps)

        def _beta(a, b):
            return math.exp(math.lgamma(a) + math.lgamma(b) - math.lgamma(a + b))
        D, H, FF = (128, 16, 512)
        HD = D // H
        BETA_N = _beta(D / 2, 0.5)
        BETA_H = _beta(HD / 2, 0.5)

        def _to_heads(p):
            B, S, _ = p.shape
            t = logmap0(p).reshape(B, S, H, HD) * (BETA_H / BETA_N)
            return expmap0(jnp.transpose(t, (0, 2, 1, 3)))

        def _from_heads(ph):
            B, _, S, _ = ph.shape
            t = logmap0(ph) * (BETA_N / BETA_H)
            t = jnp.transpose(t, (0, 2, 1, 3)).reshape(B, S, D)
            return expmap0(t)
        key = jax.random.key(seed)
        ks = jax.random.split(key, 20)
        B, S = (4, 128)
        x = expmap0(0.02 * jax.random.normal(ks[0], (B, S, D), jnp.float32))
        t_emb = jax.random.normal(ks[1], (B, 1, D), jnp.float32)
        g = lambda k, sh: 0.02 * jax.random.normal(k, sh, jnp.float32)
        return {'x': x, 't_emb': t_emb, 'w_q': g(ks[2], (D, D)), 'b_q': jnp.zeros((D,), jnp.float32), 'w_k': g(ks[3], (D, D)), 'b_k': jnp.zeros((D,), jnp.float32), 'w_v': g(ks[4], (D, D)), 'b_v': jnp.zeros((D,), jnp.float32), 'w_o': g(ks[5], (D, D)), 'b_o': jnp.zeros((D,), jnp.float32), 'w_f1': g(ks[6], (D, FF)), 'b_f1': jnp.zeros((FF,), jnp.float32), 'w_f2': g(ks[7], (FF, D)), 'b_f2': jnp.zeros((D,), jnp.float32), 'w_ada': g(ks[8], (D, 6 * D)), 'b_ada': jnp.zeros((6 * D,), jnp.float32)}
    _L1_cond_all = _L1_cond_setup()
    _L1_cond_in = {k: v for k, v in _L1_cond_all.items() if k in ('w_q', 'b_q', 'w_k', 'b_k', 'w_v', 'b_v', 'w_o', 'b_o', 'w_f1', 'b_f1', 'w_f2', 'b_f2', 'w_ada', 'b_ada')}
    del _L1_cond_all
    return {'x': x, 'cond_1024': cond_1024, 'L0_cond_weight': _L0_cond_in['weight'], 'L0_cond_bias': _L0_cond_in['bias'], 'L1_cond_w_q': _L1_cond_in['w_q'], 'L1_cond_b_q': _L1_cond_in['b_q'], 'L1_cond_w_k': _L1_cond_in['w_k'], 'L1_cond_b_k': _L1_cond_in['b_k'], 'L1_cond_w_v': _L1_cond_in['w_v'], 'L1_cond_b_v': _L1_cond_in['b_v'], 'L1_cond_w_o': _L1_cond_in['w_o'], 'L1_cond_b_o': _L1_cond_in['b_o'], 'L1_cond_w_f1': _L1_cond_in['w_f1'], 'L1_cond_b_f1': _L1_cond_in['b_f1'], 'L1_cond_w_f2': _L1_cond_in['w_f2'], 'L1_cond_b_f2': _L1_cond_in['b_f2'], 'L1_cond_w_ada': _L1_cond_in['w_ada'], 'L1_cond_b_ada': _L1_cond_in['b_ada']}

def reference(x, cond_1024, L0_cond_weight, L0_cond_bias, L1_cond_w_q, L1_cond_b_q, L1_cond_w_k, L1_cond_b_k, L1_cond_w_v, L1_cond_b_v, L1_cond_w_o, L1_cond_b_o, L1_cond_w_f1, L1_cond_b_f1, L1_cond_w_f2, L1_cond_b_f2, L1_cond_w_ada, L1_cond_b_ada):
    import jax
    import jax.numpy as jnp

    def _L0_cond_ref(x, h0, weight, bias):
        import jax, jax.numpy as jnp
        from jax import lax
        import numpy as np
        B, T, U = (64, 64, 128)
        'UGRNN cell scanned over time. x:[B,T,U], h0:[B,U] -> outputs [B,T,U].'
        units = h0.shape[-1]

        def step(h, xt):
            cell_inputs = jnp.concatenate([xt, h], axis=-1)
            m = cell_inputs @ weight + bias
            g_act = m[:, :units]
            c_act = m[:, units:]
            c = jnp.tanh(c_act)
            g = jax.nn.sigmoid(g_act + 1.0)
            h_new = g * h + (1.0 - g) * c
            return (h_new, h_new)
        xs = jnp.swapaxes(x, 0, 1)
        _, ys = lax.scan(step, h0, xs)
        return jnp.swapaxes(ys, 0, 1)

    def _L1_cond_ref(x, t_emb, w_q, b_q, w_k, b_k, w_v, b_v, w_o, b_o, w_f1, b_f1, w_f2, b_f2, w_ada, b_ada):
        import math
        import jax, jax.numpy as jnp
        import numpy as np
        EPS = 1e-07
        MAX_TANH_ARG = 1.0 - 1e-05

        def _norm(x):
            return jnp.sqrt(jnp.sum(x * x, axis=-1, keepdims=True)).clip(EPS)

        def logmap0(x):
            n = _norm(x)
            return jnp.arctanh(jnp.clip(n, EPS, MAX_TANH_ARG)) * x / n

        def expmap0(v):
            n = _norm(v)
            return jnp.tanh(n) * v / n

        def mobius_add(x, y):
            x2 = jnp.sum(x * x, -1, keepdims=True)
            y2 = jnp.sum(y * y, -1, keepdims=True)
            xy = jnp.sum(x * y, -1, keepdims=True)
            num = (1 + 2 * xy + y2) * x + (1 - x2) * y
            den = (1 + 2 * xy + x2 * y2).clip(EPS)
            return num / den

        def plin(x, w, b):
            return expmap0(logmap0(x) @ w + b)

        def layer_norm(x, eps=1e-06):
            m = x.mean(-1, keepdims=True)
            v = ((x - m) ** 2).mean(-1, keepdims=True)
            return (x - m) / jnp.sqrt(v + eps)

        def _beta(a, b):
            return math.exp(math.lgamma(a) + math.lgamma(b) - math.lgamma(a + b))
        D, H, FF = (128, 16, 512)
        HD = D // H
        BETA_N = _beta(D / 2, 0.5)
        BETA_H = _beta(HD / 2, 0.5)

        def _to_heads(p):
            B, S, _ = p.shape
            t = logmap0(p).reshape(B, S, H, HD) * (BETA_H / BETA_N)
            return expmap0(jnp.transpose(t, (0, 2, 1, 3)))

        def _from_heads(ph):
            B, _, S, _ = ph.shape
            t = logmap0(ph) * (BETA_N / BETA_H)
            t = jnp.transpose(t, (0, 2, 1, 3)).reshape(B, S, D)
            return expmap0(t)
        ada = t_emb @ w_ada + b_ada
        sh_msa, sc_msa, g_msa, sh_mlp, sc_mlp, g_mlp = jnp.split(ada, 6, axis=-1)
        residual = x
        xn = layer_norm(logmap0(x))
        xm = expmap0(xn * (1 + sc_msa) + sh_msa)
        q = _to_heads(plin(xm, w_q, b_q))
        k = _to_heads(plin(xm, w_k, b_k))
        v = _to_heads(plin(xm, w_v, b_v))
        qt, kt, vt = (logmap0(q), logmap0(k), logmap0(v))
        scores = jnp.einsum('bhqd,bhkd->bhqk', qt, kt) / math.sqrt(HD)
        attn = jax.nn.softmax(scores, axis=-1)
        out_h = expmap0(jnp.einsum('bhqk,bhkd->bhqd', attn, vt))
        attn_out = plin(_from_heads(out_h), w_o, b_o)
        attn_t = g_msa * logmap0(attn_out)
        x = mobius_add(residual, expmap0(attn_t))
        residual = x
        xn = layer_norm(logmap0(x))
        xm = expmap0(xn * (1 + sc_mlp) + sh_mlp)
        ff = plin(plin(xm, w_f1, b_f1), w_f2, b_f2)
        ff_t = g_mlp * logmap0(ff)
        return mobius_add(residual, expmap0(ff_t))
    x = x + _L0_cond_ref(x, cond_1024, L0_cond_weight, L0_cond_bias)
    x = x + _L1_cond_ref(x, cond_1024[:, None, :], L1_cond_w_q, L1_cond_b_q, L1_cond_w_k, L1_cond_b_k, L1_cond_w_v, L1_cond_b_v, L1_cond_w_o, L1_cond_b_o, L1_cond_w_f1, L1_cond_b_f1, L1_cond_w_f2, L1_cond_b_f2, L1_cond_w_ada, L1_cond_b_ada)
    return x

_drawn_inputs = setup_inputs


def setup_inputs(seed=0):
    import zlib

    import numpy as np

    out = dict(_drawn_inputs(seed))
    spreads = {'L0_cond_bias': (0.0, 0.1),
     'L1_cond_b_q': (0.0, 0.8),
     'L1_cond_b_k': (0.0, 0.8),
     'L1_cond_b_v': (0.0, 0.31),
     'L1_cond_b_o': (0.0, 0.1),
     'L1_cond_b_f1': (0.0, 0.1),
     'L1_cond_b_f2': (0.0, 0.1),
     'L1_cond_b_ada': (0.0, 0.1)}
    factors = {'L1_cond_w_q': 8.0, 'L1_cond_w_k': 8.0, 'L1_cond_w_v': 4.733}
    for name, (base, spread) in spreads.items():
        noise = np.random.default_rng([zlib.crc32(name.encode()), seed]).standard_normal(out[name].shape)
        drawn = base * np.exp(spread * noise) if base else spread * noise
        out[name] = jnp.asarray(drawn.astype(out[name].dtype))
    for name, factor in factors.items():
        out[name] = (out[name] * factor).astype(out[name].dtype)
    return out
```

```python
import math
from contextlib import ExitStack

import concourse.bass as bass
import numpy as np
from concourse import mybir

ALU = mybir.AluOpType
ACT = mybir.ActivationFunctionType
AX = mybir.AxisListType
F32 = mybir.dt.float32
F16 = mybir.dt.float16
I32 = mybir.dt.int32

P = 128
D = 128
NB = 8
STEPS = 256
CH = 64
NC = STEPS // CH
NJ = NB // 2
NT = NC * NJ
NH = 16
HD = D // NH
NI = 4
FF = 512
SW = 24
STACK = 32
VW = 32
VC = 16


def _beta(a, b):
    return math.exp(math.lgamma(a) + math.lgamma(b) - math.lgamma(a + b))


MAXT = float(np.float32(1.0 - 1e-5))
M_CLIP = float(np.arctanh(np.float64(np.float32(1.0 - 1e-5))))
C_HEAD = _beta(HD / 2, 0.5) / _beta(D / 2, 0.5)
SCALE = 1.0 / math.sqrt(HD)
LN_EPS = 1e-6
EPS = 1e-7
ZS = 64.0
assert math.sqrt(NH) * M_CLIP / C_HEAD < M_CLIP


def batch_of(c, j, slot):
    return 2 * j + (slot ^ (c & 1))


def view(ap, *free):
    return bass.AP(ap.tensor, ap.offset, [list(ap.ap[0])] + [list(f) for f in free])


def tok_base(c):
    return CH * (c + 1)


TOK = dict(hcopy=0, transpose=1, resid=2, moments=3, norm=4, artanh=6, rho=16, modulate=17, usq=21, clip=23,
           uscale=25, utrans=27, uevac=28, qkv=29, qcopy=32, qsq=33, qreduce=35, factor=46,
           scale=53, high=54, low=55, stack=57, sevac=58)
LAST = STEPS + 80
END = LAST + 400


def att_groups():
    out = []
    for b in range(NB):
        for i in range(NI):
            out.append((0, b, i, (0, 1, 2, 3), 0, (0, 1), tok_base(1) + 60 + 2 * (NI * b + i)))
    for b in range(NB):
        for i in range(NI):
            out.append((1, b, i, (0, 1, 2, 3), 0, (2,), tok_base(2) + 62 + 2 * (NI * b + i)))
    for b in range(NB):
        for i in range(NI):
            t = LAST + 36 * b + 9 * i
            out.append((2, b, i, (0, 1, 2, 3), 0, (3,), t))
            out.append((2, b, i, (0, 1), 1, (0, 1, 2, 3), t + 3))
            out.append((2, b, i, (2, 3), 1, (0, 1, 2, 3), t + 6))
    return out


def ugrnn_block_kernel(nc, x, cond, w0, b0, wq, bq, wk, bk, wv, bv, wo, bo, wf1, bf1, wf2, bf2, wada,
                       bada, out):
    ctx = ExitStack()
    with ctx:
        def sb(name, shape, dt=F32):
            return ctx.enter_context(nc.sbuf_tensor(name, shape, dt))

        def sem(name):
            return ctx.enter_context(nc.semaphore(name))

        ada_dram = nc.dram_tensor("ada_rows", [NB, 6 * D], F32, kind="Internal").ap()

        resid = sb("resid", [P, NT, D])
        state = sb("state", [P, (STEPS + 1) * SW + NB])
        xT = sb("xT", [P, STEPS * NB])
        res = sb("res", [P, 2, NC, D])
        w0x = res[:, 0, 0:2, :].rearrange("p a d -> p (a d)")
        w0h = res[:, 0, 2:4, :].rearrange("p a d -> p (a d)")
        w0s = sb("w0s", [P, 2, D])
        whs = res[:, 1, :, :].rearrange("p (a b) d -> p a b d", a=2)
        whh = sb("whh", [P, 2, 2, 2, D], F16)
        pr = sb("pr", [P, 4, 512])
        b0row = pr[0:1, 0, 0:2 * D]
        b0s = pr[0:1, 1, 0:2 * D].rearrange("p (a d) -> p a d", a=2)
        bqkv = pr[0:1, 2, 0:3 * D]
        b0h = sb("b0h", [1, 2, 2, D], F16)
        onesh = sb("onesh", [1, 512], F16)
        ones = sb("ones", [1, P])
        identf = sb("identf", [P, P])
        identh = sb("identh", [P, P], F16)
        condr = sb("condr", [NB, D])
        condT = sb("condT", [P, NB])
        prod = sb("prod", [P, 2 * NB])
        prod_hi = sb("prod_hi", [P, 2 * NB], F16)
        prod_lo = sb("prod_lo", [P, 2 * NB], F16)
        y = sb("y", [P, NJ, 3 * D])
        ysq = sb("ysq", [P, 2, 3 * D])
        wada_s = ysq[:, :, :].rearrange("p a n -> p (a n)")
        badar = y[0:1, 0:2, :].rearrange("p a n -> p (a n)")
        ada = sb("ada", [NB, 6 * D])
        mod = sb("mod", [P, 2, NJ, 6 * D])
        wqkv = sb("wqkv", [P, 3 * D])
        bqkvh = sb("bqkvh", [1, 2, 3 * D], F16)
        wo_s = sb("wo_s", [P, D])
        bor = sb("bor", [1, D])
        b2b = sb("b2b", [P, D])
        w1 = sb("w1", [P, FF])
        ffw = sb("ffw", [P, 4, 2 * D + 1])
        gw = sb("gw", [P, 2 * D])
        gwrow = sb("gwrow", [1, 2 * D + 1])
        beta = sb("beta", [P, 1])
        neg_half = sb("neg_half", [P, 4])
        mv = sb("mv", [P, 2, NT, 2])
        bnst = sb("bnst", [P, 4, 6])
        bnst2 = sb("bnst2", [P, 4, 6])
        NS = 40
        stat = sb("stat", [P, NS, NT])
        tmp = sb("tmp", [P, 2, 32, 4])
        itmp = sb("itmp", [P, 2, 2, 4], I32)
        tu = sb("tu", [P, NJ, D])
        tus = sb("tus", [P, NJ, D])
        tuT = sb("tuT", [P, NJ, D])
        hsum = sb("hsum", [P, NJ * 48 + NJ * 3])
        hy = sb("hy", [P, NJ * 51])
        ht = sb("ht", [P, NJ * 51])
        hi32 = sb("hi32", [P, NJ * 51], I32)
        hfac = sb("hfac", [P, NJ * 48])
        qs = sb("qs", [P, 2, 2, NH, 4, HD], F16)
        KT = sb("KT", [P, 4, NB, 2, P], F16)
        QT = sb("QT", [P, NJ, 4, NC * P], F16)
        V = sb("V", [P, NB, 2, NH, VC])
        O = sb("O", [P, NJ, NI, NC * P])
        rec = sb("rec", [P, 2, NH])
        def tiles_of(buf, k):
            return buf[:, 4 * D * k:4 * D * k + 4 * D].rearrange("p (c d) -> p c d", c=NC)

        o_t, oT, x2 = tiles_of(xT, 0), tiles_of(xT, 1), tiles_of(xT, 2)
        fy = tiles_of(xT, 3)
        att = tiles_of(w1, 0)
        vu, vus, vuT = tu, tus, tuT
        scr_a = sb("scr_a", [P, 4, D])
        scr_v = whh.rearrange("p h a k d -> p (h a k d)").bitcast(F32).rearrange("p (c d) -> p c d", c=4)

        zb = ctx.enter_context(nc.psum_tensor("zb", [P, 2, 2, 512], F32))
        tb = ctx.enter_context(nc.psum_tensor("tb", [P, 2, 512], F32))
        sbk = ctx.enter_context(nc.psum_tensor("sbk", [P, 512], F32))
        ob = ctx.enter_context(nc.psum_tensor("ob", [P, 512], F32))

        def score_bank(g):
            if GROUPS[g][0] < 2:
                return sbk[:, :]
            return zb[:, 0, g % 2, :]

        def o_bank(part, b, i):
            if part < 2:
                return ob, 128 * i if part == 0 else 64 * i
            if b % 2 == 0:
                return zb[:, 1, i // 2, :], 256 * (i % 2)
            return (sbk, ob)[i // 2], 256 * (i % 2)

        GROUPS = att_groups()

        load_scan, load_x0 = sem("load_scan"), sem("load_x0")
        load_x, load_rest = sem("load_x"), sem("load_rest")
        consts = sem("consts")
        consts16 = sem("consts16")
        pool_init = sem("pool_init")
        w_split = sem("w_split")
        condT_ps, condT_sb = sem("condT_ps"), sem("condT_sb")
        xT_ps, xT_sb = sem("xT_ps"), sem("xT_sb")
        hi_ready, lo_ready = sem("hi_ready"), sem("lo_ready")
        gate_z, cand_z = sem("gate_z"), sem("cand_z")
        products = sem("products")
        step_in = sem("step_in")
        ada_ps, ada_sb, ada_dr, mod_in = sem("ada_ps"), sem("ada_sb"), sem("ada_dr"), sem("mod_in")
        w1T_ps, w1T_sb, gw_ps, gw_sb = sem("w1T_ps"), sem("w1T_sb"), sem("gw_ps"), sem("gw_sb")
        beta_ps, beta_sb = sem("beta_ps"), sem("beta_sb")
        h_copied, h_transposed = sem("h_copied"), sem("h_transposed")
        dve_done, act_done, pool_done = sem("dve_done"), sem("act_done"), sem("pool_done")
        tok_moments, tok_norm, tok_a = sem("tok_moments"), sem("tok_norm"), sem("tok_a")
        tok_u, tok_usq, tok_clip, tok_us = sem("tok_u"), sem("tok_usq"), sem("tok_clip"), sem("tok_us")
        tok_uT_ps, tok_uT = sem("tok_uT_ps"), sem("tok_uT")
        qkv_ps, qkv_copied, qkv_squared = sem("qkv_ps"), sem("qkv_copied"), sem("qkv_squared")
        qkv_reduced = sem("qkv_reduced")
        qkv_scaled, split_high, split_low = sem("qkv_scaled"), sem("split_high"), sem("split_low")
        stack_ps, q_stack, k_stack = sem("stack_ps"), sem("q_stack"), sem("k_stack")
        scores_ready, probs_ready, pv_done = sem("scores_ready"), sem("probs_ready"), sem("pv_done")
        o_saved = sem("o_saved")
        ot_ps, o_ready, oT_ps, oT_sb = sem("ot_ps"), sem("o_ready"), sem("oT_ps"), sem("oT_sb")
        wo_ps, wo_sq, att_clip, att_ready = sem("wo_ps"), sem("wo_sq"), sem("att_clip"), sem("att_ready")
        att_sq, att_dot, att_n, att_th = sem("att_sq"), sem("att_dot"), sem("att_n"), sem("att_th")
        att_co, att_scaled = sem("att_co"), sem("att_scaled")
        v_moments, v_norm, v_a, v_u0, v_u = (sem("v_moments"), sem("v_norm"), sem("v_a"), sem("v_u0"),
                                             sem("v_u"))
        v_usq, v_clip, v_us, v_uT_ps, v_uT = (sem("v_usq"), sem("v_clip"), sem("v_us"),
                                              sem("v_uT_ps"), sem("v_uT"))
        gu_ps, f1_sum, f1_clip, f2_y, f2_sq = (sem("gu_ps"), sem("f1_sum"), sem("f1_clip"),
                                               sem("f2_y"), sem("f2_sq"))
        f2_clip, ff_ready, ff_sq, ff_dot = sem("f2_clip"), sem("ff_ready"), sem("ff_sq"), sem("ff_dot")
        ff_n, ff_th, ff_co, ff_scaled = sem("ff_n"), sem("ff_th"), sem("ff_co"), sem("ff_scaled")
        block_out, res_ready = sem("block_out"), sem("res_ready")
        stored = [sem(f"stored_{j}") for j in range(NJ)]

        names = {}

        def st(name, sel):
            k = names.setdefault(name, len(names))
            assert k < NS
            return stat[:, k, sel]

        def tok_tiles(c):
            return slice(NJ * c, NJ * c + NJ)

        def tail_tiles(j):
            return slice(j, NT, NJ)

        def q_cols(base, b, chunks):
            s = b % 2
            if len(chunks) == 1:
                c = chunks[0]
                return view(base[:, P * c + CH * (s ^ (c & 1)):P * c + CH * (s ^ (c & 1)) + 1],
                            [1, CH])
            first = base[:, CH * s:CH * s + 1]
            if len(chunks) == 2:
                return view(first, [CH * (3 - 2 * s), 2], [1, CH])
            return view(first, [2 * P, 2], [CH * (3 - 2 * s), 2], [1, CH])

        def at_ticks(now, start):
            while now[0] < start:
                yield

        def run(step, workers):
            now = [0]
            live = [w(now) for w in workers]
            for t in range(END):
                now[0] = t
                if t < STEPS:
                    step(t)
                for w in list(live):
                    if next(w, w) is w:
                        live.remove(w)
            assert not live

        block = ctx.enter_context(nc.Block())

        def tile_dma(eng, dram, sbuf, c, slot, to_dram):
            par = c & 1
            d = bass.AP(dram.tensor, ((slot ^ par) * STEPS + CH * c) * D,
                        [[D, CH], [2 * STEPS * D, NJ], [1, D]])
            s = sbuf[CH * slot:CH * slot + CH, NJ * c:NJ * c + NJ, :]
            return eng.dma_start(d, s) if to_dram else eng.dma_start(s, d)

        def row(ap):
            return ap.rearrange("(a n) -> a n", a=1)

        @block.sync
        def _(sp):
            sp.dma_start(w0h[:, :], w0[D:2 * D, :]).then_inc(load_scan, 16)
            sp.dma_start(condr[:, :], cond).then_inc(load_scan, 16)
            sp.dma_start(b0row[:, :], row(b0)).then_inc(load_scan, 16)
            sp.dma_start(w0x[:, :], w0[0:D, :]).then_inc(load_scan, 16)
            for c in range(1, NC):
                for slot in range(2):
                    tile_dma(sp, x, resid, c, slot, False).then_inc(load_x, 16)
            sp.dma_start(wada_s[:, :], wada).then_inc(load_rest, 16)
            sp.dma_start(badar[:, :], row(bada)).then_inc(load_rest, 16)
            for n, (w, b) in enumerate(((wq, bq), (wk, bk), (wv, bv))):
                sp.dma_start(wqkv[:, D * n:D * n + D], w).then_inc(load_rest, 16)
                sp.dma_start(bqkv[:, D * n:D * n + D], row(b)).then_inc(load_rest, 16)
            sp.dma_start(wo_s[:, :], wo).then_inc(load_rest, 16)
            sp.dma_start(bor[:, :], row(bo)).then_inc(load_rest, 16)
            sp.dma_start(w1[:, :], wf1).then_inc(load_rest, 16)
            sp.dma_start(ffw[:, :, D:2 * D], wf2.rearrange("(k p) n -> p k n", p=P)).then_inc(load_rest, 16)
            sp.dma_start(ffw[:, :, 2 * D:2 * D + 1], bf1.rearrange("(k p a) -> p k a", p=P, a=1),
                         allow_slow_non_contiguous=True)\
              .then_inc(load_rest, 16)
            sp.dma_start(b2b[:, :], bass.AP(bf2.tensor, 0, [[0, P], [1, D]])).then_inc(load_rest, 16)
            sp.wait_ge(ada_sb, 1)
            sp.dma_start(ada_dram, ada[:, :]).then_inc(ada_dr, 16)
            sp.wait_ge(ada_dr, 16)
            for par in range(2):
                for slot in range(2):
                    sp.dma_start(mod[CH * slot:CH * slot + CH, par, :, :],
                                 bass.AP(ada_dram.tensor, (slot ^ par) * 6 * D,
                                         [[0, CH], [2 * 6 * D, NJ], [1, 6 * D]])).then_inc(mod_in, 16)
            for j in range(NJ):
                sp.wait_ge(res_ready, j + 1)
                for c in range(NC):
                    for slot in range(2):
                        b = batch_of(c, j, slot)
                        sp.dma_start(out[b, CH * c:CH * c + CH, :],
                                     res[CH * slot:CH * slot + CH, j % 2, c, :]).then_inc(stored[j], 16)
            for j in range(NJ):
                sp.wait_ge(stored[j], 16 * 2 * NC)

        LOADS_REST = 16 * 14

        @block.gpsimd
        def _(pool):
            for slot in range(2):
                tile_dma(pool, x, resid, 0, slot, False).then_inc(load_x0, 16)
            done = [0]

            def settled(ins):
                done[0] += 1
                ins.then_inc(pool_done, 1)
                pool.wait_ge(pool_done, done[0])

            settled(pool.memset(identf[:, :], 0.0))
            pool.affine_select(out=identf[:, :], in_=identf[:, :], compare_op=ALU.not_equal, fill=1.0,
                               base=0, pattern=[[-1, P]], channel_multiplier=1).then_inc(consts, 1)
            settled(pool.memset(identh[:, :], 0.0))
            pool.affine_select(out=identh[:, :], in_=identh[:, :], compare_op=ALU.not_equal, fill=1.0,
                               base=0, pattern=[[-1, P]], channel_multiplier=1).then_inc(consts16, 1)
            pool.memset(neg_half[:, :], -0.5)
            settled(pool.memset(V[:, :, :, :, :], 0.0))
            pool.memset(V[:, :, :, :, HD:HD + 1], C_HEAD)
            pool.memset(O[:, :, :, (NC - 1) * P:NC * P], 0.0).then_inc(pool_init, 1)

            def clip_factor(dst, sums):
                settled(pool.tensor_scalar(dst, sums, 1e-14, None, ALU.max))
                settled(pool.tensor_tensor(dst, dst, neg_half[:, :], ALU.pow))
                return pool.tensor_scalar(dst, dst, M_CLIP, 1.0, ALU.mult, ALU.min)

            def norm_chain(k, sel, tag, ready, wait):
                mean, var = mv[:, k, sel, 0], mv[:, k, sel, 1]
                ss, rn, cl = st("ss" + tag, sel), st("rn" + tag, sel), st("cl" + tag, sel)
                pool.wait_ge(*wait)
                settled(pool.tensor_tensor(ss, mean, mean, ALU.mult))
                settled(pool.tensor_tensor(ss, ss, var, ALU.add))
                settled(pool.tensor_scalar(ss, ss, float(D), 1e-14, ALU.mult, ALU.max))
                settled(pool.tensor_tensor(rn, ss, neg_half[:, :], ALU.pow))
                settled(pool.tensor_tensor(cl, ss, rn, ALU.mult))
                pool.tensor_scalar(cl, cl, MAXT, None, ALU.min).then_inc(ready, 1)

            def rho_chain(k, sel, tag, wait):
                mean, var = mv[:, k, sel, 0], mv[:, k, sel, 1]
                a, rho, off = st("a" + tag, sel), st("rho" + tag, sel), st("off" + tag, sel)
                pool.wait_ge(*wait)
                settled(pool.tensor_tensor(rho, a, a, ALU.mult))
                settled(pool.tensor_tensor(rho, rho, var, ALU.mult))
                settled(pool.tensor_scalar(rho, rho, LN_EPS, None, ALU.add))
                settled(pool.tensor_tensor(rho, rho, neg_half[:, :], ALU.pow))
                settled(pool.tensor_tensor(rho, rho, a, ALU.mult))
                settled(pool.tensor_tensor(off, mean, rho, ALU.mult))
                settled(pool.tensor_scalar(off, off, -1.0, None, ALU.mult))

            def tokens(now):
                pool.wait_ge(mod_in, 64)
                for c in range(NC):
                    base, sel = tok_base(c), tok_tiles(c)
                    yield from at_ticks(now, base + TOK["norm"])
                    norm_chain(0, sel, "1", tok_norm, (tok_moments, c + 1))
                    yield from at_ticks(now, base + TOK["rho"])
                    rho_chain(0, sel, "1", (tok_a, c + 1))
                    if c:
                        pool.wait_ge(tok_us, c)
                    for j in range(NJ):
                        n = NJ * c + j
                        i = pool.tensor_scalar(tu[:, j, :], resid[:, n, :], st("rho1", slice(n, n + 1)),
                                               st("off1", slice(n, n + 1)), ALU.mult, ALU.add)
                    settled(i)
                    yield from at_ticks(now, base + TOK["modulate"])
                    settled(pool.tensor_tensor(tu[:, :, :], tu[:, :, :], mod[:, c & 1, :, D:2 * D],
                                               ALU.mult))
                    pool.tensor_tensor(tu[:, :, :], tu[:, :, :], mod[:, c & 1, :, 0:D], ALU.add)\
                        .then_inc(tok_u, 1)
                    yield from at_ticks(now, base + TOK["clip"])
                    pool.wait_ge(tok_usq, c + 1)
                    clip_factor(st("uclip1", sel), st("usq1", sel)).then_inc(tok_clip, 1)

            def tail(now):
                for j in range(NJ):
                    sel = tail_tiles(j)
                    T = tail_ticks(j)
                    yield from at_ticks(now, T["clip"])
                    pool.wait_ge(wo_sq, j + 1)
                    clip_factor(st("oclip", sel), st("osq", sel)).then_inc(att_clip, 1)
                    yield from at_ticks(now, T["norm"])
                    pool.wait_ge(att_sq, j + 1)
                    an, arn = st("an", sel), st("arn", sel)
                    settled(pool.tensor_scalar(an, st("asq", sel), 1e-14, None, ALU.max))
                    settled(pool.tensor_tensor(arn, an, neg_half[:, :], ALU.pow))
                    pool.tensor_tensor(an, an, arn, ALU.mult).then_inc(att_n, 1)
                    yield from at_ticks(now, T["norm2"])
                    norm_chain(1, sel, "2", v_norm, (v_moments, j + 1))
                    yield from at_ticks(now, T["rho2"])
                    rho_chain(1, sel, "2", (v_a, j + 1))
                    if j:
                        pool.wait_ge(v_us, j)
                    for c in range(NC):
                        n = NJ * c + j
                        i = pool.tensor_scalar(vu[:, c, :], x2[:, c, :], st("rho2", slice(n, n + 1)),
                                               st("off2", slice(n, n + 1)), ALU.mult, ALU.add)
                    i.then_inc(v_u0, 1)
                    yield from at_ticks(now, T["clip2"])
                    pool.wait_ge(v_usq, j + 1)
                    clip_factor(st("uclip2", sel), st("usq2", sel)).then_inc(v_clip, 1)
                    yield from at_ticks(now, T["clip3"])
                    pool.wait_ge(f1_sum, j + 1)
                    clip_factor(st("fclip1", sel), st("fsq1", sel)).then_inc(f1_clip, 1)
                    yield from at_ticks(now, T["clip4"])
                    pool.wait_ge(f2_sq, j + 1)
                    clip_factor(st("fclip2", sel), st("fsq2", sel)).then_inc(f2_clip, 1)
                    yield from at_ticks(now, T["norm3"])
                    pool.wait_ge(ff_sq, j + 1)
                    fn, frn = st("fn", sel), st("frn", sel)
                    settled(pool.tensor_scalar(fn, st("fsq3", sel), 1e-14, None, ALU.max))
                    settled(pool.tensor_tensor(frn, fn, neg_half[:, :], ALU.pow))
                    pool.tensor_tensor(fn, fn, frn, ALU.mult).then_inc(ff_n, 1)
                    yield from at_ticks(now, T["add"])
                    pool.wait_ge(block_out, j + 1)
                    pool.tensor_tensor(res[:, j % 2, :, :], res[:, j % 2, :, :],
                                       view(resid[:, j, 0:1], [NJ * D, NC], [1, D]), ALU.add)\
                        .then_inc(res_ready, 1)

            run(lambda t: None, [tokens, tail])

        @block.tensor
        def _(pe):
            def transpose(dst, src, ident):
                k = src.ap[0][1]
                return pe.transpose(dst, src, ident[0:k, 0:k])

            def x_transposes(c):
                if c == 0:
                    pe.wait_ge(load_x0, 32)
                else:
                    pe.wait_ge(load_x, 32 * (NC - 1))
                    pe.wait_ge(xT_sb, c)
                for j in range(NJ):
                    i = transpose(sbk[:, D * j:D * j + D], resid[:, NJ * c + j, :], identf)
                i.then_inc(xT_ps, 1)

            def x_part(c):
                for k in range(2):
                    for q in range(4):
                        if q == 0 and k == 0:
                            pe.wait_ge(xT_sb, c + 1)
                        pe.matmul(zb[:, c % 2, k, 128 * q:128 * q + 128], w0s[:, k, :],
                                  xT[:, 512 * c + 128 * q:512 * c + 128 * q + 128],
                                  start=(q == 0), stop=False, skip_group_check=True)
                        yield
                    for half in range(2):
                        pe.matmul(zb[:, c % 2, k, :], b0h[:, half, k, :], onesh[:, :],
                                  start=False, stop=False, skip_group_check=True)
                        yield

            pe.wait_ge(load_scan, 64)
            pe.wait_ge(consts, 1)
            transpose(tb[:, 0, 0:NB], condr[:, :], identf).then_inc(condT_ps, 1)
            x_transposes(0)
            pe.wait_ge(w_split, 1)
            for _ in x_part(0):
                pass

            def z_part(src, half, k, t):
                for p in range(2):
                    i = pe.matmul(zb[:, t // CH % 2, k, NB * (t % CH):NB * (t % CH) + NB],
                                  whh[:, half, p, k, :], src[:, NB * p:NB * p + NB],
                                  start=False, stop=False, skip_group_check=True)
                return i

            def step(t):
                pe.wait_ge(hi_ready, t + 1)
                for k in (1, 0):
                    for half in range(2):
                        z_part(prod_hi, half, k, t)
                pe.wait_ge(lo_ready, t + 1)
                z_part(prod_lo, 0, 1, t).then_inc(gate_z, 1)
                z_part(prod_lo, 0, 0, t).then_inc(cand_z, 1)

            def prepare(now):
                pe.wait_ge(load_rest, LOADS_REST)
                yield from at_ticks(now, 2)
                for h in range(2):
                    for q in range(3):
                        cols = slice(384 * h + 128 * q, 384 * h + 128 * q + 128)
                        pe.matmul(tb[0:NB, h, 128 * q:128 * q + 128], condT[:, :], wada_s[:, cols],
                                  start=(q == 0), stop=False, skip_group_check=True)
                        i = pe.matmul(tb[0:NB, h, 128 * q:128 * q + 128], ones[:, 0:NB],
                                      badar[:, cols], start=False, stop=True,
                                      skip_group_check=True)
                        yield
                i.then_inc(ada_ps, 1)
                for c in range(1, NC):
                    yield from at_ticks(now, 9 + 4 * c)
                    x_transposes(c)
                yield from at_ticks(now, 23)
                yield from x_part(1)
                for k in range(4):
                    i = transpose(ob[:, D * k:D * k + D], w1[:, D * k:D * k + D], identf)
                    yield
                i.then_inc(w1T_ps, 1)
                yield from at_ticks(now, 43)
                pe.wait_ge(w1T_sb, 1)
                for k in range(4):
                    i = pe.matmul(sbk[:, 0:2 * D + 1], ffw[:, k, 0:D], ffw[:, k, :],
                                  start=(k == 0), stop=(k == 3))
                    yield
                for k in range(4):
                    i = pe.matmul(ob[0:1, 0:2 * D + 1], ffw[:, k, 2 * D:2 * D + 1], ffw[:, k, :],
                                  start=(k == 0), stop=(k == 3))
                    yield
                i.then_inc(gw_ps, 1)
                yield from at_ticks(now, 56)
                pe.wait_ge(gw_sb, 1)
                pe.matmul(sbk[:, 0:1], ones[:, :], gwrow[:, 2 * D:2 * D + 1], start=True, stop=True)\
                    .then_inc(beta_ps, 1)
                for c in range(2, NC):
                    yield from at_ticks(now, CH * (c - 1) + 4)
                    yield from x_part(c)

            def tokens(now):
                pe.wait_ge(consts16, 1)
                for c in range(NC):
                    base = tok_base(c)
                    yield from at_ticks(now, base + TOK["transpose"])
                    if c == 0:
                        pe.wait_ge(ada_sb, 1)
                    else:
                        pe.wait_ge(q_stack, NT // NC * c)
                        pe.wait_ge(k_stack, NT // NC * c)
                    pe.wait_ge(h_copied, c + 1)
                    for j in range(NJ):
                        i = transpose(tb[:, 0, D * j:D * j + D], tus[:, j, :], identf)
                    i.then_inc(h_transposed, 1)
                    yield from at_ticks(now, base + TOK["utrans"])
                    pe.wait_ge(tok_us, c + 1)
                    for j in range(NJ):
                        i = transpose(tb[:, 1, D * j:D * j + D], tus[:, j, :], identf)
                    i.then_inc(tok_uT_ps, 1)
                    for j in range(NJ):
                        for n in range(3):
                            yield from at_ticks(now, base + TOK["qkv"] + 3 * j + n)
                            if n == 0:
                                pe.wait_ge(tok_uT, c + 1)
                                if j >= 2:
                                    pe.wait_ge(qkv_copied, NJ * c + j - 1)
                            pe.matmul(tb[:, j % 2, D * n:D * n + D], tuT[:, j, :],
                                      wqkv[:, D * n:D * n + D], start=(n == 0), stop=False,
                                      skip_group_check=True)
                        for half in range(2):
                            i = pe.matmul(tb[:, j % 2, 0:3 * D], onesh[:, 0:P], bqkvh[:, half, :],
                                          start=False, stop=(half == 1), skip_group_check=True)
                        i.then_inc(qkv_ps, 1)
                    for j in range(NJ):
                        yield from at_ticks(now, base + TOK["stack"] + j)
                        n = NJ * c + j
                        pe.wait_ge(split_low, n + 1)
                        if j < 2:
                            pe.wait_ge(qkv_copied, NJ * c + NJ)
                        else:
                            pe.wait_ge(q_stack, n - 1)
                            pe.wait_ge(k_stack, n - 1)
                        bank = tb[:, j % 2, :].bitcast(F16)
                        for k in range(2):
                            src = qs[:, n % 2, k].rearrange("p h s d -> p (h s d)")
                            for g in range(4):
                                i = transpose(bank[:, 512 * k + 128 * g:512 * k + 128 * g + 128],
                                              src[:, 128 * g:128 * g + 128], identh)
                        i.then_inc(stack_ps, 1)

            def attention(now):
                last = {}
                started = set()

                def values(g):
                    part, b, i, hgs, kb, chunks, _ = GROUPS[g]
                    nq = CH * len(chunks)
                    pe.wait_ge(probs_ready, g + 1)
                    if i == 0 and (b, part) not in started:
                        started.add((b, part))
                        if part < 2:
                            if NB * part + b:
                                pe.wait_ge(o_saved, NB * part + b)
                            else:
                                pe.wait_ge(beta_sb, 1)
                        elif b >= 2:
                            pe.wait_ge(o_saved, 2 * NB + 2 * (b - 1))
                        else:
                            pe.wait_ge(o_saved, 2 * NB)
                            pe.wait_ge(step_in, 2 * STEPS)
                    bank, col = o_bank(part, b, i)
                    for n, hg in enumerate(hgs):
                        first = (i == 0 if part < 2 else (i % 2 == 0 and kb == 0))
                        c0 = col + (192 if part == 2 and kb == 0 else 0)
                        ins = pe.matmul(bank[VW * hg:VW * hg + VC, c0:c0 + nq],
                                        V[:, b, kb, NI * hg + i, :], pr[:, g % 4, nq * n:nq * n + nq],
                                        start=first, stop=False, skip_group_check=True)
                    ins.then_inc(pv_done, 1)

                def scores(g):
                    part, b, i, hgs, kb, chunks, _ = GROUPS[g]
                    nq = CH * len(chunks)
                    c_need = {0: 1, 1: 2, 2: 3}[part]
                    pe.wait_ge(q_stack, NJ * c_need + b // 2 + 1)
                    pe.wait_ge(k_stack, NJ * c_need + b // 2 + 1)
                    before = last.get(id_of(g))
                    if before is not None:
                        pe.wait_ge(probs_ready, before + 1)
                    elif part == 0:
                        pe.wait_ge(beta_sb, 1)
                    else:
                        pe.wait_ge(step_in, 2 * STEPS)
                    last[id_of(g)] = g
                    bank = score_bank(g)
                    for n, hg in enumerate(hgs):
                        rows = slice(STACK * i, STACK * i + STACK)
                        q = q_cols(QT[rows, b // 2, hg, :], b, chunks)
                        ins = pe.matmul(bank[:, nq * n:nq * n + nq], KT[rows, hg, b, kb, :], q,
                                        start=(n == 0), stop=(n == len(hgs) - 1),
                                        skip_group_check=True)
                    ins.then_inc(scores_ready, 1)

                def id_of(g):
                    return "s" if GROUPS[g][0] < 2 else g % 2

                pe.wait_ge(pool_init, 1)
                for g in range(len(GROUPS)):
                    yield from at_ticks(now, GROUPS[g][6])
                    scores(g)
                    if g >= 1:
                        values(g - 1)
                yield from at_ticks(now, GROUPS[-1][6] + 2)
                values(len(GROUPS) - 1)

            def tail(now):
                for j in range(NJ):
                    T = tail_ticks(j)
                    tbank = [tb[:, (9 * j + m) % 2, :] for m in range(9)]
                    for c in range(NC):
                        yield from at_ticks(now, T["ot"] + c)
                        if c == 0:
                            pe.wait_ge(o_saved, 2 * NB + 4 * (j + 1))
                            if j:
                                pe.wait_ge(f2_y, NC * (j - 1) + 2)
                            else:
                                pe.wait_ge(q_stack, NT)
                                pe.wait_ge(k_stack, NT)
                        elif c == 1:
                            if j:
                                pe.wait_ge(f2_y, NC * j)
                        else:
                            pe.wait_ge(o_ready, NC * j + c - 1)
                        for i in range(NI):
                            ins = transpose(tbank[c][:, P * i:P * i + P],
                                            O[:, j, i, P * c:P * c + P], identf)
                        ins.then_inc(ot_ps, 1)
                    yield from at_ticks(now, T["oT"])
                    pe.wait_ge(o_ready, NC * j + NC)
                    for c in range(NC):
                        ins = transpose(tbank[4][:, D * c:D * c + D], o_t[:, c, :], identf)
                    ins.then_inc(oT_ps, 1)
                    yield from at_ticks(now, T["wo"])
                    pe.wait_ge(oT_sb, j + 1)
                    for c in range(NC):
                        pe.matmul(tbank[5][:, D * c:D * c + D], oT[:, c, :], wo_s[:, :],
                                  start=(c == 0), stop=False, skip_group_check=True)
                        ins = pe.matmul(tbank[5][:, D * c:D * c + D], ones[:, :], bor[:, :],
                                        start=False, stop=True, skip_group_check=True)
                    ins.then_inc(wo_ps, 1)
                    yield from at_ticks(now, T["utrans"])
                    pe.wait_ge(v_us, j + 1)
                    for c in range(NC):
                        ins = transpose(tbank[6][:, D * c:D * c + D], vus[:, c, :], identf)
                    ins.then_inc(v_uT_ps, 1)
                    for c in range(NC):
                        yield from at_ticks(now, T["gw"] + c)
                        if c == 0:
                            pe.wait_ge(v_uT, j + 1)
                        o = tbank[7 + c // 2][:, 256 * (c % 2):256 * (c % 2) + 256]
                        pe.matmul(o, vuT[:, c, :], gw[:, :], start=(c % 2 == 0), stop=False,
                                  skip_group_check=True)
                        pe.matmul(o, ones[:, :], gwrow[:, 0:2 * D], start=False, stop=True,
                                  skip_group_check=True).then_inc(gu_ps, 1)

            run(step, [prepare, tokens, attention, tail])

        @block.scalar
        def _(act):
            done = [0]

            def settled(ins):
                done[0] += 1
                ins.then_inc(act_done, 1)
                act.wait_ge(act_done, done[0])

            act.wait_ge(condT_ps, 1)
            act.activation(state[:, 0:NB], tb[:, 0, 0:NB], ACT.Copy, scale=2.0).then_inc(condT_sb, 1)
            act.activation(condT[:, :], tb[:, 0, 0:NB], ACT.Copy).then_inc(condT_sb, 1)

            def copy_xT(c):
                act.wait_ge(xT_ps, c + 1)
                first = xT[:, STEPS // NC * NB * c + batch_of(c, 0, 0):][:, 0:1]
                s = batch_of(c, 0, 1) - batch_of(c, 0, 0)
                act.activation(view(first, [2, NJ], [s, 2], [NB, CH]),
                               sbk[:, :].rearrange("p (j s t) -> p j s t", j=NJ, s=2),
                               ACT.Copy).then_inc(xT_sb, 1)

            copy_xT(0)

            def step(t):
                r = state[:, SW * t:SW * t + 32]
                p, k = t // CH % 2, NB * (t % CH)
                act.wait_ge(gate_z, t + 1)
                act.activation(r[:, 24:32], zb[:, p, 1, k:k + NB], ACT.Tanh, scale=-1.0 / ZS)
                act.wait_ge(cand_z, t + 1)
                act.activation(r[:, 8:24].rearrange("p (a b) -> p a b", a=2), zb[:, p, :, k:k + NB],
                               ACT.Tanh, scale=1.0 / ZS).then_inc(step_in, 1)

            def squares(srcs, name, tiles, ready):
                for n, (s, t) in enumerate(zip(srcs, tiles)):
                    i = act.activation(scr_a[:, n, :], s, ACT.Square, accum_out=st(name, slice(t, t + 1)))
                i.then_inc(ready, 1)

            def prepare(now):
                yield from at_ticks(now, 12)
                act.wait_ge(ada_ps, 1)
                act.activation(ada[:, 0:384], tb[0:NB, 0, 0:384], ACT.Copy)
                settled(act.activation(ada[:, 384:768], tb[0:NB, 1, 0:384], ACT.Copy))
                act.activation(ada[:, D:2 * D], ada[:, D:2 * D], ACT.Copy, bias=1.0)
                act.activation(ada[:, 4 * D:5 * D], ada[:, 4 * D:5 * D], ACT.Copy, bias=1.0)\
                    .then_inc(ada_sb, 1)
                for c in range(1, NC):
                    yield from at_ticks(now, 10 + 4 * c)
                    copy_xT(c)
                yield from at_ticks(now, 40)
                act.wait_ge(w1T_ps, 1)
                act.activation(ffw[:, :, 0:D], ob[:, :].rearrange("p (k n) -> p k n", k=4), ACT.Copy)\
                    .then_inc(w1T_sb, 1)
                yield from at_ticks(now, 54)
                act.wait_ge(gw_ps, 1)
                act.activation(gw[:, :], sbk[:, 0:2 * D], ACT.Copy)
                act.activation(gwrow[:, 0:D], ob[0:1, 0:D], ACT.Copy, scale=2.0)
                act.activation(gwrow[:, D:2 * D + 1], ob[0:1, D:2 * D + 1], ACT.Copy).then_inc(gw_sb, 1)
                yield from at_ticks(now, 58)
                act.wait_ge(beta_ps, 1)
                act.activation(beta[:, :], sbk[:, 0:1], ACT.Copy).then_inc(beta_sb, 1)

            def tokens(now):
                for c in range(NC):
                    base, sel = tok_base(c), tok_tiles(c)
                    tiles = range(NJ * c, NJ * c + NJ)
                    yield from at_ticks(now, base + TOK["hcopy"])
                    act.wait_ge(step_in, 2 * CH * (c + 1) + (1 if c < NC - 1 else 0))
                    first = state[:, SW * (CH * c + 1) + batch_of(c, 0, 0):][:, 0:1]
                    act.activation(tus[:, :, :].rearrange("p j (s t) -> p j s t", s=2),
                                   view(first, [2, NJ], [batch_of(c, 0, 1) - batch_of(c, 0, 0), 2],
                                        [SW, CH]), ACT.Copy).then_inc(h_copied, 1)
                    yield from at_ticks(now, base + TOK["usq"])
                    act.wait_ge(tok_u, c + 1)
                    squares([tu[:, j, :] for j in range(NJ)], "usq1", tiles, tok_usq)
                    yield from at_ticks(now, base + TOK["uscale"])
                    act.wait_ge(tok_clip, c + 1)
                    for j in range(NJ):
                        i = act.activation(tus[:, j, :], tu[:, j, :], ACT.Copy,
                                           scale=st("uclip1", slice(NJ * c + j, NJ * c + j + 1)))
                    i.then_inc(tok_us, 1)
                    yield from at_ticks(now, base + TOK["uevac"])
                    act.wait_ge(tok_uT_ps, c + 1)
                    act.activation(tuT[:, :, :], tb[:, 1, :].rearrange("p (j t) -> p j t", j=NJ),
                                   ACT.Copy).then_inc(tok_uT, 1)
                    for j in range(NJ):
                        n = NJ * c + j
                        yield from at_ticks(now, base + TOK["qcopy"] + 3 * j)
                        act.wait_ge(qkv_ps, n + 1)
                        if c:
                            act.wait_ge(qkv_scaled, NJ * (c - 1) + j + 1)
                            act.wait_ge(split_low, NJ * (c - 1) + j + 1)
                        act.activation(y[:, j, :], tb[:, j % 2, 0:3 * D], ACT.Copy)\
                            .then_inc(qkv_copied, 1)
                        yield from at_ticks(now, base + TOK["qsq"] + 3 * j)
                        if n >= 2:
                            act.wait_ge(qkv_reduced, n - 1)
                        act.wait_ge(qkv_copied, n + 1)
                        act.activation(ysq[:, n % 2, :], y[:, j, :], ACT.Square)\
                            .then_inc(qkv_squared, 1)
                    for j in range(NJ):
                        n = NJ * c + j
                        yield from at_ticks(now, base + TOK["high"] + j)
                        act.wait_ge(qkv_scaled, n + 1)
                        if n >= 2:
                            act.wait_ge(stack_ps, n - 1)
                        for k in range(2):
                            src = view(y[:, j, D * k:D * k + 1], [HD, NH], [0, 2], [1, HD])
                            dst = view(qs[:, n % 2, k, 0, 0, 0:1], [4 * HD, NH], [(2, 1)[k] * HD, 2],
                                       [1, HD])
                            i = act.activation(dst, src, ACT.Copy)
                        i.then_inc(split_high, 1)
                    for j in range(NJ):
                        n = NJ * c + j
                        yield from at_ticks(now, base + TOK["sevac"] + j)
                        act.wait_ge(stack_ps, n + 1)
                        act.activation(QT[:, j, :, P * c:P * c + P],
                                       tb[:, j % 2, :].bitcast(F16)[:, 0:512]
                                       .rearrange("p (g t) -> p g t", g=4), ACT.Copy)\
                            .then_inc(q_stack, 1)

            def attention(now):
                for g, (part, b, i, hgs, kb, chunks, tick) in enumerate(GROUPS):
                    yield from at_ticks(now, tick + 1)
                    n = CH * len(chunks) * len(hgs)
                    act.wait_ge(scores_ready, g + 1)
                    if g >= 4:
                        act.wait_ge(pv_done, g - 3)
                    act.activation(pr[:, g % 4, 0:n], score_bank(g)[:, 0:n], ACT.Exp, scale=SCALE)\
                        .then_inc(probs_ready, 1)

            def tail(now):
                for j in range(NJ):
                    sel, T = tail_tiles(j), tail_ticks(j)
                    tiles = [NJ * c + j for c in range(NC)]
                    tbank = [tb[:, (9 * j + m) % 2, :] for m in range(9)]

                    def scaled(dst, src, name, ready):
                        for c in range(NC):
                            i = act.activation(dst[:, c, :], src[:, c, :], ACT.Copy,
                                               scale=st(name, slice(tiles[c], tiles[c] + 1)))
                        i.then_inc(ready, 1)

                    yield from at_ticks(now, T["oevac"])
                    act.wait_ge(oT_ps, j + 1)
                    act.activation(oT[:, :, :], tbank[4].rearrange("p (c t) -> p c t", c=NC), ACT.Copy)\
                        .then_inc(oT_sb, 1)
                    yield from at_ticks(now, T["wosq"])
                    act.wait_ge(wo_ps, j + 1)
                    squares([tbank[5][:, D * c:D * c + D] for c in range(NC)], "osq", tiles, wo_sq)
                    yield from at_ticks(now, T["asq"])
                    act.wait_ge(att_ready, j + 1)
                    squares([att[:, c, :] for c in range(NC)], "asq", tiles, att_sq)
                    yield from at_ticks(now, T["tanh"])
                    act.wait_ge(att_n, j + 1)
                    act.activation(st("ath", sel), st("an", sel), ACT.Tanh).then_inc(att_th, 1)
                    yield from at_ticks(now, T["ascale"])
                    act.wait_ge(att_co, j + 1)
                    scaled(x2, att, "aQ", att_scaled)
                    yield from at_ticks(now, T["usq"])
                    act.wait_ge(v_u, j + 1)
                    squares([vu[:, c, :] for c in range(NC)], "usq2", tiles, v_usq)
                    yield from at_ticks(now, T["uscale"])
                    act.wait_ge(v_clip, j + 1)
                    scaled(vus, vu, "uclip2", v_us)
                    yield from at_ticks(now, T["uevac"])
                    act.wait_ge(v_uT_ps, j + 1)
                    act.activation(vuT[:, :, :], tbank[6].rearrange("p (c t) -> p c t", c=NC), ACT.Copy)\
                        .then_inc(v_uT, 1)
                    yield from at_ticks(now, T["f2sq"])
                    act.wait_ge(f2_y, NC * j + NC)
                    squares([fy[:, c, :] for c in range(NC)], "fsq2", tiles, f2_sq)
                    yield from at_ticks(now, T["ffsq"])
                    act.wait_ge(ff_ready, j + 1)
                    squares([fy[:, c, :] for c in range(NC)], "fsq3", tiles, ff_sq)
                    yield from at_ticks(now, T["fftanh"])
                    act.wait_ge(ff_n, j + 1)
                    act.activation(st("fth", sel), st("fn", sel), ACT.Tanh).then_inc(ff_th, 1)
                    yield from at_ticks(now, T["ffscale"])
                    act.wait_ge(ff_co, j + 1)
                    if j >= 2:
                        act.wait_ge(stored[j - 2], 16 * 2 * NC)
                    scaled(res[:, j % 2], fy, "fQ", ff_scaled)

            run(step, [prepare, tokens, attention, tail])

        @block.vector
        def _(dve):
            done = [0]

            def done_(ins):
                done[0] += 1
                ins.then_inc(dve_done, 1)

            def settle():
                dve.wait_ge(dve_done, done[0])

            def settled(ins):
                done_(ins)
                settle()

            dve.memset(ones[:, :], 1.0)
            dve.memset(onesh[:, :], 1.0)
            dve.wait_ge(load_scan, 64)
            for k, off in ((0, D), (1, 0)):
                s = ZS * (1.0, 0.5)[k]
                dve.tensor_scalar(w0s[:, k, :], w0x[:, off:off + D], s, None, ALU.mult)
                dve.tensor_scalar(whs[:, 0, k, :], w0h[:, off:off + D], s / 4, None, ALU.mult)
                dve.tensor_scalar(whs[:, 1, k, :], w0h[:, off:off + D], s / 2, None, ALU.mult)
                done_(dve.tensor_scalar(b0s[:, k, :], b0row[:, off:off + D], s, (0.0, s)[k],
                                        ALU.mult, ALU.add))
            settle()
            dve.tensor_copy(b0h[:, 0], b0s[:, :, :])
            settled(dve.tensor_copy(whh[:, 0], whs[:, :, :, :]))
            dve.tensor_tensor(b0h[:, 1], b0s[:, :, :], b0h[:, 0], ALU.subtract)
            dve.tensor_tensor(whh[:, 1], whs[:, :, :, :], whh[:, 0], ALU.subtract).then_inc(w_split, 1)
            done_(dve.memset(prod[:, NB:2 * NB], 0.0))
            dve.wait_ge(condT_sb, 2)
            settled(dve.tensor_scalar(prod[:, 0:NB], state[:, 0:NB], 2.0, None, ALU.mult))
            done_(dve.tensor_copy(prod_hi[:, :], prod[:, :]))
            settle()
            dve.tensor_tensor(prod_lo[:, :], prod[:, :], prod_hi[:, :], ALU.subtract)\
                .then_inc(lo_ready, 1)
            dve.wait_ge(w_split, 1)
            dve.memset(tmp[:, 0, 0, 0:1], 0.0).then_inc(hi_ready, 1)

            def step(t):
                r = state[:, SW * t:SW * t + 32]
                dve.wait_ge(step_in, 2 * t + 1)
                if t < STEPS - 1:
                    dve.scalar_tensor_tensor(prod_hi[:, :], r[:, 16:32], 1.0, r[:, 0:16], ALU.add,
                                             ALU.mult).then_inc(hi_ready, 1)
                dve.scalar_tensor_tensor(prod[:, :], r[:, 16:32], 1.0, r[:, 0:16], ALU.add,
                                         ALU.mult).then_inc(products, 1)
                dve.wait_ge(products, t + 1)
                if t < STEPS - 1:
                    dve.tensor_tensor(prod_lo[:, :], prod[:, :], prod_hi[:, :], ALU.subtract)\
                        .then_inc(lo_ready, 1)
                dve.scalar_tensor_tensor(state[:, SW * (t + 1):SW * (t + 1) + NB], prod[:, 0:NB], 0.5,
                                         prod[:, NB:2 * NB], ALU.mult, ALU.add).then_inc(step_in, 1)

            def prepare(now):
                dve.wait_ge(load_rest, LOADS_REST)
                yield from at_ticks(now, 3)
                settled(dve.tensor_copy(bqkvh[:, 0, :], bqkv[:, :]))
                dve.tensor_tensor(bqkvh[:, 1, :], bqkv[:, :], bqkvh[:, 0, :], ALU.subtract)
                yield

            def artanh(now, k, sel, tag, wait, ready, per_tick):
                n = [0]

                def tk(i):
                    return tmp[:, k, i, :]

                def pace(ins):
                    settled(ins)
                    n[0] += 1
                    return n[0] % per_tick == 0

                c, a = st("cl" + tag, sel), st("a" + tag, sel)
                om, op, w, ef, lo, hi_, z, zz, s, cc, m = (tk(i) for i in range(11))
                eb, mb = itmp[:, k, 0, :], itmp[:, k, 1, :]
                dve.wait_ge(*wait)
                done_(dve.tensor_scalar(om, c, -1.0, 1.0, ALU.mult, ALU.add))
                done_(dve.tensor_scalar(op, c, 1.0, None, ALU.add))
                done_(dve.tensor_tensor(cc, c, c, ALU.mult))
                settled(dve.tensor_scalar(m, c, 0.25, None, ALU.is_lt))
                settled(dve.reciprocal(om, om))
                yield
                done_(dve.tensor_tensor(w, op, om, ALU.mult))
                settled(dve.tensor_scalar(s, cc, 1.0 / 13, None, ALU.mult))
                for d in (11, 9):
                    settled(dve.scalar_tensor_tensor(s, s, 1.0 / d, cc, ALU.add, ALU.mult))
                yield
                done_(dve.tensor_scalar(eb, w.bitcast(I32), 23, None, ALU.logical_shift_right))
                done_(dve.tensor_scalar(mb, w.bitcast(I32), 0x7FFFFF, 0x3F800000, ALU.bitwise_and,
                                        ALU.bitwise_or))
                settle()
                half = 0.5 * math.log(2.0)
                done_(dve.tensor_scalar(ef, eb, half, -127 * half + 0.25 * math.log(2.0), ALU.mult,
                                        ALU.add))
                mf, r2 = mb.bitcast(F32), math.sqrt(2.0)
                done_(dve.tensor_scalar(lo, mf, -r2, None, ALU.add))
                settled(dve.tensor_scalar(hi_, mf, r2, None, ALU.add))
                yield
                settled(dve.reciprocal(hi_, hi_))
                settled(dve.tensor_tensor(z, lo, hi_, ALU.mult))
                settled(dve.tensor_tensor(zz, z, z, ALU.mult))
                yield
                lnm = lo
                done_(dve.tensor_scalar(lnm, zz, 1.0 / 9, None, ALU.mult))
                for d in (7, 5, 3):
                    settle()
                    done_(dve.scalar_tensor_tensor(s, s, 1.0 / d, cc, ALU.add, ALU.mult))
                    done_(dve.scalar_tensor_tensor(lnm, lnm, 1.0 / d, zz, ALU.add, ALU.mult))
                    if d == 5:
                        yield
                settle()
                done_(dve.scalar_tensor_tensor(s, s, 1.0, c, ALU.add, ALU.mult))
                settled(dve.scalar_tensor_tensor(lnm, lnm, 1.0, z, ALU.add, ALU.mult))
                yield
                settled(dve.tensor_tensor(lnm, lnm, ef, ALU.add))
                settled(dve.tensor_tensor(s, s, lnm, ALU.subtract))
                settled(dve.tensor_tensor(s, s, m, ALU.mult))
                yield
                settled(dve.tensor_tensor(lnm, lnm, s, ALU.add))
                dve.tensor_tensor(a, lnm, st("rn" + tag, sel), ALU.mult).then_inc(ready, 1)

            def moments(srcs, bn, k, tiles, ready):
                for n, s in enumerate(srcs):
                    done_(dve.bn_stats(bn[:, n, :], s))
                    if n % 2:
                        yield
                settle()
                for n, t in enumerate(tiles):
                    i = dve.bn_aggr(mv[:, k, t, :], bn[:, n, :])
                i.then_inc(ready, 1)

            def tokens(now):
                for c in range(NC):
                    base, sel = tok_base(c), tok_tiles(c)
                    tiles = range(NJ * c, NJ * c + NJ)
                    yield from at_ticks(now, base + TOK["resid"])
                    dve.wait_ge(h_transposed, c + 1)
                    dve.wait_ge(xT_ps, NC)
                    for h in range(2):
                        r = resid[:, NJ * c + 2 * h:NJ * c + 2 * h + 2, :]
                        done_(dve.scalar_tensor_tensor(
                            r, tb[:, 0, 256 * h:256 * h + 256].rearrange("p (j t) -> p j t", j=2), 0.5,
                            r, ALU.mult, ALU.add))
                        yield
                    yield from at_ticks(now, base + TOK["moments"])
                    settle()
                    yield from moments([resid[:, t, :] for t in tiles], bnst, 0, tiles, tok_moments)
                    yield from at_ticks(now, base + TOK["artanh"])
                    yield from artanh(now, 0, sel, "1", (tok_norm, c + 1), tok_a, 3)
                    for j in range(NJ):
                        n = NJ * c + j
                        yield from at_ticks(now, base + TOK["qreduce"] + 3 * j)
                        dve.wait_ge(qkv_squared, n + 1)
                        ins = dve.tensor_reduce(
                            hsum[:, 48 * j:48 * j + 48],
                            ysq[:, n % 2, :].rearrange("p (h d) -> p h d", d=HD), AX.X, ALU.add)
                        ins.then_inc(qkv_reduced, 1)
                    yield from at_ticks(now, base + TOK["factor"])
                    N, NA = NJ * 48, NJ * 51
                    dve.wait_ge(qkv_reduced, NJ * c + NJ)
                    settled(dve.tensor_reduce(hsum[:, N:NA],
                                              hsum[:, 0:N].rearrange("p (a h) -> p a h", h=NH), AX.X,
                                              ALU.add))
                    settled(dve.tensor_scalar(hsum[:, :], hsum[:, :], 1e-30, None, ALU.max))
                    yield
                    settled(dve.tensor_scalar(hi32[:, :], hsum[:, :].bitcast(I32), 1, None,
                                              ALU.logical_shift_right))
                    settled(dve.tensor_scalar(hy[:, :].bitcast(I32), hi32[:, :], -1.0,
                                              float(0x5F3759DF), ALU.mult, ALU.add))
                    yield
                    for _ in range(3):
                        settled(dve.tensor_tensor(ht[:, :], hy[:, :], hy[:, :], ALU.mult))
                        settled(dve.scalar_tensor_tensor(ht[:, :], ht[:, :], -0.5, hsum[:, :], ALU.mult,
                                                         ALU.mult))
                        yield
                        settled(dve.scalar_tensor_tensor(hy[:, :], ht[:, :], 1.5, hy[:, :], ALU.add,
                                                         ALU.mult))
                    settled(dve.tensor_scalar(ht[:, N:NA], hy[:, N:NA], C_HEAD * M_CLIP, C_HEAD,
                                              ALU.mult, ALU.min))
                    settled(dve.scalar_tensor_tensor(
                        hfac[:, :].rearrange("p (a h) -> p a h", h=NH),
                        hy[:, 0:N].rearrange("p (a h) -> p a h", h=NH), M_CLIP,
                        view(ht[:, N:N + 1], [1, NJ * 3], [0, NH]), ALU.mult, ALU.min))
                    for j in range(NJ):
                        n = NJ * c + j
                        kb = c // 2
                        yield from at_ticks(now, base + TOK["scale"] + j)
                        if n == 0:
                            dve.wait_ge(pool_init, 1)
                        yh = y[:, j, :].rearrange("p (h d) -> p h d", d=HD)
                        f = view(hfac[:, 48 * j:48 * j + 1], [1, 2 * NH], [0, HD])
                        dve.tensor_tensor(yh[:, 0:2 * NH, :], yh[:, 0:2 * NH, :], f, ALU.mult)\
                            .then_inc(qkv_scaled, 1)
                        for slot in range(2):
                            pp = slice(CH * slot, CH * slot + CH)
                            fv = view(hfac[pp, 48 * j + 32:48 * j + 33], [1, NH], [0, HD])
                            dve.tensor_tensor(V[pp, batch_of(c, j, slot), kb, :, 0:HD],
                                              yh[pp, 2 * NH:3 * NH, :], fv, ALU.mult)
                    for j in range(NJ):
                        n = NJ * c + j
                        yield from at_ticks(now, base + TOK["low"] + j)
                        dve.wait_ge(split_high, n + 1)
                        for k in range(2):
                            src = view(y[:, j, D * k:D * k + 1], [HD, NH], [0, 2], [1, HD])
                            q0 = view(qs[:, n % 2, k, 0, 0, 0:1], [4 * HD, NH],
                                      [(2, 1)[k] * HD, 2], [1, HD])
                            q1 = view(qs[:, n % 2, k, 0, (1, 2)[k], 0:1], [4 * HD, NH],
                                      [(2, 1)[k] * HD, 2], [1, HD])
                            ins = dve.tensor_tensor(q1, src, q0, ALU.subtract)
                        ins.then_inc(split_low, 1)
                    for j in range(NJ):
                        n = NJ * c + j
                        yield from at_ticks(now, base + TOK["sevac"] + j + 1)
                        dve.wait_ge(q_stack, n + 1)
                        s = (320, -192)[c & 1]
                        b0_ = batch_of(c, j, 0)
                        dst = view(KT[:, 0, b0_, c // 2, 0:1], [NB * 2 * P, 4], [s, 2], [1, CH])
                        dve.tensor_copy(dst, tb[:, j % 2, :].bitcast(F16)[:, 512:1024]
                                        .rearrange("p (g s t) -> p g s t", g=4, s=2))\
                            .then_inc(k_stack, 1)

            def attention(now):
                ends = {}
                for g, (part, b, i, *_rest) in enumerate(GROUPS):
                    if part < 2 and i == NI - 1:
                        ends[g] = (part, b, 0)
                    if part == 2 and i % 2 == 1 and _rest[0] == (2, 3):
                        ends[g] = (part, b, i // 2)
                for g, (part, b, h) in ends.items():
                    tick = GROUPS[g + 1][6] if g + 1 < len(GROUPS) else GROUPS[g][6] + 2
                    yield from at_ticks(now, tick + 1)
                    dve.wait_ge(pv_done, g + 1)
                    s, j = b % 2, b // 2
                    if part < 2:
                        chunks = (0, 1) if part == 0 else (2,)
                        n = CH * len(chunks)
                        first = q_cols(O[:, j, 0, :], b, chunks)
                        dst = view(first, [NC * P, NI], *[list(d) for d in list(first.ap)[1:]])
                        src = ob[:, 0:NI * n].rearrange("p (i q) -> p i q", i=NI)
                        if part == 0:
                            src = ob[:, 0:NI * n].rearrange("p (i c q) -> p i c q", i=NI, c=2)
                        dve.tensor_copy(dst, src).then_inc(o_saved, 1)
                    else:
                        bank, _ = o_bank(2, b, 2 * h)
                        dst = view(O[:, j, 2 * h, CH * s:CH * s + 1], [2 * P, 4], [CH * (3 - 2 * s), 2],
                                   [1, CH])
                        if b == 0 and h == 0:
                            dve.wait_ge(o_saved, 2 * NB)
                        dve.tensor_tensor(dst, bank[:, :].rearrange("p (a c q) -> p a c q", a=4, c=2),
                                          dst, ALU.add).then_inc(o_saved, 1)

            def mobius(k, sel, pre, norms, dots, x2s):
                def tk(i):
                    return tmp[:, k, i, :]
                tau, xy, y2, al, den = (tk(i) for i in range(16, 21))
                done_(dve.tensor_tensor(tau, st(pre + "th", sel), st(pre + "rn", sel), ALU.mult))
                settle()
                done_(dve.tensor_tensor(xy, dots, tau, ALU.mult))
                settled(dve.tensor_tensor(y2, tau, tau, ALU.mult))
                done_(dve.tensor_scalar(xy, xy, 2.0, 1.0, ALU.mult, ALU.add))
                settled(dve.tensor_tensor(y2, y2, norms, ALU.mult))
                done_(dve.tensor_tensor(al, xy, y2, ALU.add))
                settled(dve.tensor_tensor(den, x2s, y2, ALU.mult))
                settled(dve.tensor_tensor(den, den, xy, ALU.add))
                settled(dve.tensor_scalar(den, den, EPS, None, ALU.max))
                done_(dve.reciprocal(den, den))
                done_(dve.tensor_scalar(y2, x2s, -1.0, 1.0, ALU.mult, ALU.add))
                settle()
                done_(dve.tensor_tensor(tau, tau, den, ALU.mult))
                done_(dve.tensor_tensor(st(pre + "P", sel), al, den, ALU.mult))
                settle()
                return dve.tensor_tensor(st(pre + "Q", sel), y2, tau, ALU.mult)

            def tail(now):
                for j in range(NJ):
                    sel, T = tail_tiles(j), tail_ticks(j)
                    tiles = [NJ * c + j for c in range(NC)]
                    tbank = [tb[:, (9 * j + m) % 2, :] for m in range(9)]

                    def sec(s):
                        return view(mod[:, 0, j, D * s:D * s + 1], [0, 2], [NJ * 6 * D, 2], [1, D])

                    for c in range(NC):
                        yield from at_ticks(now, T["ot"] + c)
                        dve.wait_ge(ot_ps, NC * j + c + 1)
                        heads = tbank[c].rearrange("p (i g w) -> p i g w", i=NI, w=VW)
                        settled(dve.reciprocal(rec[:, c % 2, :].rearrange("p (i g) -> p i g", i=NI),
                                               heads[:, :, :, HD]))
                        if j and c == 0:
                            dve.wait_ge(oT_ps, j)
                        dst = o_t[:, c, :].rearrange("p (g i d) -> p i g d", g=4, d=HD)
                        dve.tensor_tensor(dst, heads[:, :, :, 0:HD],
                                          view(rec[:, c % 2, 0:1], [4, NI], [1, 4], [0, HD]), ALU.mult)\
                            .then_inc(o_ready, 1)
                    yield from at_ticks(now, T["a"])
                    dve.wait_ge(att_clip, j + 1)
                    for c in range(NC):
                        ins = dve.scalar_tensor_tensor(
                            att[:, c, :], tbank[5][:, D * c:D * c + D],
                            st("oclip", slice(tiles[c], tiles[c] + 1)),
                            mod[:, c & 1, j, 2 * D:3 * D], ALU.mult, ALU.mult)
                    ins.then_inc(att_ready, 1)
                    dve.wait_ge(att_ready, j + 1)
                    for c in range(NC):
                        done_(dve.tensor_tensor_reduce(scr_v[:, c, :], att[:, c, :], resid[:, tiles[c], :],
                                                       1.0, 0.0, ALU.mult, ALU.add,
                                                       st("adot", slice(tiles[c], tiles[c] + 1))))
                    yield from at_ticks(now, T["mob"])
                    settle()
                    dve.wait_ge(att_th, j + 1)
                    mobius(1, sel, "a", st("asq", sel), st("adot", sel), st("ss1", sel))\
                        .then_inc(att_co, 1)
                    yield from at_ticks(now, T["x2"])
                    dve.wait_ge(att_co, j + 1)
                    dve.wait_ge(att_scaled, j + 1)
                    for c in range(NC):
                        done_(dve.scalar_tensor_tensor(x2[:, c, :], resid[:, tiles[c], :],
                                                       st("aP", slice(tiles[c], tiles[c] + 1)),
                                                       x2[:, c, :], ALU.mult, ALU.add))
                    settle()
                    for _ in moments([x2[:, c, :] for c in range(NC)], bnst2, 1, tiles, v_moments):
                        pass
                    yield from at_ticks(now, T["artanh2"])
                    for _ in artanh(now, 1, sel, "2", (v_norm, j + 1), v_a, 99):
                        pass
                    yield from at_ticks(now, T["modulate"])
                    dve.wait_ge(v_u0, j + 1)
                    vu4 = vu[:, :, :].rearrange("p (a b) d -> p a b d", a=2)
                    settled(dve.tensor_tensor(vu4, vu4, sec(4), ALU.mult))
                    dve.tensor_tensor(vu4, vu4, sec(3), ALU.add).then_inc(v_u, 1)
                    yield from at_ticks(now, T["f1"])
                    for c in range(NC):
                        if c % 2 == 0:
                            dve.wait_ge(gu_ps, NC * j + c + 2)
                        done_(dve.tensor_tensor_reduce(
                            scr_v[:, c, :], tbank[7 + c // 2][:, 256 * (c % 2):256 * (c % 2) + D],
                            vus[:, c, :], 1.0, 0.0, ALU.mult, ALU.add,
                            st("fsq1", slice(tiles[c], tiles[c] + 1))))
                    settle()
                    dve.tensor_scalar(st("fsq1", sel), st("fsq1", sel), beta[:, 0:1], None, ALU.add)\
                        .then_inc(f1_sum, 1)
                    yield from at_ticks(now, T["f2"])
                    dve.wait_ge(f1_clip, j + 1)
                    if j:
                        dve.wait_ge(ff_scaled, j)
                    for c in range(NC):
                        dve.scalar_tensor_tensor(
                            fy[:, c, :], tbank[7 + c // 2][:, 256 * (c % 2) + D:256 * (c % 2) + 2 * D],
                            st("fclip1", slice(tiles[c], tiles[c] + 1)), b2b[:, :], ALU.mult,
                            ALU.add).then_inc(f2_y, 1)
                    yield from at_ticks(now, T["ff"])
                    dve.wait_ge(f2_clip, j + 1)
                    dve.wait_ge(f2_y, NC * j + NC)
                    for c in range(NC):
                        ins = dve.scalar_tensor_tensor(
                            fy[:, c, :], fy[:, c, :], st("fclip2", slice(tiles[c], tiles[c] + 1)),
                            mod[:, c & 1, j, 5 * D:6 * D], ALU.mult, ALU.mult)
                    ins.then_inc(ff_ready, 1)
                    dve.wait_ge(ff_ready, j + 1)
                    for c in range(NC):
                        done_(dve.tensor_tensor_reduce(scr_v[:, c, :], fy[:, c, :], x2[:, c, :], 1.0, 0.0,
                                                       ALU.mult, ALU.add,
                                                       st("fdot", slice(tiles[c], tiles[c] + 1))))
                    yield from at_ticks(now, T["mob2"])
                    settle()
                    dve.wait_ge(ff_th, j + 1)
                    mobius(1, sel, "f", st("fsq3", sel), st("fdot", sel), st("ss2", sel))\
                        .then_inc(ff_co, 1)
                    yield from at_ticks(now, T["out"])
                    dve.wait_ge(ff_co, j + 1)
                    dve.wait_ge(ff_scaled, j + 1)
                    for c in range(NC):
                        ins = dve.scalar_tensor_tensor(
                            res[:, j % 2, c, :], x2[:, c, :], st("fP", slice(tiles[c], tiles[c] + 1)),
                            res[:, j % 2, c, :], ALU.mult, ALU.add)
                    ins.then_inc(block_out, 1)

            run(step, [prepare, tokens, attention, tail])


TAIL_ORDER = ("ot", "ot1", "ot2", "ot3", "oT", "oevac", "wo", "wosq", "clip", "a", "asq", "norm",
              "tanh", "mob", "ascale", "x2", "norm2", "artanh2", "rho2", "modulate", "usq", "clip2",
              "uscale", "utrans", "uevac", "gw", "gw1", "gw2", "gw3", "f1", "clip3", "f2", "f2sq",
              "clip4", "ff", "ffsq", "norm3", "fftanh", "mob2", "ffscale", "out", "add")


def tail_ticks(j):
    base = LAST + 72 * (j + 1) + 4
    return {name: base + n for n, name in enumerate(TAIL_ORDER)}


_INS = ['x', 'cond_1024', 'L0_cond_weight', 'L0_cond_bias', 'L1_cond_w_q', 'L1_cond_b_q', 'L1_cond_w_k',
        'L1_cond_b_k', 'L1_cond_w_v', 'L1_cond_b_v', 'L1_cond_w_o', 'L1_cond_b_o', 'L1_cond_w_f1',
        'L1_cond_b_f1', 'L1_cond_w_f2', 'L1_cond_b_f2', 'L1_cond_w_ada', 'L1_cond_b_ada']


def kernel(**inputs):
    import concourse.bacc as _bacc
    from concourse.bass_utils import run_bass_kernel_spmd as _run

    nc = _bacc.Bacc("TRN2", target_bir_lowering=False, num_devices=1)
    arrays, args = {}, []
    for name in _INS:
        a = np.ascontiguousarray(inputs[name])
        arrays[f"in_{name}_dram"] = a
        args.append(nc.dram_tensor(f"in_{name}_dram", a.shape, mybir.dt.from_np(a.dtype),
                                   kind="ExternalInput").ap())
    args.append(nc.dram_tensor("out_0_dram", (NB, STEPS, D), F32, kind="ExternalOutput").ap())
    ugrnn_block_kernel(nc, *args)
    r = _run(nc, [arrays], core_ids=[0])
    return r.results[0]["out_0_dram"]
```

```python
import math
from contextlib import ExitStack

import concourse.bass as bass
import numpy as np
from concourse import mybir

ALU = mybir.AluOpType
ACT = mybir.ActivationFunctionType
AX = mybir.AxisListType
F32 = mybir.dt.float32
F16 = mybir.dt.float16
I32 = mybir.dt.int32

P = 128
D = 128
NB = 8
STEPS = 256
CH = 64
NC = STEPS // CH
NJ = NB // 2
NT = NC * NJ
NH = 16
HD = D // NH
NI = 4
FF = 512
SW = 24
STACK = 32
VW = 32
VC = HD + 1
VP = 2 * VC


def _beta(a, b):
    return math.exp(math.lgamma(a) + math.lgamma(b) - math.lgamma(a + b))


MAXT = float(np.float32(1.0 - 1e-5))
M_CLIP = float(np.arctanh(np.float64(np.float32(1.0 - 1e-5))))
C_HEAD = _beta(HD / 2, 0.5) / _beta(D / 2, 0.5)
SCALE = 1.0 / math.sqrt(HD)
LN_EPS = 1e-6
EPS = 1e-7
ZS = 64.0
assert math.sqrt(NH) * M_CLIP / C_HEAD < M_CLIP


def batch_of(c, j, slot):
    return 2 * j + (slot ^ (c & 1))


def view(ap, *free):
    return bass.AP(ap.tensor, ap.offset, [list(ap.ap[0])] + [list(f) for f in free])


def tok_base(c):
    return CH * (c + 1)


TOK = dict(hcopy=0, transpose=1, resid=2, moments=4, norm=7, artanh=10, rho=16, xn=18, modulate=20,
           utrans=22, uevac=23, usq=24, clip=25, qkv=26, yevac=28, qsq=29, qreduce=31, factor=(34, 41),
           scale=(42, 43, 50, 51), high=(43, 44, 51, 52), low=(44, 46, 52, 54), stack=(46, 48, 54, 56),
           queries=(47, 49, 55, 57), keys=(48, 52, 56, 58), values=(43, 52))
LAST = STEPS + 54
END = LAST + 240


def tail_ticks(base, pace):
    order = dict(
        ot=(0, 1, 2, 5), o=(1, 3, 5, 7), oT=(6, 9), oevac=(7, 10), wo=(8, 11), wosq=(12, 16),
        m=(17, 14), asq=(20, 18), adot=(20, 18), norm=23, tanh=28, mob=29, ascale=(33, 35),
        x2=(35, 37), norm2=41, artanh=45, rho2=57, xn=(59, 61), modulate=(61, 64), utrans=(63, 66),
        uevac=(64, 67), usq=(66, 68), g=(66, 69), clip2=71, gdot=(69, 71), gy=(73, 74), f1=74, gyevac=(75, 76),
        clip3=75, f2=(80, 83), f2sq=(82, 86), ffsq=(84, 88), fdot=(85, 88), norm3=90, fftanh=96,
        mob2=97, ffscale=(101, 103), out=(102, 104), add=(104, 106))
    out = {k: tuple(base + n for n in v) if isinstance(v, tuple) else base + v
           for k, v in order.items()}
    out["pace"] = pace
    return out


TAIL = (tail_ticks(LAST + 53, 1), tail_ticks(LAST + 101, 99))


def att_groups():
    out = []
    for b in range(NB):
        for i in range(NI):
            out.append((0, b, i, (0, 1, 2, 3), 0, (0, 1), tok_base(1) + 60 + 2 * (NI * b + i)))
    for b in range(NB):
        for i in range(NI):
            out.append((1, b, i, (0, 1, 2, 3), 0, (2,), tok_base(2) + 60 + NI * b + i))
    for b in range(NB):
        for i in range(NI):
            t = LAST + 12 * b + 3 * i
            out.append((2, b, i, (0, 1, 2, 3), 0, (3,), t))
            out.append((2, b, i, (0, 1), 1, (0, 1, 2, 3), t + 1))
            out.append((2, b, i, (2, 3), 1, (0, 1, 2, 3), t + 2))
    return out


def ugrnn_block_kernel(nc, x, cond, w0, b0, wq, bq, wk, bk, wv, bv, wo, bo, wf1, bf1, wf2, bf2, wada,
                       bada, out):
    ctx = ExitStack()
    with ctx:
        def sb(name, shape, dt=F32):
            return ctx.enter_context(nc.sbuf_tensor(name, shape, dt))

        def sem(name):
            return ctx.enter_context(nc.semaphore(name))

        ada_dram = nc.dram_tensor("ada_rows", [NB, 6 * D], F32, kind="Internal").ap()

        resid = sb("resid", [P, NT, D])
        state = sb("state", [P, (STEPS + 1) * SW + NB])
        xT = sb("xT", [P, STEPS * NB])
        early = sb("early", [P, 2, NC, D])
        w0x = early[:, 0, 0:2, :].rearrange("p a d -> p (a d)")
        w0h = early[:, 0, 2:4, :].rearrange("p a d -> p (a d)")
        w0s = sb("w0s", [P, 2, D])
        whs = early[:, 1, :, :].rearrange("p (a b) d -> p a b d", a=2)
        whh = sb("whh", [P, 2, 2, 2, D], F16)
        pr = sb("pr", [P, 4, 512])
        b0row = pr[0:1, 0, 0:2 * D]
        b0s = pr[0:1, 1, 0:2 * D].rearrange("p (a d) -> p a d", a=2)
        b0h = sb("b0h", [1, 2, 2, D], F16)
        onesh = sb("onesh", [1, 512], F16)
        ones = sb("ones", [1, P])
        identf = sb("identf", [P, P])
        identh = sb("identh", [P, P], F16)
        condr = sb("condr", [NB, D])
        condT = sb("condT", [P, NB])
        prod = sb("prod", [P, 2 * NB])
        prod_hi = sb("prod_hi", [P, 2 * NB], F16)
        prod_lo = sb("prod_lo", [P, 2 * NB], F16)
        yy = sb("yy", [P, NJ + 2, 3 * D])
        y, ysq = yy[:, 0:NJ, :], yy[:, NJ:NJ + 2, :]
        wada_s = ysq[:, :, :].rearrange("p a n -> p (a n)")
        badar = y[0:1, 0:2, :].rearrange("p a n -> p (a n)")
        ada = sb("ada", [NB, 6 * D])
        mod = sb("mod", [P, 2, NJ, 6 * D])
        wqkv = sb("wqkv", [P, 3 * D])
        bqkvb = sb("bqkvb", [P, 3 * D])
        wo_s = sb("wo_s", [P, D])
        bor = pr[0:1, 2, 0:D]
        boh = sb("boh", [1, 2, NC, D], F16)
        b2b = sb("b2b", [P, D])
        w1 = sb("w1", [P, FF])
        ffw = sb("ffw", [P, 4, 2 * D + 1])
        gw = sb("gw", [P, 2 * D + 1])
        gwrow = sb("gwrow", [1, D + 1])
        b12 = sb("b12", [P, D + 1])
        neg_half = sb("neg_half", [P, 2 * NC])
        half_ = sb("half_", [P, 2 * NC])
        mv = sb("mv", [P, 2, NT, 2])
        bnst = sb("bnst", [P, NJ, 6])
        bnst2 = sb("bnst2", [P, 2, 2 * NC, 6])
        NS = 44
        stat = sb("stat", [P, NS, NT])
        tmp = sb("tmp", [P, 3, 24, 2 * NC])
        itmp = sb("itmp", [P, 3, 2, 2 * NC], I32)
        tw = sb("tw", [P, 3, NJ, D])
        tu, tus, tuT = tw[:, 0], tw[:, 1], tw[:, 2]
        NH2, NA2 = 2 * 3 * NH, 2 * 3 * NH + 2 * 3
        hsum = sb("hsum", [P, 2, NA2])
        hy = sb("hy", [P, 2, NA2])
        ht = sb("ht", [P, 2, NA2])
        hi32 = sb("hi32", [P, 2, NA2], I32)
        hfac = sb("hfac", [P, 2, NH2])
        qs = sb("qs", [P, 2, 2, NH, 4, HD], F16)
        KT = sb("KT", [P, 4, NB, 2, P], F16)
        QT = sb("QT", [P, NJ, 4, NC * P], F16)
        V = sb("V", [P, NB, 2, NH, VP])
        O = sb("O", [P, NJ, 2, NC * P])
        rec = sb("rec", [P, 2, 2, 2 * NH])
        def tiles_of(flat, k):
            n = 2 * NC * D
            return flat[:, n * k:n * k + n].rearrange("p (m d) -> p m d", d=D)

        flat_y = yy.rearrange("p a n -> p (a n)")
        flat_w = tw.rearrange("p a j d -> p (a j d)")
        T_O = (tiles_of(state, 0), tiles_of(xT, 0))
        T_OT = (tiles_of(state, 1), tiles_of(xT, 1))
        T_M = (tiles_of(state, 2), tiles_of(flat_y, 0))
        T_X = (tiles_of(state, 3), tiles_of(flat_y, 1))
        T_F = (tiles_of(state, 4), tiles_of(flat_w, 0))
        T_R = (tiles_of(state, 5), tiles_of(early.rearrange("p a c d -> p (a c d)"), 0))
        scr_a = sb("scr_a", [P, 4, D])

        zb = ctx.enter_context(nc.psum_tensor("zb", [P, 2, 2, 512], F32))
        tb = ctx.enter_context(nc.psum_tensor("tb", [P, 2, 512], F32))
        sbk = ctx.enter_context(nc.psum_tensor("sbk", [P, 512], F32))
        ob = ctx.enter_context(nc.psum_tensor("ob", [P, 512], F32))

        def score_bank(g):
            part = GROUPS[g][0]
            if part == 0:
                return 0, sbk[:, :]
            if part == 1:
                return 1 + g % 2, zb[:, 0, g % 2, :]
            return ((1, zb[:, 0, 0, :]), (2, zb[:, 0, 1, :]), (0, sbk[:, :]))[g % 3]

        def o_bank(part, b):
            return ob[:, :] if part < 2 else zb[:, 1, b % 2, :]

        def tail_bank(h, k):
            return ((tb[:, 0, :], tb[:, 1, :], ob[:, :]),
                    (zb[:, 0, 0, :], zb[:, 0, 1, :], sbk[:, :]))[h][k % 3]

        GROUPS = att_groups()

        load_scan, load_x0 = sem("load_scan"), sem("load_x0")
        load_x, load_rest = sem("load_x"), sem("load_rest")
        consts = sem("consts")
        consts16 = sem("consts16")
        pool_init = sem("pool_init")
        w_split = sem("w_split")
        condT_ps, condT_sb = sem("condT_ps"), sem("condT_sb")
        xT_ps, xT_sb = sem("xT_ps"), sem("xT_sb")
        hi_ready, lo_ready = sem("hi_ready"), sem("lo_ready")
        gate_z, cand_z = sem("gate_z"), sem("cand_z")
        products = sem("products")
        step_in = sem("step_in")
        ada_ps, ada_sb, ada_dr, mod_in = sem("ada_ps"), sem("ada_sb"), sem("ada_dr"), sem("mod_in")
        w1T_ps, w1T_sb, gw_ps, gw_sb = sem("w1T_ps"), sem("w1T_sb"), sem("gw_ps"), sem("gw_sb")
        beta_ps, beta_sb = sem("beta_ps"), sem("beta_sb")
        bo_split = sem("bo_split")
        h_copied, h_transposed = sem("h_copied"), sem("h_transposed")
        dve_done, act_done, pool_done = sem("dve_done"), sem("act_done"), sem("pool_done")
        tok_moments, tok_norm, tok_a, tok_rho = sem("tok_moments"), sem("tok_norm"), sem("tok_a"), sem("tok_rho")
        tok_xn, tok_u, tok_u2, tok_usq, tok_clip = (sem("tok_xn"), sem("tok_u"), sem("tok_u2"),
                                                    sem("tok_usq"), sem("tok_clip"))
        tok_uT_ps, tok_uT = sem("tok_uT_ps"), sem("tok_uT")
        qkv_ps, qkv_copied, qkv_squared = sem("qkv_ps"), sem("qkv_copied"), sem("qkv_squared")
        qkv_reduced, factor_bits = sem("qkv_reduced"), sem("factor_bits")
        roots, factors = sem("roots"), sem("factors")
        qk_scaled, v_scaled, split_high, split_low = (sem("qk_scaled"), sem("v_scaled"),
                                                      sem("split_high"), sem("split_low"))
        stack_ps, q_stack, k_stack = sem("stack_ps"), sem("q_stack"), sem("k_stack")
        scores_ready, probs_ready, pv_done = sem("scores_ready"), sem("probs_ready"), sem("pv_done")
        o_saved = sem("o_saved")
        ot_ps, o_ready, oT_ps, oT_sb = sem("ot_ps"), sem("o_ready"), sem("oT_ps"), sem("oT_sb")
        wo_ps, wo_sq, att_sq, att_dot = sem("wo_ps"), sem("wo_sq"), sem("att_sq"), sem("att_dot")
        att_m = (sem("att_m_0"), sem("att_m_1"))
        att_n, att_th, att_co, att_scaled = sem("att_n"), sem("att_th"), sem("att_co"), sem("att_scaled")
        v_moments, v_norm, v_a, v_xn, v_u = (sem("v_moments"), sem("v_norm"), sem("v_a"),
                                             sem("v_xn"), sem("v_u"))
        v_usq, v_clip, v_uT_ps, v_uT = sem("v_usq"), sem("v_clip"), sem("v_uT_ps"), sem("v_uT")
        g_ps, t2_ps, gy_ps, f1_dot, f1_sum, f1_clip = (sem("g_ps"), sem("t2_ps"), sem("gy_ps"),
                                                       sem("f1_dot"), sem("f1_sum"), sem("f1_clip"))
        ff_dot = sem("ff_dot")
        f2_y, f2_sq, ff_m, ff_sq = sem("f2_y"), sem("f2_sq"), sem("ff_m"), sem("ff_sq")
        ff_n, ff_th, ff_co, ff_scaled = sem("ff_n"), sem("ff_th"), sem("ff_co"), sem("ff_scaled")
        block_out, res_ready = sem("block_out"), sem("res_ready")
        stored = [sem(f"stored_{j}") for j in range(NJ)]

        names = {}

        def st(name, sel):
            k = names.setdefault(name, len(names))
            assert k < NS
            return stat[:, k, sel]

        def tok_tiles(c):
            return slice(c, NT, NC)

        def tok_tile(c, j):
            return slice(NC * j + c, NC * j + c + 1)

        def half_tiles(h):
            return slice(2 * NC * h, 2 * NC * h + 2 * NC)

        def half_tile(h, m):
            return slice(2 * NC * h + m, 2 * NC * h + m + 1)

        def head_factors(eng, q, settled, fused):
            x, r, t = hsum[:, q, :], hy[:, q, :], ht[:, q, :]
            settled(eng.tensor_scalar(r.bitcast(I32), hi32[:, q, :], -1.0, float(0x5F3759DF), ALU.mult,
                                      ALU.add))
            for _ in range(3):
                settled(eng.tensor_tensor(t, r, r, ALU.mult))
                if fused:
                    settled(eng.scalar_tensor_tensor(t, t, -0.5, x, ALU.mult, ALU.mult))
                    settled(eng.scalar_tensor_tensor(r, t, 1.5, r, ALU.add, ALU.mult))
                else:
                    settled(eng.tensor_tensor(t, t, x, ALU.mult))
                    settled(eng.tensor_scalar(t, t, -0.5, 1.5, ALU.mult, ALU.add))
                    settled(eng.tensor_tensor(r, t, r, ALU.mult))
            return eng.tensor_scalar(t[:, NH2:NA2], r[:, NH2:NA2], C_HEAD * M_CLIP, C_HEAD, ALU.mult,
                                     ALU.min)

        def x_tile(h, m):
            return NJ * (m % NC) + 2 * h + m // NC

        def q_cols(base, b, chunks):
            s = b % 2
            if len(chunks) == 1:
                c = chunks[0]
                return view(base[:, P * c + CH * (s ^ (c & 1)):P * c + CH * (s ^ (c & 1)) + 1],
                            [1, CH])
            first = base[:, CH * s:CH * s + 1]
            if len(chunks) == 2:
                return view(first, [CH * (3 - 2 * s), 2], [1, CH])
            return view(first, [2 * P, 2], [CH * (3 - 2 * s), 2], [1, CH])

        def at_ticks(now, start):
            while now[0] < start:
                yield

        def run(step, workers):
            now = [0]
            live = [w(now) for w in workers]
            for t in range(END):
                now[0] = t
                if t < STEPS:
                    step(t)
                for w in list(live):
                    if next(w, w) is w:
                        live.remove(w)
            assert not live

        block = ctx.enter_context(nc.Block())

        def tile_dma(eng, dram, sbuf, c, slot, to_dram):
            par = c & 1
            d = bass.AP(dram.tensor, ((slot ^ par) * STEPS + CH * c) * D,
                        [[D, CH], [2 * STEPS * D, NJ], [1, D]])
            s = sbuf[CH * slot:CH * slot + CH, NJ * c:NJ * c + NJ, :]
            return eng.dma_start(d, s) if to_dram else eng.dma_start(s, d)

        def row(ap):
            return ap.rearrange("(a n) -> a n", a=1)

        @block.sync
        def _(sp):
            sp.dma_start(w0h[:, :], w0[D:2 * D, :]).then_inc(load_scan, 16)
            sp.dma_start(condr[:, :], cond).then_inc(load_scan, 16)
            sp.dma_start(b0row[:, :], row(b0)).then_inc(load_scan, 16)
            sp.dma_start(w0x[:, :], w0[0:D, :]).then_inc(load_scan, 16)
            for c in range(1, NC):
                for slot in range(2):
                    tile_dma(sp, x, resid, c, slot, False).then_inc(load_x, 16)
            sp.dma_start(wada_s[:, :], wada).then_inc(load_rest, 16)
            sp.dma_start(badar[:, :], row(bada)).then_inc(load_rest, 16)
            for n, (w, b) in enumerate(((wq, bq), (wk, bk), (wv, bv))):
                sp.dma_start(wqkv[:, D * n:D * n + D], w).then_inc(load_rest, 16)
                sp.dma_start(bqkvb[:, D * n:D * n + D], bass.AP(b.tensor, 0, [[0, P], [1, D]]))\
                  .then_inc(load_rest, 16)
            sp.dma_start(wo_s[:, :], wo).then_inc(load_rest, 16)
            sp.dma_start(bor[:, :], row(bo)).then_inc(load_rest, 16)
            sp.dma_start(w1[:, :], wf1).then_inc(load_rest, 16)
            sp.dma_start(ffw[:, :, D:2 * D], wf2.rearrange("(k p) n -> p k n", p=P)).then_inc(load_rest, 16)
            sp.dma_start(ffw[:, :, 2 * D:2 * D + 1], bf1.rearrange("(k p a) -> p k a", p=P, a=1),
                         allow_slow_non_contiguous=True)\
              .then_inc(load_rest, 16)
            sp.dma_start(b2b[:, :], bass.AP(bf2.tensor, 0, [[0, P], [1, D]])).then_inc(load_rest, 16)
            sp.wait_ge(ada_sb, 1)
            sp.dma_start(ada_dram, ada[:, :]).then_inc(ada_dr, 16)
            sp.wait_ge(ada_dr, 16)
            for par in range(2):
                for slot in range(2):
                    sp.dma_start(mod[CH * slot:CH * slot + CH, par, :, :],
                                 bass.AP(ada_dram.tensor, (slot ^ par) * 6 * D,
                                         [[0, CH], [2 * 6 * D, NJ], [1, 6 * D]])).then_inc(mod_in, 16)
            for j in range(NJ):
                h, m0 = j // 2, NC * (j % 2)
                sp.wait_ge(res_ready, j + 1)
                for par in range(2):
                    for slot in range(2):
                        sp.dma_start(
                            bass.AP(out.tensor, (batch_of(par, j, slot) * STEPS + CH * par) * D,
                                    [[D, CH], [2 * CH * D, NC // 2], [1, D]]),
                            T_R[h][CH * slot:CH * slot + CH, m0 + par:m0 + NC:2, :])\
                          .then_inc(stored[j], 16)
            for j in range(NJ):
                sp.wait_ge(stored[j], 16 * 4)

        LOADS_REST = 16 * 14

        @block.gpsimd
        def _(pool):
            for slot in range(2):
                tile_dma(pool, x, resid, 0, slot, False).then_inc(load_x0, 16)
            done = [0]

            def settled(ins):
                done[0] += 1
                ins.then_inc(pool_done, 1)
                pool.wait_ge(pool_done, done[0])

            settled(pool.memset(identf[:, :], 0.0))
            pool.affine_select(out=identf[:, :], in_=identf[:, :], compare_op=ALU.not_equal, fill=1.0,
                               base=0, pattern=[[-1, P]], channel_multiplier=1).then_inc(consts, 1)
            settled(pool.memset(identh[:, :], 0.0))
            pool.affine_select(out=identh[:, :], in_=identh[:, :], compare_op=ALU.not_equal, fill=1.0,
                               base=0, pattern=[[-1, P]], channel_multiplier=1).then_inc(consts16, 1)
            pool.memset(neg_half[:, :], -0.5)
            pool.memset(half_[:, :], 0.5)
            settled(pool.memset(V[:, :, :, :, :], 0.0))
            pool.memset(V[:, :, :, :, HD:HD + 1], C_HEAD)
            pool.memset(O[:, :, :, (NC - 1) * P:NC * P], 0.0).then_inc(pool_init, 1)

            def times(dst, a, b):
                return pool.tensor_tensor(dst, a, b, ALU.mult)

            def inverse_root(dst, sums):
                n = sums.free_size()
                settled(pool.tensor_scalar(dst, sums, 1e-14, None, ALU.max))
                settled(pool.tensor_tensor(dst, dst, neg_half[:, 0:n], ALU.pow))

            def clip_factor(dst, sums):
                inverse_root(dst, sums)
                return pool.tensor_scalar(dst, dst, M_CLIP, 1.0, ALU.mult, ALU.min)

            def ln_norm(k, sel, tag, ready, wait):
                mean, var = mv[:, k, sel, 0], mv[:, k, sel, 1]
                ss, cl = st("ss" + tag, sel), st("cl" + tag, sel)
                n = ss.free_size()
                pool.wait_ge(*wait)
                settled(times(ss, mean, mean))
                settled(pool.tensor_tensor(ss, ss, var, ALU.add))
                settled(pool.tensor_scalar(ss, ss, float(D), 1e-14, ALU.mult, ALU.max))
                settled(pool.tensor_tensor(cl, ss, half_[:, 0:n], ALU.pow))
                pool.tensor_scalar(cl, cl, MAXT, None, ALU.min).then_inc(ready, 1)

            def ln_rho(k, sel, tag, wait):
                rho, off = st("rho" + tag, sel), st("off" + tag, sel)
                pool.wait_ge(*wait)
                settled(pool.tensor_tensor(rho, st("va" + tag, sel), neg_half[:, 0:rho.free_size()],
                                           ALU.pow))
                settled(times(off, mv[:, k, sel, 0], rho))
                return pool.tensor_scalar(off, off, -1.0, None, ALU.mult)

            def pool_xn(dst, src, tag, col):
                return pool.tensor_scalar(dst, src, st("rho" + tag, col), st("off" + tag, col),
                                          ALU.mult, ALU.add)

            def tokens(now):
                pool.wait_ge(mod_in, 64)
                for c in range(NC):
                    base, sel = tok_base(c), tok_tiles(c)
                    yield from at_ticks(now, base + TOK["norm"])
                    ln_norm(0, sel, "1", tok_norm, (tok_moments, c + 1))
                    yield from at_ticks(now, base + TOK["rho"])
                    ln_rho(0, sel, "1", (tok_a, c + 1)).then_inc(tok_rho, 1)
                    pool.wait_ge(tok_rho, c + 1)
                    yield from at_ticks(now, base + TOK["xn"])
                    if c:
                        pool.wait_ge(tok_uT_ps, c)
                    for j in range(2):
                        i = pool_xn(tu[:, j, :], resid[:, NJ * c + j, :], "1", tok_tile(c, j))
                    settled(i)
                    settled(times(tu[:, 0:2, :], tu[:, 0:2, :], mod[:, c & 1, 0:2, D:2 * D]))
                    pool.tensor_tensor(tu[:, 0:2, :], tu[:, 0:2, :], mod[:, c & 1, 0:2, 0:D],
                                       ALU.add).then_inc(tok_u, 1)
                    yield from at_ticks(now, base + TOK["clip"])
                    pool.wait_ge(tok_usq, c + 1)
                    clip_factor(st("uclip1", sel), st("usq1", sel)).then_inc(tok_clip, 1)
                    for q in range(2):
                        yield from at_ticks(now, base + TOK["factor"][q])
                        if (c, q) != (NC - 1, 1):
                            pool.wait_ge(factor_bits, 2 * c + q + 1)
                            head_factors(pool, q, settled, False).then_inc(roots, 1)
                        yield from at_ticks(now, base + TOK["values"][q])
                        pool.wait_ge(factors, 2 * c + q + 1)
                        for j in (2 * q, 2 * q + 1):
                            for slot in range(2):
                                pp = slice(CH * slot, CH * slot + CH)
                                fv = view(hfac[pp, q, 48 * (j % 2) + 32:48 * (j % 2) + 33], [1, NH],
                                          [0, HD])
                                i = times(V[pp, batch_of(c, j, slot), c // 2, :, 0:HD],
                                          y[pp, j, 2 * D:3 * D].rearrange("p (h d) -> p h d", d=HD), fv)
                                if slot == 0:
                                    settled(i)
                            i.then_inc(v_scaled, 1)
                            pool.wait_ge(v_scaled, NJ * c + j + 1)

            def tail(h):
                def work(now):
                    sel, T = half_tiles(h), TAIL[h]
                    tmod = lambda k: tmp[:, 1 + h, k, :]

                    def vector_norms(clip, sq, msq, n, rn):
                        pw = tmod(20)
                        settled(clip_factor(clip, sq))
                        settled(times(n, msq, clip))
                        settled(times(n, n, clip))
                        settled(pool.tensor_scalar(n, n, 1e-14, None, ALU.max))
                        settled(pool.tensor_tensor(rn, n, neg_half[:, :], ALU.pow))
                        return times(n, n, rn)

                    yield from at_ticks(now, T["norm"])
                    pool.wait_ge(wo_sq, 2 * h + 2)
                    pool.wait_ge(att_sq, 2 * h + 2)
                    vector_norms(st("oclip", sel), st("osq", sel), st("asq", sel), st("an", sel),
                                 st("arn", sel)).then_inc(att_n, 1)
                    yield from at_ticks(now, T["norm2"])
                    ln_norm(1, sel, "2", v_norm, (v_moments, h + 1))
                    yield from at_ticks(now, T["rho2"])
                    settled(ln_rho(1, sel, "2", (v_a, h + 1)))
                    for q in range(2):
                        yield from at_ticks(now, T["xn"][q])
                        for m in range(NC * q, NC * q + NC):
                            i = pool_xn(T_O[h][:, m, :], T_X[h][:, m, :], "2", half_tile(h, m))
                        i.then_inc(v_xn, 1)
                    yield from at_ticks(now, T["clip2"])
                    pool.wait_ge(v_usq, 2 * h + 2)
                    clip_factor(st("uclip2", sel), st("usq2", sel)).then_inc(v_clip, 1)
                    yield from at_ticks(now, T["clip3"])
                    pool.wait_ge(f1_sum, h + 1)
                    clip_factor(st("fc1", sel), st("fsq1", sel)).then_inc(f1_clip, 1)
                    yield from at_ticks(now, T["norm3"])
                    pool.wait_ge(f2_sq, 2 * h + 2)
                    pool.wait_ge(ff_sq, 2 * h + 2)
                    vector_norms(st("fclip", sel), st("fsq2", sel), st("fsq3", sel), st("fn", sel),
                                 st("frn", sel)).then_inc(ff_n, 1)
                    for q in range(2):
                        yield from at_ticks(now, T["add"][q])
                        pool.wait_ge(block_out, 2 * h + q + 1)
                        r = T_R[h][:, NC * q:NC * q + NC, :]
                        pool.tensor_tensor(
                            r, r, view(resid[:, 2 * h + q, 0:1], [NJ * D, NC], [1, D]),
                            ALU.add).then_inc(res_ready, 1)
                return work

            run(lambda t: None, [tokens, tail(0), tail(1)])

        @block.tensor
        def _(pe):
            def transpose(dst, src, ident):
                k = src.ap[0][1]
                return pe.transpose(dst, src, ident[0:k, 0:k])

            def x_transposes(c):
                if c == 0:
                    pe.wait_ge(load_x0, 32)
                else:
                    pe.wait_ge(load_x, 32 * (NC - 1))
                    pe.wait_ge(xT_sb, c)
                for j in range(NJ):
                    i = transpose(sbk[:, D * j:D * j + D], resid[:, NJ * c + j, :], identf)
                i.then_inc(xT_ps, 1)

            def x_part(c):
                for k in range(2):
                    for q in range(4):
                        if q == 0 and k == 0:
                            pe.wait_ge(xT_sb, c + 1)
                        pe.matmul(zb[:, c % 2, k, 128 * q:128 * q + 128], w0s[:, k, :],
                                  xT[:, 512 * c + 128 * q:512 * c + 128 * q + 128],
                                  start=(q == 0), stop=False, skip_group_check=True)
                        yield
                    for half in range(2):
                        pe.matmul(zb[:, c % 2, k, :], b0h[:, half, k, :], onesh[:, :],
                                  start=False, stop=False, skip_group_check=True)
                        yield

            pe.wait_ge(load_scan, 64)
            pe.wait_ge(consts, 1)
            transpose(tb[:, 0, 0:NB], condr[:, :], identf).then_inc(condT_ps, 1)
            x_transposes(0)
            pe.wait_ge(w_split, 1)
            for _ in x_part(0):
                pass

            def z_part(src, half, k, t):
                for p in range(2):
                    i = pe.matmul(zb[:, t // CH % 2, k, NB * (t % CH):NB * (t % CH) + NB],
                                  whh[:, half, p, k, :], src[:, NB * p:NB * p + NB],
                                  start=False, stop=False, skip_group_check=True)
                return i

            def step(t):
                pe.wait_ge(hi_ready, t + 1)
                for k in (1, 0):
                    for half in range(2):
                        z_part(prod_hi, half, k, t)
                pe.wait_ge(lo_ready, t + 1)
                z_part(prod_lo, 0, 1, t).then_inc(gate_z, 1)
                z_part(prod_lo, 0, 0, t).then_inc(cand_z, 1)

            def prepare(now):
                pe.wait_ge(load_rest, LOADS_REST)
                yield from at_ticks(now, 2)
                for h in range(2):
                    for q in range(3):
                        cols = slice(384 * h + 128 * q, 384 * h + 128 * q + 128)
                        pe.matmul(tb[0:NB, h, 128 * q:128 * q + 128], condT[:, :], wada_s[:, cols],
                                  start=(q == 0), stop=False, skip_group_check=True)
                        i = pe.matmul(tb[0:NB, h, 128 * q:128 * q + 128], ones[:, 0:NB],
                                      badar[:, cols], start=False, stop=True,
                                      skip_group_check=True)
                        yield
                i.then_inc(ada_ps, 1)
                for c in range(1, NC):
                    yield from at_ticks(now, 9 + 4 * c)
                    x_transposes(c)
                yield from at_ticks(now, 23)
                yield from x_part(1)
                for k in range(4):
                    i = transpose(ob[:, D * k:D * k + D], w1[:, D * k:D * k + D], identf)
                    yield
                i.then_inc(w1T_ps, 1)
                yield from at_ticks(now, 43)
                pe.wait_ge(w1T_sb, 1)
                for k in range(4):
                    i = pe.matmul(sbk[:, 0:2 * D + 1], ffw[:, k, 0:D], ffw[:, k, :],
                                  start=(k == 0), stop=(k == 3))
                    yield
                for k in range(4):
                    i = pe.matmul(ob[0:1, 0:2 * D + 1], ffw[:, k, 2 * D:2 * D + 1], ffw[:, k, :],
                                  start=(k == 0), stop=(k == 3))
                    yield
                i.then_inc(gw_ps, 1)
                yield from at_ticks(now, 56)
                pe.wait_ge(gw_sb, 1)
                pe.matmul(sbk[:, 0:D + 1], ones[:, :], gwrow[:, :], start=True, stop=True)\
                    .then_inc(beta_ps, 1)
                for c in range(2, NC):
                    yield from at_ticks(now, CH * (c - 1) + 4)
                    yield from x_part(c)

            def tokens(now):
                pe.wait_ge(consts16, 1)
                for c in range(NC):
                    base = tok_base(c)
                    yield from at_ticks(now, base + TOK["transpose"])
                    if c == 0:
                        pe.wait_ge(ada_sb, 1)
                    else:
                        pe.wait_ge(q_stack, NT // NC * c)
                        pe.wait_ge(k_stack, NT // NC * c)
                    pe.wait_ge(h_copied, c + 1)
                    for j in range(NJ):
                        i = transpose(tb[:, 0, D * j:D * j + D], tus[:, j, :], identf)
                    i.then_inc(h_transposed, 1)
                    yield from at_ticks(now, base + TOK["utrans"])
                    pe.wait_ge(tok_u, c + 1)
                    pe.wait_ge(tok_u2, c + 1)
                    for j in range(NJ):
                        i = transpose(tb[:, 1, D * j:D * j + D], tu[:, j, :], identf)
                    i.then_inc(tok_uT_ps, 1)
                    for j in range(NJ):
                        for n in range(2):
                            yield from at_ticks(now, base + TOK["qkv"] + 2 * j + n)
                            if n == 0:
                                pe.wait_ge(tok_uT, c + 1)
                                if j >= 2:
                                    pe.wait_ge(qkv_copied, NJ * c + j - 1)
                            i = pe.matmul(tb[:, j % 2, 192 * n:192 * n + 192], tuT[:, j, :],
                                          wqkv[:, 192 * n:192 * n + 192], start=(n == 0), stop=(n == 1),
                                          skip_group_check=True)
                        i.then_inc(qkv_ps, 1)
                    for j in range(NJ):
                        yield from at_ticks(now, base + TOK["stack"][j])
                        n = NJ * c + j
                        pe.wait_ge(split_low, n + 1)
                        if j < 2:
                            pe.wait_ge(qkv_copied, NJ * c + NJ)
                        else:
                            pe.wait_ge(k_stack, n - 1)
                        bank = tb[:, j % 2, :].bitcast(F16)
                        for k in range(2):
                            src = qs[:, n % 2, k].rearrange("p h s d -> p (h s d)")
                            for g in range(4):
                                i = transpose(bank[:, 512 * k + 128 * g:512 * k + 128 * g + 128],
                                              src[:, 128 * g:128 * g + 128], identh)
                        i.then_inc(stack_ps, 1)

            def attention(now):
                last = {}
                started = set()

                def values(gs):
                    pe.wait_ge(probs_ready, gs[-1] + 1)
                    part, b, i, _, kb, chunks, _ = GROUPS[gs[0]]
                    nq = CH * len(chunks)
                    if i == 0 and (b, part) not in started:
                        started.add((b, part))
                        if part < 2:
                            if NB * part + b:
                                pe.wait_ge(o_saved, NB * part + b)
                            else:
                                pe.wait_ge(beta_sb, 1)
                        elif b >= 2:
                            pe.wait_ge(o_saved, 2 * NB + b - 1)
                        else:
                            pe.wait_ge(step_in, 2 * STEPS)
                        if part == 1 and b == 0 or part == 0 and b == 0 or part == 2 and b == 0:
                            pe.wait_ge(v_scaled, NT if part == 2 else 2 * NJ)
                    bank = o_bank(part, b)
                    c0 = 256 * (i // 2) if part == 2 else 128 * (i // 2)
                    if part == 2 and kb == 0:
                        c0 += 192
                    for g in gs:
                        for n, hg in enumerate(GROUPS[g][3]):
                            hd = NI * hg + i
                            window = view(V[:, b, kb, hd, 0:1], [1, VP])
                            if i % 2:
                                window = view(V[:, b, kb, hd - 1, VC:VC + 1], [1, VP])
                            ins = pe.matmul(bank[VW * hg:VW * hg + VP, c0:c0 + nq], window,
                                            pr[:, g % 4, nq * n:nq * n + nq],
                                            start=(i == 0 and kb == 0), stop=False,
                                            skip_group_check=True)
                    ins.then_inc(pv_done, len(gs))

                def scores(g):
                    part, b, i, hgs, kb, chunks, _ = GROUPS[g]
                    nq = CH * len(chunks)
                    c_need = {0: 1, 1: 2, 2: 3}[part]
                    pe.wait_ge(q_stack, NJ * c_need + b // 2 + 1)
                    pe.wait_ge(k_stack, NJ * c_need + b // 2 + 1)
                    k, bank = score_bank(g)
                    if k in last:
                        pe.wait_ge(probs_ready, last[k] + 1)
                    elif part == 0:
                        pe.wait_ge(beta_sb, 1)
                    last[k] = g
                    for n, hg in enumerate(hgs):
                        rows = slice(STACK * i, STACK * i + STACK)
                        q = q_cols(QT[rows, b // 2, hg, :], b, chunks)
                        ins = pe.matmul(bank[:, nq * n:nq * n + nq], KT[rows, hg, b, kb, :], q,
                                        start=(n == 0), stop=(n == len(hgs) - 1),
                                        skip_group_check=True)
                    ins.then_inc(scores_ready, 1)

                pe.wait_ge(pool_init, 1)
                waiting = []

                def oldest():
                    n = 2 if GROUPS[waiting[0]][4] == 1 else 1
                    return n

                for g in range(len(GROUPS)):
                    yield from at_ticks(now, GROUPS[g][6])
                    scores(g)
                    waiting.append(g)
                    while len(waiting) >= oldest() + (1 if GROUPS[g][0] == 0 else 2):
                        n = oldest()
                        values(waiting[:n])
                        del waiting[:n]
                yield from at_ticks(now, GROUPS[-1][6] + 2)
                while waiting:
                    n = oldest()
                    values(waiting[:n])
                    del waiting[:n]

            def tail(h):
                def work(now):
                    T = TAIL[h]
                    bank = lambda k: tail_bank(h, k)
                    for q in range(4):
                        yield from at_ticks(now, T["ot"][q])
                        if q == 0:
                            pe.wait_ge(o_saved, 2 * NB + 4 * (h + 1))
                            if h == 0:
                                pe.wait_ge(k_stack, NT)
                            else:
                                pe.wait_ge(probs_ready, len(GROUPS))
                        elif q == 3:
                            pe.wait_ge(o_ready, 8 * h + 2)
                        for m in (2 * q, 2 * q + 1):
                            j, c = 2 * h + m // NC, m % NC
                            for i in range(2):
                                c0 = 2 * P * (m % 2) + P * i
                                ins = transpose(bank(q)[:, c0:c0 + P], O[:, j, i, P * c:P * c + P],
                                                identf)
                        ins.then_inc(ot_ps, 1)
                    for q in range(2):
                        yield from at_ticks(now, T["oT"][q])
                        pe.wait_ge(o_ready, 8 * h + 4 * q + 4)
                        for c in range(NC):
                            ins = transpose(bank(4 + q)[:, D * c:D * c + D], T_O[h][:, NC * q + c, :],
                                            identf)
                        ins.then_inc(oT_ps, 1)
                    for q in range(2):
                        yield from at_ticks(now, T["wo"][q])
                        pe.wait_ge(oT_sb, 2 * h + q + 1)
                        if q == 0:
                            pe.wait_ge(o_ready, 8 * h + 8)
                            pe.wait_ge(bo_split, 1)
                        for half in range(2):
                            pe.matmul(bank(6 + q), onesh[:, 0:P],
                                      boh[:, half].rearrange("p c d -> p (c d)"),
                                      start=(half == 0), stop=False, skip_group_check=True)
                        for c in range(NC):
                            ins = pe.matmul(bank(6 + q)[:, D * c:D * c + D], T_OT[h][:, NC * q + c, :],
                                            wo_s[:, :], start=False, stop=True, skip_group_check=True)
                        ins.then_inc(wo_ps, 1)
                    for q in range(2):
                        yield from at_ticks(now, T["utrans"][q])
                        pe.wait_ge(v_u, 2 * h + q + 1)
                        if q == 1:
                            pe.wait_ge(att_m[0], h + 1)
                        for c in range(NC):
                            ins = transpose(bank(8 + q)[:, D * c:D * c + D], T_O[h][:, NC * q + c, :],
                                            identf)
                        ins.then_inc(v_uT_ps, 1)
                    for q in range(2):
                        yield from at_ticks(now, T["g"][q])
                        pe.wait_ge(v_uT, 2 * h + q + 1)
                        if q == 0:
                            pe.wait_ge(wo_sq, 2 * h + 2)
                        for c in range(NC):
                            ins = pe.matmul(bank(10 + q)[:, D * c:D * c + D],
                                            T_OT[h][:, NC * q + c, :], gw[:, 0:D],
                                            start=(c == 0), stop=True, skip_group_check=True)
                        ins.then_inc(g_ps, 1)
                    for m in range(2 * NC):
                        ins = pe.matmul(bank(12)[:, m:m + 1], T_OT[h][:, m, :], gw[:, 2 * D:2 * D + 1],
                                        start=(m == 0), stop=True, skip_group_check=True)
                    ins.then_inc(t2_ps, 1)
                    for q in range(2):
                        yield from at_ticks(now, T["gy"][q])
                        pe.wait_ge(f1_dot, 2 * h + q + 1)
                        for c in range(NC):
                            ins = pe.matmul(bank(13 + q)[:, D * c:D * c + D],
                                            T_OT[h][:, NC * q + c, :], gw[:, D:2 * D],
                                            start=(c == 0), stop=True, skip_group_check=True)
                        ins.then_inc(gy_ps, 1)
                return work

            run(step, [prepare, tokens, attention, tail(0), tail(1)])

        @block.scalar
        def _(act):
            done = [0]

            def settled(ins):
                done[0] += 1
                ins.then_inc(act_done, 1)
                act.wait_ge(act_done, done[0])

            act.wait_ge(condT_ps, 1)
            act.activation(state[:, 0:NB], tb[:, 0, 0:NB], ACT.Copy, scale=2.0).then_inc(condT_sb, 1)
            act.activation(condT[:, :], tb[:, 0, 0:NB], ACT.Copy).then_inc(condT_sb, 1)

            def copy_xT(c):
                act.wait_ge(xT_ps, c + 1)
                first = xT[:, STEPS // NC * NB * c + batch_of(c, 0, 0):][:, 0:1]
                s = batch_of(c, 0, 1) - batch_of(c, 0, 0)
                act.activation(view(first, [2, NJ], [s, 2], [NB, CH]),
                               sbk[:, :].rearrange("p (j s t) -> p j s t", j=NJ, s=2),
                               ACT.Copy).then_inc(xT_sb, 1)

            copy_xT(0)

            def step(t):
                r = state[:, SW * t:SW * t + 32]
                p, k = t // CH % 2, NB * (t % CH)
                act.wait_ge(gate_z, t + 1)
                act.activation(r[:, 24:32], zb[:, p, 1, k:k + NB], ACT.Tanh, scale=-1.0 / ZS)
                act.wait_ge(cand_z, t + 1)
                act.activation(r[:, 8:24].rearrange("p (a b) -> p a b", a=2), zb[:, p, :, k:k + NB],
                               ACT.Tanh, scale=1.0 / ZS).then_inc(step_in, 1)

            def prepare(now):
                yield from at_ticks(now, 12)
                act.wait_ge(ada_ps, 1)
                act.activation(ada[:, 0:384], tb[0:NB, 0, 0:384], ACT.Copy)
                settled(act.activation(ada[:, 384:768], tb[0:NB, 1, 0:384], ACT.Copy))
                act.activation(ada[:, D:2 * D], ada[:, D:2 * D], ACT.Copy, bias=1.0)
                act.activation(ada[:, 4 * D:5 * D], ada[:, 4 * D:5 * D], ACT.Copy, bias=1.0)\
                    .then_inc(ada_sb, 1)
                for c in range(1, NC):
                    yield from at_ticks(now, 10 + 4 * c)
                    copy_xT(c)
                yield from at_ticks(now, 40)
                act.wait_ge(w1T_ps, 1)
                act.activation(ffw[:, :, 0:D], ob[:, :].rearrange("p (k n) -> p k n", k=4), ACT.Copy)\
                    .then_inc(w1T_sb, 1)
                yield from at_ticks(now, 54)
                act.wait_ge(gw_ps, 1)
                act.activation(gw[:, 0:2 * D], sbk[:, 0:2 * D], ACT.Copy)
                act.activation(gw[:, 2 * D:2 * D + 1], sbk[:, 2 * D:2 * D + 1], ACT.Copy, scale=2.0)
                act.activation(gwrow[:, :], ob[0:1, D:2 * D + 1], ACT.Copy).then_inc(gw_sb, 1)
                yield from at_ticks(now, 58)
                act.wait_ge(beta_ps, 1)
                act.activation(b12[:, :], sbk[:, 0:D + 1], ACT.Copy).then_inc(beta_sb, 1)

            def tokens(now):
                for c in range(NC):
                    base, sel = tok_base(c), tok_tiles(c)
                    tiles = range(NJ * c, NJ * c + NJ)
                    yield from at_ticks(now, base + TOK["hcopy"])
                    act.wait_ge(step_in, 2 * CH * (c + 1) + (1 if c < NC - 1 else 0))
                    first = state[:, SW * (CH * c + 1) + batch_of(c, 0, 0):][:, 0:1]
                    act.activation(tus[:, :, :].rearrange("p j (s t) -> p j s t", s=2),
                                   view(first, [2, NJ], [batch_of(c, 0, 1) - batch_of(c, 0, 0), 2],
                                        [SW, CH]), ACT.Copy).then_inc(h_copied, 1)
                    yield from at_ticks(now, base + TOK["xn"])
                    act.wait_ge(tok_rho, c + 1)
                    act.wait_ge(tok_moments, c + 1)
                    if c:
                        act.wait_ge(tok_uT_ps, c)
                    for j in (2, 3):
                        i = act.activation(tu[:, j, :], resid[:, NJ * c + j, :], ACT.Identity,
                                           scale=st("rho1", tok_tile(c, j)),
                                           bias=st("off1", tok_tile(c, j)))
                    i.then_inc(tok_xn, 1)
                    yield from at_ticks(now, base + TOK["uevac"])
                    act.wait_ge(tok_uT_ps, c + 1)
                    act.activation(tuT[:, :, :], tb[:, 1, :].rearrange("p (j t) -> p j t", j=NJ),
                                   ACT.Copy).then_inc(tok_uT, 1)
                    for q in range(2):
                        yield from at_ticks(now, base + TOK["usq"] + q)
                        for j in (2 * q, 2 * q + 1):
                            i = act.activation(scr_a[:, j, :], tu[:, j, :], ACT.Square,
                                               accum_out=st("usq1", tok_tile(c, j)))
                    i.then_inc(tok_usq, 1)
                    for j in range(NJ):
                        n = NJ * c + j
                        yield from at_ticks(now, base + TOK["qsq"] + 2 * j)
                        act.wait_ge(qkv_copied, n + 1)
                        if n >= 2:
                            act.wait_ge(qkv_reduced, n - 1)
                        act.activation(ysq[:, n % 2, :], y[:, j, :], ACT.Square)\
                            .then_inc(qkv_squared, 1)

                    def high(j):
                        n = NJ * c + j
                        act.wait_ge(qk_scaled, n + 1)
                        if n >= 2:
                            act.wait_ge(stack_ps, n - 1)
                        for k in range(2):
                            src = view(y[:, j, D * k:D * k + 1], [HD, NH], [0, 2], [1, HD])
                            dst = view(qs[:, n % 2, k, 0, 0, 0:1], [4 * HD, NH], [(2, 1)[k] * HD, 2],
                                       [1, HD])
                            i = act.activation(dst, src, ACT.Copy)
                        i.then_inc(split_high, 1)

                    def queries(j):
                        act.wait_ge(stack_ps, NJ * c + j + 1)
                        act.activation(QT[:, j, :, P * c:P * c + P],
                                       tb[:, j % 2, :].bitcast(F16)[:, 0:512]
                                       .rearrange("p (g t) -> p g t", g=4), ACT.Copy)\
                            .then_inc(q_stack, 1)

                    for piece, j in ((high, 0), (high, 1), (queries, 0), (queries, 1), (high, 2), (high, 3),
                                     (queries, 2), (queries, 3)):
                        yield from at_ticks(now, base + TOK[piece.__name__][j])
                        piece(j)

            def attention(now):
                for g, (part, b, i, hgs, kb, chunks, tick) in enumerate(GROUPS):
                    yield from at_ticks(now, tick + 1)
                    n = CH * len(chunks) * len(hgs)
                    act.wait_ge(scores_ready, g + 1)
                    if g >= 4:
                        act.wait_ge(pv_done, g - 3)
                    act.activation(pr[:, g % 4, 0:n], score_bank(g)[1][:, 0:n], ACT.Exp, scale=SCALE)\
                        .then_inc(probs_ready, 1)

            def tail(h):
                def work(now):
                    sel, T = half_tiles(h), TAIL[h]
                    bank = lambda k: tail_bank(h, k)

                    def squares(junk, srcs, q, name, ready):
                        for c in range(NC):
                            i = act.activation(tiles(junk, q)[c], srcs[c], ACT.Square,
                                               accum_out=st(name, half_tile(h, NC * q + c)))
                        i.then_inc(ready, 1)

                    def tiles(buf, q):
                        return [buf[h][:, NC * q + c, :] for c in range(NC)]

                    def scaled(dst, src, q, name, ready):
                        for c in range(NC):
                            i = act.activation(tiles(dst, q)[c], tiles(src, q)[c], ACT.Copy,
                                               scale=st(name, half_tile(h, NC * q + c)))
                        i.then_inc(ready, 1)

                    for q in range(2):
                        yield from at_ticks(now, T["oevac"][q])
                        act.wait_ge(oT_ps, 2 * h + q + 1)
                        act.activation(T_OT[h][:, NC * q:NC * q + NC, :],
                                       bank(4 + q).rearrange("p (c t) -> p c t", c=NC), ACT.Copy)\
                            .then_inc(oT_sb, 1)
                    for q in range(2):
                        yield from at_ticks(now, T["wosq"][q])
                        if q == 0:
                            act.wait_ge(wo_ps, 2 * h + 1)
                        else:
                            act.wait_ge(att_m[1], h + 1)
                        squares(T_F, [bank(6 + q)[:, D * c:D * c + D] for c in range(NC)], q, "osq", wo_sq)
                    for q in range(2):
                        yield from at_ticks(now, T["asq"][q])
                        act.wait_ge(att_m[q], h + 1)
                        squares(T_R, tiles(T_M, q), q, "asq", att_sq)
                    yield from at_ticks(now, T["tanh"])
                    act.wait_ge(att_n, h + 1)
                    act.activation(st("ath", sel), st("an", sel), ACT.Tanh).then_inc(att_th, 1)
                    for q in range(2):
                        yield from at_ticks(now, T["ascale"][q])
                        act.wait_ge(att_co, h + 1)
                        scaled(T_X, T_M, q, "aQ", att_scaled)
                    for q in range(2):
                        yield from at_ticks(now, T["uevac"][q])
                        act.wait_ge(v_uT_ps, 2 * h + q + 1)
                        act.activation(T_OT[h][:, NC * q:NC * q + NC, :],
                                       bank(8 + q).rearrange("p (c t) -> p c t", c=NC), ACT.Copy)\
                            .then_inc(v_uT, 1)
                    for q in range(2):
                        yield from at_ticks(now, T["usq"][q])
                        act.wait_ge(v_u, 2 * h + q + 1)
                        squares(T_F, tiles(T_O, q), q, "usq2", v_usq)
                    for q in range(2):
                        yield from at_ticks(now, T["f2sq"][q])
                        act.wait_ge(f2_y, 2 * h + q + 1)
                        squares(T_OT, tiles(T_F, q), q, "fsq2", f2_sq)
                        yield from at_ticks(now, T["ffsq"][q])
                        act.wait_ge(ff_m, 2 * h + q + 1)
                        squares(T_O, tiles(T_M, q), q, "fsq3", ff_sq)
                    yield from at_ticks(now, T["fftanh"])
                    act.wait_ge(ff_n, h + 1)
                    act.activation(st("fth", sel), st("fn", sel), ACT.Tanh).then_inc(ff_th, 1)
                    for q in range(2):
                        yield from at_ticks(now, T["ffscale"][q])
                        act.wait_ge(ff_co, h + 1)
                        scaled(T_R, T_M, q, "fQ", ff_scaled)
                return work

            run(step, [prepare, tokens, attention, tail(0), tail(1)])

        @block.vector
        def _(dve):
            done = [0]

            def done_(ins):
                done[0] += 1
                ins.then_inc(dve_done, 1)

            def settle():
                dve.wait_ge(dve_done, done[0])

            def settled(ins):
                done_(ins)
                settle()

            dve.memset(ones[:, :], 1.0)
            dve.memset(onesh[:, :], 1.0)
            dve.wait_ge(load_scan, 64)
            for k, off in ((0, D), (1, 0)):
                s = ZS * (1.0, 0.5)[k]
                dve.tensor_scalar(w0s[:, k, :], w0x[:, off:off + D], s, None, ALU.mult)
                dve.tensor_scalar(whs[:, 0, k, :], w0h[:, off:off + D], s / 4, None, ALU.mult)
                dve.tensor_scalar(whs[:, 1, k, :], w0h[:, off:off + D], s / 2, None, ALU.mult)
                done_(dve.tensor_scalar(b0s[:, k, :], b0row[:, off:off + D], s, (0.0, s)[k],
                                        ALU.mult, ALU.add))
            settle()
            dve.tensor_copy(b0h[:, 0], b0s[:, :, :])
            settled(dve.tensor_copy(whh[:, 0], whs[:, :, :, :]))
            dve.tensor_tensor(b0h[:, 1], b0s[:, :, :], b0h[:, 0], ALU.subtract)
            dve.tensor_tensor(whh[:, 1], whs[:, :, :, :], whh[:, 0], ALU.subtract).then_inc(w_split, 1)
            done_(dve.memset(prod[:, NB:2 * NB], 0.0))
            dve.wait_ge(condT_sb, 2)
            settled(dve.tensor_scalar(prod[:, 0:NB], state[:, 0:NB], 2.0, None, ALU.mult))
            done_(dve.tensor_copy(prod_hi[:, :], prod[:, :]))
            settle()
            dve.tensor_tensor(prod_lo[:, :], prod[:, :], prod_hi[:, :], ALU.subtract)\
                .then_inc(lo_ready, 1)
            dve.wait_ge(w_split, 1)
            dve.memset(tmp[:, 0, 0, 0:1], 0.0).then_inc(hi_ready, 1)

            def step(t):
                r = state[:, SW * t:SW * t + 32]
                dve.wait_ge(step_in, 2 * t + 1)
                if t < STEPS - 1:
                    dve.scalar_tensor_tensor(prod_hi[:, :], r[:, 16:32], 1.0, r[:, 0:16], ALU.add,
                                             ALU.mult).then_inc(hi_ready, 1)
                dve.scalar_tensor_tensor(prod[:, :], r[:, 16:32], 1.0, r[:, 0:16], ALU.add,
                                         ALU.mult).then_inc(products, 1)
                dve.wait_ge(products, t + 1)
                if t < STEPS - 1:
                    dve.tensor_tensor(prod_lo[:, :], prod[:, :], prod_hi[:, :], ALU.subtract)\
                        .then_inc(lo_ready, 1)
                dve.scalar_tensor_tensor(state[:, SW * (t + 1):SW * (t + 1) + NB], prod[:, 0:NB], 0.5,
                                         prod[:, NB:2 * NB], ALU.mult, ALU.add).then_inc(step_in, 1)

            def prepare(now):
                dve.wait_ge(load_rest, LOADS_REST)
                yield from at_ticks(now, 3)
                rows = view(bor[:, 0:1], [0, NC], [1, D])
                settled(dve.tensor_copy(boh[:, 0], rows))
                dve.tensor_tensor(boh[:, 1], rows, boh[:, 0], ALU.subtract).then_inc(bo_split, 1)
                yield

            def artanh(k, sel, tag, wait, ready, per_piece):
                c = st("cl" + tag, sel)
                size = c.free_size()
                om, op, w, ef, lo, hi_, z, d, zz, l = (tmp[:, k, i, 0:size] for i in range(10))
                eb, mb = itmp[:, k, 0, 0:size], itmp[:, k, 1, 0:size]
                r2, half = math.sqrt(2.0), 0.5 * math.log(2.0)
                n = 0
                dve.wait_ge(*wait)
                chain = (
                    (lambda: dve.tensor_scalar(om, c, -1.0, 1.0, ALU.mult, ALU.add), 0),
                    (lambda: dve.tensor_scalar(op, c, r2, r2, ALU.mult, ALU.add), 1),
                    (lambda: dve.reciprocal(om, om), 1),
                    (lambda: dve.tensor_tensor(w, op, om, ALU.mult), 1),
                    (lambda: dve.tensor_scalar(mb, w.bitcast(I32), 0x7FFFFF, 0x3F800000,
                                               ALU.bitwise_and, ALU.bitwise_or), 0),
                    (lambda: dve.tensor_scalar(eb, w.bitcast(I32), 23, None,
                                               ALU.logical_shift_right), 1),
                    (lambda: dve.tensor_scalar(hi_, mb.bitcast(F32), r2, None, ALU.add), 0),
                    (lambda: dve.tensor_scalar(lo, mb.bitcast(F32), -r2, None, ALU.add), 1),
                    (lambda: dve.reciprocal(hi_, hi_), 0),
                    (lambda: dve.tensor_scalar(ef, eb, -127.0, half, ALU.add, ALU.mult), 1),
                    (lambda: dve.tensor_tensor(z, lo, hi_, ALU.mult), 1),
                    (lambda: dve.tensor_tensor(d, c, z, ALU.subtract), 1),
                    (lambda: dve.scalar_tensor_tensor(d, eb, 127.5, d, ALU.is_lt, ALU.mult), 1),
                    (lambda: dve.tensor_tensor(z, z, d, ALU.add), 1),
                    (lambda: dve.tensor_tensor(zz, z, z, ALU.mult), 1),
                    (lambda: dve.tensor_scalar(l, zz, 1.0 / 9, 1.0 / 7, ALU.mult, ALU.add), 1),
                    (lambda: dve.tensor_tensor(l, l, zz, ALU.mult), 1),
                    (lambda: dve.scalar_tensor_tensor(l, l, 1.0 / 5, zz, ALU.add, ALU.mult), 1),
                    (lambda: dve.scalar_tensor_tensor(l, l, 1.0 / 3, zz, ALU.add, ALU.mult), 1),
                    (lambda: dve.scalar_tensor_tensor(l, l, 1.0, z, ALU.add, ALU.mult), 1),
                    (lambda: dve.tensor_tensor(l, l, ef, ALU.add), 1),
                    (lambda: dve.tensor_tensor(l, l, l, ALU.mult), 1),
                    (lambda: dve.reciprocal(l, l), 1),
                    (lambda: dve.tensor_tensor(l, l, st("ss" + tag, sel), ALU.mult), 1))
                for op_, waits in chain:
                    done_(op_())
                    if waits:
                        settle()
                        n += 1
                        if n % per_piece == 0:
                            yield
                dve.scalar_tensor_tensor(st("va" + tag, sel), l, LN_EPS, mv[:, min(k, 1), sel, 1],
                                         ALU.mult, ALU.add).then_inc(ready, 1)

            def tokens(now):
                for c in range(NC):
                    base, sel = tok_base(c), tok_tiles(c)
                    yield from at_ticks(now, base + TOK["resid"])
                    dve.wait_ge(h_transposed, c + 1)
                    dve.wait_ge(xT_ps, NC)
                    for q in range(2):
                        r = resid[:, NJ * c + 2 * q:NJ * c + 2 * q + 2, :]
                        done_(dve.scalar_tensor_tensor(
                            r, tb[:, 0, 256 * q:256 * q + 256].rearrange("p (j t) -> p j t", j=2), 0.5,
                            r, ALU.mult, ALU.add))
                        yield
                    yield from at_ticks(now, base + TOK["moments"])
                    settle()
                    for j in range(NJ):
                        done_(dve.bn_stats(bnst[:, j, :], resid[:, NJ * c + j, :]))
                        if j % 2:
                            yield
                    settle()
                    for j in range(NJ):
                        i = dve.bn_aggr(mv[:, 0, NC * j + c, :], bnst[:, j, :])
                    i.then_inc(tok_moments, 1)
                    yield from at_ticks(now, base + TOK["artanh"])
                    yield from artanh(0, sel, "1", (tok_norm, c + 1), tok_a, 3 if c < NC - 1 else 99)
                    yield from at_ticks(now, base + TOK["modulate"])
                    if c == 0:
                        dve.wait_ge(mod_in, 64)
                    dve.wait_ge(tok_xn, c + 1)
                    settled(dve.tensor_tensor(tu[:, 2:4, :], tu[:, 2:4, :], mod[:, c & 1, 2:4, D:2 * D],
                                              ALU.mult))
                    yield
                    dve.tensor_tensor(tu[:, 2:4, :], tu[:, 2:4, :], mod[:, c & 1, 2:4, 0:D],
                                      ALU.add).then_inc(tok_u2, 1)
                    for j in range(NJ):
                        n = NJ * c + j
                        yield from at_ticks(now, base + TOK["yevac"] + 2 * j)
                        dve.wait_ge(qkv_ps, n + 1)
                        if j == 0:
                            dve.wait_ge(tok_clip, c + 1)
                            if c:
                                dve.wait_ge(v_scaled, NJ * c)
                        dve.scalar_tensor_tensor(y[:, j, :], tb[:, j % 2, 0:3 * D],
                                                 st("uclip1", tok_tile(c, j)), bqkvb[:, :], ALU.mult,
                                                 ALU.add).then_inc(qkv_copied, 1)
                        if j:
                            yield from at_ticks(now, base + TOK["qreduce"] + 2 * (j - 1))
                            head_sums(c, j - 1)
                    yield from at_ticks(now, base + TOK["qreduce"] + 2 * (NJ - 1))
                    head_sums(c, NJ - 1)

                    def scale(j, _):
                        if j % 2 == 0:
                            q = j // 2
                            if (c, q) == (NC - 1, 1):
                                settle()
                            else:
                                dve.wait_ge(roots, 2 * c + q + 1)
                            dve.scalar_tensor_tensor(
                                hfac[:, q, :].rearrange("p (a h) -> p a h", h=NH),
                                hy[:, q, 0:NH2].rearrange("p (a h) -> p a h", h=NH), M_CLIP,
                                view(ht[:, q, NH2:NH2 + 1], [1, 6], [0, NH]), ALU.mult, ALU.min)                                .then_inc(factors, 1)
                            dve.wait_ge(factors, 2 * c + q + 1)
                        yh = y[:, j, 0:2 * D].rearrange("p (h d) -> p h d", d=HD)
                        f = view(hfac[:, j // 2, 48 * (j % 2):48 * (j % 2) + 1], [1, 2 * NH], [0, HD])
                        dve.tensor_tensor(yh, yh, f, ALU.mult).then_inc(qk_scaled, 1)

                    def low(j, k):
                        n = NJ * c + j
                        dve.wait_ge(split_high, n + 1)
                        src = view(y[:, j, D * k:D * k + 1], [HD, NH], [0, 2], [1, HD])
                        q0 = view(qs[:, n % 2, k, 0, 0, 0:1], [4 * HD, NH], [(2, 1)[k] * HD, 2], [1, HD])
                        q1 = view(qs[:, n % 2, k, 0, (1, 2)[k], 0:1], [4 * HD, NH],
                                  [(2, 1)[k] * HD, 2], [1, HD])
                        ins = dve.tensor_tensor(q1, src, q0, ALU.subtract)
                        if k:
                            ins.then_inc(split_low, 1)

                    def keys(j, _):
                        dve.wait_ge(q_stack, NJ * c + j + 1)
                        other = 2 * P * (batch_of(c, j, 1) - batch_of(c, j, 0)) + CH
                        dst = view(KT[:, 0, batch_of(c, j, 0), c // 2, 0:1], [NB * 2 * P, 4],
                                   [other, 2], [1, CH])
                        dve.tensor_copy(dst, tb[:, j % 2, :].bitcast(F16)[:, 512:1024]
                                        .rearrange("p (g s t) -> p g s t", g=4, s=2))\
                            .then_inc(k_stack, 1)

                    for piece, j in ((scale, 0), (scale, 1), (low, 0), (low, 1), (keys, 0), (scale, 2),
                                     (scale, 3), (keys, 1), (low, 2), (low, 3), (keys, 2), (keys, 3)):
                        yield from at_ticks(now, base + TOK[piece.__name__][j])
                        piece(j, 0)
                        if piece is low:
                            yield
                            piece(j, 1)

            def head_sums(c, j):
                n, q = NJ * c + j, j // 2
                dve.wait_ge(qkv_squared, n + 1)
                dve.tensor_reduce(hsum[:, q, 48 * (j % 2):48 * (j % 2) + 48],
                                  ysq[:, n % 2, :].rearrange("p (h d) -> p h d", d=HD), AX.X,
                                  ALU.add).then_inc(qkv_reduced, 1)
                if j % 2 == 0:
                    return
                dve.wait_ge(qkv_reduced, n + 1)
                done_(dve.tensor_reduce(hsum[:, q, NH2:NA2],
                                        hsum[:, q, 0:NH2].rearrange("p (a h) -> p a h", h=NH), AX.X,
                                        ALU.add))
                settle()
                settled(dve.tensor_scalar(hsum[:, q, :], hsum[:, q, :], 1e-30, None, ALU.max))
                dve.tensor_scalar(hi32[:, q, :], hsum[:, q, :].bitcast(I32), 1, None,
                                  ALU.logical_shift_right).then_inc(factor_bits, 1)
                if (c, q) == (NC - 1, 1):
                    dve.wait_ge(factor_bits, 2 * c + q + 1)
                    done_(head_factors(dve, q, settled, True))

            def attention(now):
                for g, (part, b, i, hgs, *_rest) in enumerate(GROUPS):
                    if i < NI - 1 or part == 2 and hgs != (2, 3):
                        continue
                    nxt = g + 1 if part < 2 else min(g + 3, len(GROUPS) - 1)
                    tick = GROUPS[nxt][6] if g + 1 < len(GROUPS) else GROUPS[g][6] + 2
                    yield from at_ticks(now, tick + 1)
                    dve.wait_ge(pv_done, g + 1)
                    s, j = b % 2, b // 2
                    bank = o_bank(part, b)
                    if part < 2:
                        chunks = (0, 1) if part == 0 else (2,)
                        n = CH * len(chunks)
                        first = q_cols(O[:, j, 0, :], b, chunks)
                        dst = view(first, [NC * P, 2], *[list(d) for d in list(first.ap)[1:]])
                        src = view(bank[:, 0:1], [P, 2], [CH, len(chunks)], [1, CH])
                        if part == 1:
                            src = view(bank[:, 0:1], [P, 2], [1, CH])
                        dve.tensor_copy(dst, src).then_inc(o_saved, 1)
                    else:
                        if b == 0:
                            dve.wait_ge(o_saved, 2 * NB)
                        dst = view(O[:, j, 0, CH * s:CH * s + 1], [2 * P, 4], [CH * (3 - 2 * s), 2],
                                   [1, CH])
                        dve.tensor_tensor(dst, bank.rearrange("p (a c q) -> p a c q", a=4, c=2),
                                          dst, ALU.add).then_inc(o_saved, 1)

            def mobius(h, sel, pre, dots, x2s, clip):
                tau, xy, y2, al, den, w = (tmp[:, 1 + h, i, :] for i in range(12, 18))
                th = st(pre + "th", sel)
                done_(dve.tensor_tensor(tau, th, st(pre + "rn", sel), ALU.mult))
                done_(dve.tensor_tensor(y2, th, th, ALU.mult))
                settle()
                done_(dve.tensor_tensor(tau, tau, clip, ALU.mult))
                done_(dve.tensor_tensor(den, x2s, y2, ALU.mult))
                settle()
                done_(dve.tensor_tensor(xy, dots, tau, ALU.mult))
                done_(dve.tensor_scalar(w, x2s, -1.0, 1.0, ALU.mult, ALU.add))
                settle()
                done_(dve.tensor_scalar(xy, xy, 2.0, 1.0, ALU.mult, ALU.add))
                done_(dve.tensor_tensor(w, w, tau, ALU.mult))
                settle()
                done_(dve.tensor_tensor(den, den, xy, ALU.add))
                done_(dve.tensor_tensor(al, xy, y2, ALU.add))
                settle()
                settled(dve.tensor_scalar(den, den, EPS, None, ALU.max))
                settled(dve.reciprocal(den, den))
                done_(dve.tensor_tensor(st(pre + "P", sel), al, den, ALU.mult))
                return dve.tensor_tensor(st(pre + "Q", sel), w, den, ALU.mult)

            def tail(h):
                def work(now):
                    sel, T = half_tiles(h), TAIL[h]
                    bank = lambda k: tail_bank(h, k)

                    def sec(q, s):
                        return view(mod[:, 0, 2 * h + q, D * s:D * s + 1], [0, 2], [NJ * 6 * D, 2],
                                    [1, D])

                    def pair_of(buf, q):
                        return buf[h][:, NC * q:NC * q + NC, :].rearrange("p (a b) d -> p a b d", a=2)

                    def dots(q, name, junk, a, b, ready):
                        for c in range(NC):
                            ins = dve.tensor_tensor_reduce(junk[c], a[c], b[c], 1.0, 0.0, ALU.mult,
                                                           ALU.add, st(name, half_tile(h, NC * q + c)))
                        ins.then_inc(ready, 1)

                    def tiles(buf, q):
                        return [buf[h][:, NC * q + c, :] for c in range(NC)]

                    for q in range(4):
                        yield from at_ticks(now, T["o"][q])
                        dve.wait_ge(ot_ps, 4 * h + q + 1)
                        r = rec[:, h, q % 2, :]
                        settled(dve.reciprocal(
                            view(r[:, 0:1], [8, 4], [2, 4], [1, 2]),
                            view(bank(q)[:, HD:HD + 1], [P, 4], [VW, 4], [VC, 2])))
                        for m in (2 * q, 2 * q + 1):
                            dst = view(T_O[h][:, m, 0:1], [2 * HD, 2], [4 * HD, 4], [HD, 2], [1, HD])
                            src = view(bank(q)[:, 2 * P * (m % 2):2 * P * (m % 2) + 1], [P, 2], [VW, 4],
                                       [VC, 2], [1, HD])
                            f = view(r[:, 16 * (m % 2):16 * (m % 2) + 1], [8, 2], [2, 4], [1, 2],
                                     [0, HD])
                            dve.tensor_tensor(dst, src, f, ALU.mult).then_inc(o_ready, 1)
                    for q in (1, 0):
                        yield from at_ticks(now, T["m"][q])
                        if q:
                            dve.wait_ge(wo_ps, 2 * h + 2)
                        else:
                            dve.wait_ge(wo_sq, 2 * h + 1)
                        dve.tensor_tensor(pair_of(T_M, q),
                                          bank(6 + q).rearrange("p (a b d) -> p a b d", a=2, b=2),
                                          sec(q, 2), ALU.mult).then_inc(att_m[q], 1)
                    for q in range(2):
                        yield from at_ticks(now, T["adot"][q])
                        dve.wait_ge(att_m[q], h + 1)
                        dots(q, "adot", tiles(T_X, q), tiles(T_M, q), [resid[:, x_tile(h, NC * q + c), :]
                                                        for c in range(NC)], att_dot)
                    yield from at_ticks(now, T["mob"])
                    dve.wait_ge(att_dot, 2 * h + 2)
                    dve.wait_ge(att_th, h + 1)
                    mobius(h, sel, "a", st("adot", sel), st("ss1", sel), st("oclip", sel))\
                        .then_inc(att_co, 1)
                    dve.wait_ge(att_co, h + 1)
                    for q in range(2):
                        yield from at_ticks(now, T["x2"][q])
                        dve.wait_ge(att_scaled, 2 * h + q + 1)
                        for c in range(NC):
                            m = NC * q + c
                            x = T_X[h][:, m, :]
                            done_(dve.scalar_tensor_tensor(x, resid[:, x_tile(h, m), :],
                                                           st("aP", half_tile(h, m)), x, ALU.mult,
                                                           ALU.add))
                        settle()
                        for c in range(NC):
                            done_(dve.bn_stats(bnst2[:, h, NC * q + c, :], T_X[h][:, NC * q + c, :]))
                    settle()
                    for m in range(2 * NC):
                        ins = dve.bn_aggr(mv[:, 1, 2 * NC * h + m, :], bnst2[:, h, m, :])
                    ins.then_inc(v_moments, 1)
                    yield from at_ticks(now, T["artanh"])
                    yield from artanh(1 + h, sel, "2", (v_norm, h + 1), v_a, T["pace"])
                    for q in range(2):
                        yield from at_ticks(now, T["modulate"][q])
                        dve.wait_ge(v_xn, 2 * h + q + 1)
                        u = pair_of(T_O, q)
                        settled(dve.tensor_tensor(u, u, sec(q, 4), ALU.mult))
                        dve.tensor_tensor(u, u, sec(q, 3), ALU.add).then_inc(v_u, 1)
                    for q in range(2):
                        yield from at_ticks(now, T["gdot"][q])
                        dve.wait_ge(g_ps, 2 * h + q + 1)
                        if q == 0:
                            dve.wait_ge(v_u, 2 * h + 2)
                        dots(q, "gdot", tiles(T_R, q), [bank(10 + q)[:, D * c:D * c + D] for c in range(NC)],
                             tiles(T_O, q), f1_dot)
                    yield from at_ticks(now, T["f1"])
                    dve.wait_ge(f1_dot, 2 * h + 2)
                    dve.wait_ge(t2_ps, h + 1)
                    dve.wait_ge(v_clip, h + 1)
                    f = st("fsq1", sel)
                    settled(dve.tensor_tensor(f, st("gdot", sel), st("uclip2", sel), ALU.mult))
                    settled(dve.tensor_tensor(f, bank(12)[:, 0:2 * NC], f, ALU.add))
                    settled(dve.tensor_tensor(f, f, st("uclip2", sel), ALU.mult))
                    dve.tensor_scalar(f, f, b12[:, D:D + 1], None, ALU.add).then_inc(f1_sum, 1)
                    for q in range(2):
                        yield from at_ticks(now, T["gyevac"][q])
                        dve.wait_ge(gy_ps, 2 * h + q + 1)
                        for c in range(NC):
                            m = NC * q + c
                            done_(dve.scalar_tensor_tensor(
                                T_F[h][:, m, :], bank(13 + q)[:, D * c:D * c + D],
                                st("uclip2", half_tile(h, m)), b12[:, 0:D], ALU.mult, ALU.add))
                    settle()
                    dve.wait_ge(f1_clip, h + 1)
                    for q in range(2):
                        yield from at_ticks(now, T["f2"][q])
                        for c in range(NC):
                            m = NC * q + c
                            ins = dve.scalar_tensor_tensor(T_F[h][:, m, :], T_F[h][:, m, :],
                                                           st("fc1", half_tile(h, m)), b2b[:, :],
                                                           ALU.mult, ALU.add)
                        ins.then_inc(f2_y, 1)
                        dve.wait_ge(f2_y, 2 * h + q + 1)
                        dve.tensor_tensor(pair_of(T_M, q), pair_of(T_F, q), sec(q, 5), ALU.mult)\
                            .then_inc(ff_m, 1)
                    dve.wait_ge(ff_m, 2 * h + 2)
                    for q in range(2):
                        yield from at_ticks(now, T["fdot"][q])
                        dots(q, "fdot", tiles(T_R, q), tiles(T_M, q), tiles(T_X, q), ff_dot)
                    yield from at_ticks(now, T["mob2"])
                    dve.wait_ge(ff_dot, 2 * h + 2)
                    dve.wait_ge(ff_th, h + 1)
                    mobius(h, sel, "f", st("fdot", sel), st("ss2", sel), st("fclip", sel))\
                        .then_inc(ff_co, 1)
                    dve.wait_ge(ff_co, h + 1)
                    for q in range(2):
                        yield from at_ticks(now, T["out"][q])
                        dve.wait_ge(ff_scaled, 2 * h + q + 1)
                        for c in range(NC):
                            m = NC * q + c
                            ins = dve.scalar_tensor_tensor(
                                T_R[h][:, m, :], T_X[h][:, m, :], st("fP", half_tile(h, m)),
                                T_R[h][:, m, :], ALU.mult, ALU.add)
                        ins.then_inc(block_out, 1)
                return work

            run(step, [prepare, tokens, attention, tail(0), tail(1)])


_INS = ['x', 'cond_1024', 'L0_cond_weight', 'L0_cond_bias', 'L1_cond_w_q', 'L1_cond_b_q', 'L1_cond_w_k',
        'L1_cond_b_k', 'L1_cond_w_v', 'L1_cond_b_v', 'L1_cond_w_o', 'L1_cond_b_o', 'L1_cond_w_f1',
        'L1_cond_b_f1', 'L1_cond_w_f2', 'L1_cond_b_f2', 'L1_cond_w_ada', 'L1_cond_b_ada']


def kernel(**inputs):
    import concourse.bacc as _bacc
    from concourse.bass_utils import run_bass_kernel_spmd as _run

    nc = _bacc.Bacc("TRN2", target_bir_lowering=False, num_devices=1)
    arrays, args = {}, []
    for name in _INS:
        a = np.ascontiguousarray(inputs[name])
        arrays[f"in_{name}_dram"] = a
        args.append(nc.dram_tensor(f"in_{name}_dram", a.shape, mybir.dt.from_np(a.dtype),
                                   kind="ExternalInput").ap())
    args.append(nc.dram_tensor("out_0_dram", (NB, STEPS, D), F32, kind="ExternalOutput").ap())
    ugrnn_block_kernel(nc, *args)
    r = _run(nc, [arrays], core_ids=[0])
    return r.results[0]["out_0_dram"]
```

```python
import math
from contextlib import ExitStack

import concourse.bass as bass
import numpy as np
from concourse import mybir

ALU = mybir.AluOpType
ACT = mybir.ActivationFunctionType
AX = mybir.AxisListType
F32 = mybir.dt.float32
F16 = mybir.dt.float16
I32 = mybir.dt.int32

P = 128
D = 128
NB = 8
STEPS = 256
CH = 64
FIRST = 16
NC = STEPS // CH
NJ = NB // 2
NT = NC * NJ
NH = 16
HD = D // NH
NI = 4
FF = 512
SW = 24
STACK = 32
VW = 32
VC = HD + 1
VP = 2 * VC


def _beta(a, b):
    return math.exp(math.lgamma(a) + math.lgamma(b) - math.lgamma(a + b))


MAXT = float(np.float32(1.0 - 1e-5))
M_CLIP = float(np.arctanh(np.float64(np.float32(1.0 - 1e-5))))
C_HEAD = _beta(HD / 2, 0.5) / _beta(D / 2, 0.5)
SCALE = 1.0 / math.sqrt(HD)
LN_EPS = 1e-6
EPS = 1e-7
ZS = 64.0
assert math.sqrt(NH) * M_CLIP / C_HEAD < M_CLIP


def batch_of(c, j, slot):
    return 2 * j + (slot ^ (c & 1))


def view(ap, *free):
    return bass.AP(ap.tensor, ap.offset, [list(ap.ap[0])] + [list(f) for f in free])


def tok_base(c):
    return CH * (c + 1)


TOK = dict(hcopy=0, transpose=1, resid=3, moments=5, norm=8, artanh=10, rho=17, xn=19, modulate=21,
           utrans=24, uevac=26, usq=(24, 25), clip=27, qkv=27, yevac=29, qsq=30, qreduce=32,
           factor=(36, 41), scale=(42, 43, 48, 49), high=(43, 44, 51, 52), low=(44, 46, 52, 54),
           stack=(46, 48, 54, 56), queries=(48, 50, 56, 58), keys=(50, 51, 57, 59), values=(48, 50))
LAST = STEPS + 66


TAIL = dict(
    ot=(0, 2), o=(1, 3), oT=5, oevac=6, wo=9, m=14, wosq=13, asq=19, adot=20, norm=22, tanh=29,
    mob=34, ascale=36, x2=39, norm2=47, artanh=47, rho2=57, xn=60, modulate=64, utrans=67,
    uevac=69, usq=75, g=70, t2=78, clip2=77, gdot=77, gy=79, f1=80, gyevac=79, clip3=86, f2=86,
    f2sq=89, ffsq=89, fdot=88, norm3=96, fftanh=99, mob2=102, ffscale=108, out=105, add=109)
TAIL_LAST = dict(
    ot=(0, 2), o=(1, 3), oT=5, oevac=6, wo=8, m=14, wosq=13, asq=19, adot=20, norm=20, tanh=29,
    mob=31, ascale=36, x2=39, norm2=47, artanh=47, rho2=59, xn=59, modulate=63, utrans=66,
    uevac=68, usq=74, g=71, t2=77, clip2=76, gdot=76, gy=72, f1=75, gyevac=76, clip3=78, f2=81,
    f2sq=84, ffsq=78, fdot=83, norm3=91, fftanh=95, mob2=97, ffscale=102, out=105, add=106)
PSUM_USERS = ("ot0", "ot1", "oT", "wo", "uT", "g", "t2", "gy")


def tail_base(j):
    return LAST + (46, 86, 126, 166)[j]


def tail_of(j):
    return TAIL_LAST if j == NJ - 1 else TAIL


def psum_ticks(j):
    t = tail_of(j)
    return zip(PSUM_USERS, t["ot"] + (t["oT"], t["wo"], t["utrans"], t["g"], t["t2"], t["gy"]))


END = tail_base(NJ - 1) + 160
USES = sorted((tail_base(j) + t, j, u) for j in range(NJ) for u, t in psum_ticks(j))
TURN = {(j, u): n for n, (_, j, u) in enumerate(USES)}


def att_groups():
    out = []
    for b in range(NB):
        for i in range(NI):
            t = tok_base(1) + 52 + 2 * (NI * b + i)
            out.append((0, b, i, (0, 1, 2, 3), 0, (0, 1), t if t < tok_base(2) + 26 else t + 8))
    for b in range(NB):
        for i in range(NI):
            k = NI * b + i
            t = tok_base(2) + 60 + k if k < 20 else tok_base(NC - 1) + 33 + k - 20
            out.append((1, b, i, (0, 1, 2, 3), 0, (2,), t))
    for b in range(NB):
        for i in range(NI):
            t = LAST + 20 * b + 5 * i
            out.append((2, b, i, (0, 1, 2, 3), 0, (3,), t))
            out.append((2, b, i, (0, 1), 1, (0, 1, 2, 3), t + 1))
            out.append((2, b, i, (2, 3), 1, (0, 1, 2, 3), t + 3))
    return out


def ugrnn_block_kernel(nc, x, cond, w0, b0, wq, bq, wk, bk, wv, bv, wo, bo, wf1, bf1, wf2, bf2, wada,
                       bada, out):
    ctx = ExitStack()
    with ctx:
        def sb(name, shape, dt=F32):
            return ctx.enter_context(nc.sbuf_tensor(name, shape, dt))

        def sem(name):
            return ctx.enter_context(nc.semaphore(name))

        ada_dram = nc.dram_tensor("ada_rows", [NB, 6 * D], F32, kind="Internal").ap()

        resid = sb("resid", [P, NT, D])
        state = sb("state", [P, (STEPS + 1) * SW + NB])
        xT = sb("xT", [P, STEPS * NB])
        early = sb("early", [P, 2, NC, D])
        w0x = early[:, 0, 0:2, :].rearrange("p a d -> p (a d)")
        w0h = early[:, 0, 2:4, :].rearrange("p a d -> p (a d)")
        w0s = sb("w0s", [P, 2, D])
        whs = early[:, 1, :, :].rearrange("p (a b) d -> p a b d", a=2)
        whh = sb("whh", [P, 2, 2, 2, D], F16)
        pr = sb("pr", [P, 4, 512])
        b0row = pr[0:1, 0, 0:2 * D]
        b0s = pr[0:1, 1, 0:2 * D].rearrange("p (a d) -> p a d", a=2)
        b0h = sb("b0h", [1, 2, 2, D], F16)
        onesh = sb("onesh", [1, 512], F16)
        ones = sb("ones", [1, P])
        identf = sb("identf", [P, P])
        identh = sb("identh", [P, P], F16)
        condr = sb("condr", [NB, D])
        condT = sb("condT", [P, NB])
        prod = sb("prod", [P, 2 * NB])
        prod_hi = sb("prod_hi", [P, 2 * NB], F16)
        prod_lo = sb("prod_lo", [P, 2 * NB], F16)
        yy = sb("yy", [P, NJ + 2, 3 * D])
        y, ysq = yy[:, 0:NJ, :], yy[:, NJ:NJ + 2, :]
        wada_s = ysq[:, :, :].rearrange("p a n -> p (a n)")
        badar = y[0:1, 0:2, :].rearrange("p a n -> p (a n)")
        ada = sb("ada", [NB, 6 * D])
        mod = sb("mod", [P, 2, NJ, 6 * D])
        wqkv = sb("wqkv", [P, 3 * D])
        bqkvb = sb("bqkvb", [P, 3 * D])
        wo_s = sb("wo_s", [P, D])
        bor = pr[0:1, 2, 0:D]
        boh = sb("boh", [1, 2, NC, D], F16)
        b2b = sb("b2b", [P, D])
        w1 = sb("w1", [P, FF])
        ffw = sb("ffw", [P, 4, 2 * D + 1])
        gw = sb("gw", [P, 2 * D + 1])
        gwrow = sb("gwrow", [1, D + 1])
        b12 = sb("b12", [P, D + 1])
        neg_half = sb("neg_half", [P, NC])
        half_ = sb("half_", [P, NC])
        mv = sb("mv", [P, 2, NT, 2])
        bnst = sb("bnst", [P, NJ, 6])
        bnst2 = sb("bnst2", [P, NJ, NC, 6])
        NS = 44
        stat = sb("stat", [P, NS, NT])
        tmp = sb("tmp", [P, 1 + NJ, 24, NC])
        itmp = sb("itmp", [P, 1 + NJ, 2, NC], I32)
        tw = sb("tw", [P, 3, NJ, D])
        tu, tus, tuT = tw[:, 0], tw[:, 1], tw[:, 2]
        NH2, NA2 = 2 * 3 * NH, 2 * 3 * NH + 2 * 3
        hsum = sb("hsum", [P, 2, NA2])
        hy = sb("hy", [P, 2, NA2])
        ht = sb("ht", [P, 2, NA2])
        hi32 = sb("hi32", [P, 2, NA2], I32)
        hfac = sb("hfac", [P, 2, NH2])
        qs = sb("qs", [P, 2, 2, NH, 4, HD], F16)
        KT = sb("KT", [P, 4, NB, 2, P], F16)
        QT = sb("QT", [P, NJ, 4, NC * P], F16)
        V = sb("V", [P, NB, 2, NH, VP])
        O = sb("O", [P, NJ, 2, NC * P])
        rec = sb("rec", [P, NJ, 2, 2 * NH])
        def tiles_of(flat, k):
            n = NC * D
            return flat[:, n * k:n * k + n].rearrange("p (c d) -> p c d", d=D)

        flat_y = yy.rearrange("p a n -> p (a n)")
        flat_w = tw.rearrange("p a j d -> p (a j d)")
        flat_e = early.rearrange("p a c d -> p (a c d)")

        def tail_buffer(n, flat, k):
            return [tiles_of(state, 2 * n), tiles_of(state, 2 * n + 1), tiles_of(flat, k),
                    tiles_of(flat, k + 1)]

        T_O = tail_buffer(0, xT, 0)
        T_OT = tail_buffer(1, xT, 2)
        T_M = tail_buffer(2, flat_y, 0)
        T_X = tail_buffer(3, flat_y, 2)
        T_F = tail_buffer(4, flat_w, 0)
        T_R = tail_buffer(5, flat_e, 0)
        scr_a = sb("scr_a", [P, 4, D])

        zb = ctx.enter_context(nc.psum_tensor("zb", [P, 2, 2, 512], F32))
        tb = ctx.enter_context(nc.psum_tensor("tb", [P, 2, 512], F32))
        firsts = ctx.enter_context(nc.psum_tensor("firsts", [P, 2, 512], F32))
        sbk, ob = firsts[:, 0, :], firsts[:, 1, :]

        def z_bank(t, k):
            if t < FIRST:
                return (sbk, ob)[k]
            return zb[:, t // CH % 2, k, :]

        def xT_bank(c):
            return tb[:, 1, :] if c == 0 else sbk[:, :]

        def score_bank(g):
            part = GROUPS[g][0]
            if part == 0:
                return 0, sbk[:, :]
            if part == 1:
                return 1 + g % 2, zb[:, 0, g % 2, :]
            return ((1, zb[:, 0, 0, :]), (2, zb[:, 0, 1, :]), (0, sbk[:, :]))[g % 3]

        def o_bank(part, b):
            return ob[:, :] if part < 2 else zb[:, 1, b % 2, :]

        def tail_bank(j, user):
            return (tb[:, 0, :], tb[:, 1, :], ob[:, :])[TURN[j, user] % 3]

        GROUPS = att_groups()

        load_scan, load_x0 = sem("load_scan"), sem("load_x0")
        load_x, load_rest = sem("load_x"), sem("load_rest")
        consts = sem("consts")
        consts16 = sem("consts16")
        pool_init = sem("pool_init")
        x_split, w_split = sem("x_split"), sem("w_split")
        condT_ps, condT_sb = sem("condT_ps"), sem("condT_sb")
        xT_ps, xT_sb = sem("xT_ps"), sem("xT_sb")
        hi_ready, lo_ready = sem("hi_ready"), sem("lo_ready")
        gate_z, cand_z = sem("gate_z"), sem("cand_z")
        products = sem("products")
        step_in = sem("step_in")
        ada_ps, ada_sb, ada_dr, mod_in = sem("ada_ps"), sem("ada_sb"), sem("ada_dr"), sem("mod_in")
        w1T_ps, w1T_sb, gw_ps, gw_sb = sem("w1T_ps"), sem("w1T_sb"), sem("gw_ps"), sem("gw_sb")
        beta_ps, beta_sb = sem("beta_ps"), sem("beta_sb")
        bo_split = sem("bo_split")
        h_copied, h_transposed = sem("h_copied"), sem("h_transposed")
        dve_done, act_done, pool_done = sem("dve_done"), sem("act_done"), sem("pool_done")
        tok_moments, tok_norm, tok_a, tok_rho = sem("tok_moments"), sem("tok_norm"), sem("tok_a"), sem("tok_rho")
        tok_xn, tok_u, tok_u2, tok_usq, tok_clip = (sem("tok_xn"), sem("tok_u"), sem("tok_u2"),
                                                    sem("tok_usq"), sem("tok_clip"))
        tok_uT_ps, tok_uT = sem("tok_uT_ps"), sem("tok_uT")
        qkv_ps, qkv_copied, qkv_squared = sem("qkv_ps"), sem("qkv_copied"), sem("qkv_squared")
        qkv_reduced, factor_bits = sem("qkv_reduced"), sem("factor_bits")
        roots, factors = sem("roots"), sem("factors")
        qk_scaled, v_scaled, split_high, split_low = (sem("qk_scaled"), sem("v_scaled"),
                                                      sem("split_high"), sem("split_low"))
        stack_ps, q_stack, k_stack = sem("stack_ps"), sem("q_stack"), sem("k_stack")
        scores_ready, probs_ready, pv_done = sem("scores_ready"), sem("probs_ready"), sem("pv_done")
        o_saved = sem("o_saved")
        ot_ps, o_ready, oT_ps, oT_sb = sem("ot_ps"), sem("o_ready"), sem("oT_ps"), sem("oT_sb")
        wo_ps, wo_sq, att_sq, att_dot = sem("wo_ps"), sem("wo_sq"), sem("att_sq"), sem("att_dot")
        att_m, gy_saved = sem("att_m"), sem("gy_saved")
        att_n, att_th, att_co, att_scaled = sem("att_n"), sem("att_th"), sem("att_co"), sem("att_scaled")
        v_moments, v_norm, v_a, v_rho = sem("v_moments"), sem("v_norm"), sem("v_a"), sem("v_rho")
        v_xn, v_xn2, v_u = sem("v_xn"), sem("v_xn2"), sem("v_u")
        v_usq, v_clip, v_uT_ps, v_uT = sem("v_usq"), sem("v_clip"), sem("v_uT_ps"), sem("v_uT")
        g_ps, t2_ps, gy_ps, f1_dot, f1_sum, f1_clip = (sem("g_ps"), sem("t2_ps"), sem("gy_ps"),
                                                       sem("f1_dot"), sem("f1_sum"), sem("f1_clip"))
        ff_dot = sem("ff_dot")
        f2_y, f2_sq, ff_m, ff_sq = sem("f2_y"), sem("f2_sq"), sem("ff_m"), sem("ff_sq")
        ff_n, ff_th, ff_co, ff_scaled = sem("ff_n"), sem("ff_th"), sem("ff_co"), sem("ff_scaled")
        block_out, res_ready, last_out = sem("block_out"), sem("res_ready"), sem("last_out")
        stored = [sem(f"stored_{j}") for j in range(NJ)]

        names = {}

        def st(name, sel):
            k = names.setdefault(name, len(names))
            assert k < NS
            return stat[:, k, sel]

        def tok_tiles(c):
            return slice(c, NT, NC)

        def tok_tile(c, j):
            return slice(NC * j + c, NC * j + c + 1)

        def pair_tiles(j):
            return slice(NC * j, NC * j + NC)

        def head_factors(eng, q, settled, fused):
            x, r, t = hsum[:, q, :], hy[:, q, :], ht[:, q, :]
            eng.tensor_scalar(x, x, 1.2e-38, None, ALU.max)
            settled(eng.tensor_scalar(r.bitcast(I32), hi32[:, q, :], -1.0, float(0x5F3759DF), ALU.mult,
                                      ALU.add))
            for _ in range(3):
                settled(eng.tensor_tensor(t, r, r, ALU.mult))
                if fused:
                    settled(eng.scalar_tensor_tensor(t, t, -0.5, x, ALU.mult, ALU.mult))
                    settled(eng.scalar_tensor_tensor(r, t, 1.5, r, ALU.add, ALU.mult))
                else:
                    settled(eng.tensor_tensor(t, t, x, ALU.mult))
                    settled(eng.tensor_scalar(t, t, -0.5, 1.5, ALU.mult, ALU.add))
                    settled(eng.tensor_tensor(r, t, r, ALU.mult))
            return eng.tensor_scalar(t[:, NH2:NA2], r[:, NH2:NA2], C_HEAD * M_CLIP, C_HEAD, ALU.mult,
                                     ALU.min)

        def q_cols(base, b, chunks):
            s = b % 2
            if len(chunks) == 1:
                c = chunks[0]
                return view(base[:, P * c + CH * (s ^ (c & 1)):P * c + CH * (s ^ (c & 1)) + 1],
                            [1, CH])
            first = base[:, CH * s:CH * s + 1]
            if len(chunks) == 2:
                return view(first, [CH * (3 - 2 * s), 2], [1, CH])
            return view(first, [2 * P, 2], [CH * (3 - 2 * s), 2], [1, CH])

        def at_ticks(now, start):
            while now[0] < start:
                yield

        def run(step, workers):
            now = [0]
            live = [w(now) for w in workers]
            for t in range(END):
                now[0] = t
                if t < STEPS:
                    step(t)
                for w in list(live):
                    if next(w, w) is w:
                        live.remove(w)
            assert not live

        block = ctx.enter_context(nc.Block())

        def tile_dma(eng, dram, sbuf, c, slot, to_dram):
            par = c & 1
            d = bass.AP(dram.tensor, ((slot ^ par) * STEPS + CH * c) * D,
                        [[D, CH], [2 * STEPS * D, NJ], [1, D]])
            s = sbuf[CH * slot:CH * slot + CH, NJ * c:NJ * c + NJ, :]
            return eng.dma_start(d, s) if to_dram else eng.dma_start(s, d)

        def row(ap):
            return ap.rearrange("(a n) -> a n", a=1)

        @block.sync
        def _(sp):
            sp.dma_start(w0h[:, :], w0[D:2 * D, :]).then_inc(load_scan, 16)
            sp.dma_start(condr[:, :], cond).then_inc(load_scan, 16)
            sp.dma_start(b0row[:, :], row(b0)).then_inc(load_scan, 16)
            sp.dma_start(w0x[:, :], w0[0:D, :]).then_inc(load_scan, 16)
            for c in range(1, NC):
                for slot in range(2):
                    tile_dma(sp, x, resid, c, slot, False).then_inc(load_x, 16)
            sp.dma_start(wada_s[:, :], wada).then_inc(load_rest, 16)
            sp.dma_start(badar[:, :], row(bada)).then_inc(load_rest, 16)
            for n, (w, b) in enumerate(((wq, bq), (wk, bk), (wv, bv))):
                sp.dma_start(wqkv[:, D * n:D * n + D], w).then_inc(load_rest, 16)
                sp.dma_start(bqkvb[:, D * n:D * n + D], bass.AP(b.tensor, 0, [[0, P], [1, D]]))\
                  .then_inc(load_rest, 16)
            sp.dma_start(wo_s[:, :], wo).then_inc(load_rest, 16)
            sp.dma_start(bor[:, :], row(bo)).then_inc(load_rest, 16)
            sp.dma_start(w1[:, :], wf1).then_inc(load_rest, 16)
            sp.dma_start(ffw[:, :, D:2 * D], wf2.rearrange("(k p) n -> p k n", p=P)).then_inc(load_rest, 16)
            sp.dma_start(ffw[:, :, 2 * D:2 * D + 1], bf1.rearrange("(k p a) -> p k a", p=P, a=1),
                         allow_slow_non_contiguous=True)\
              .then_inc(load_rest, 16)
            sp.dma_start(b2b[:, :], bass.AP(bf2.tensor, 0, [[0, P], [1, D]])).then_inc(load_rest, 16)
            sp.wait_ge(ada_sb, 1)
            sp.dma_start(ada_dram, ada[:, :]).then_inc(ada_dr, 16)
            sp.wait_ge(ada_dr, 16)
            for par in range(2):
                for slot in range(2):
                    sp.dma_start(mod[CH * slot:CH * slot + CH, par, :, :],
                                 bass.AP(ada_dram.tensor, (slot ^ par) * 6 * D,
                                         [[0, CH], [2 * 6 * D, NJ], [1, 6 * D]])).then_inc(mod_in, 16)
            for j in range(NJ):
                if j < NJ - 1:
                    sp.wait_ge(res_ready, j + 1)
                for par in range(2):
                    if j == NJ - 1:
                        sp.wait_ge(last_out, par + 1)
                    for slot in range(2):
                        sp.dma_start(
                            bass.AP(out.tensor, (batch_of(par, j, slot) * STEPS + CH * par) * D,
                                    [[D, CH], [2 * CH * D, NC // 2], [1, D]]),
                            T_R[j][CH * slot:CH * slot + CH, par:NC:2, :])\
                          .then_inc(stored[j], 16)
            for j in range(NJ):
                sp.wait_ge(stored[j], 16 * 4)

        LOADS_REST = 16 * 14

        @block.gpsimd
        def _(pool):
            for slot in range(2):
                tile_dma(pool, x, resid, 0, slot, False).then_inc(load_x0, 16)
            done = [0]

            def settled(ins):
                done[0] += 1
                ins.then_inc(pool_done, 1)
                pool.wait_ge(pool_done, done[0])

            settled(pool.memset(identf[:, :], 0.0))
            pool.affine_select(out=identf[:, :], in_=identf[:, :], compare_op=ALU.not_equal, fill=1.0,
                               base=0, pattern=[[-1, P]], channel_multiplier=1).then_inc(consts, 1)
            settled(pool.memset(identh[:, :], 0.0))
            pool.affine_select(out=identh[:, :], in_=identh[:, :], compare_op=ALU.not_equal, fill=1.0,
                               base=0, pattern=[[-1, P]], channel_multiplier=1).then_inc(consts16, 1)
            pool.memset(neg_half[:, :], -0.5)
            pool.memset(half_[:, :], 0.5)
            settled(pool.memset(V[:, :, :, :, :], 0.0))
            pool.memset(V[:, :, :, :, HD:HD + 1], C_HEAD)
            pool.memset(O[:, :, :, (NC - 1) * P:NC * P], 0.0).then_inc(pool_init, 1)

            def times(dst, a, b):
                return pool.tensor_tensor(dst, a, b, ALU.mult)

            def inverse_root(dst, sums):
                n = sums.free_size()
                settled(pool.tensor_scalar(dst, sums, 1e-14, None, ALU.max))
                settled(pool.tensor_tensor(dst, dst, neg_half[:, 0:n], ALU.pow))

            def clip_factor(dst, sums):
                inverse_root(dst, sums)
                return pool.tensor_scalar(dst, dst, M_CLIP, 1.0, ALU.mult, ALU.min)

            def ln_norm(k, sel, tag, ready, wait):
                mean, var = mv[:, k, sel, 0], mv[:, k, sel, 1]
                ss, cl = st("ss" + tag, sel), st("cl" + tag, sel)
                n = ss.free_size()
                pool.wait_ge(*wait)
                settled(times(ss, mean, mean))
                settled(pool.tensor_tensor(ss, ss, var, ALU.add))
                settled(pool.tensor_scalar(ss, ss, float(D), 1e-14, ALU.mult, ALU.max))
                settled(pool.tensor_tensor(cl, ss, half_[:, 0:n], ALU.pow))
                pool.tensor_scalar(cl, cl, MAXT, None, ALU.min).then_inc(ready, 1)

            def ln_rho(k, sel, tag, wait):
                rho, off = st("rho" + tag, sel), st("off" + tag, sel)
                pool.wait_ge(*wait)
                settled(pool.tensor_tensor(rho, st("va" + tag, sel), neg_half[:, 0:rho.free_size()],
                                           ALU.pow))
                settled(times(off, mv[:, k, sel, 0], rho))
                return pool.tensor_scalar(off, off, -1.0, None, ALU.mult)

            def pool_xn(dst, src, tag, col):
                return pool.tensor_scalar(dst, src, st("rho" + tag, col), st("off" + tag, col),
                                          ALU.mult, ALU.add)

            def tokens(now):
                pool.wait_ge(mod_in, 64)
                for c in range(NC):
                    base, sel = tok_base(c), tok_tiles(c)
                    yield from at_ticks(now, base + TOK["norm"])
                    ln_norm(0, sel, "1", tok_norm, (tok_moments, c + 1))
                    yield from at_ticks(now, base + TOK["rho"])
                    ln_rho(0, sel, "1", (tok_a, c + 1)).then_inc(tok_rho, 1)
                    pool.wait_ge(tok_rho, c + 1)
                    yield from at_ticks(now, base + TOK["xn"])
                    if c:
                        pool.wait_ge(tok_uT_ps, c)
                    for j in range(2):
                        i = pool_xn(tu[:, j, :], resid[:, NJ * c + j, :], "1", tok_tile(c, j))
                    settled(i)
                    settled(times(tu[:, 0:2, :], tu[:, 0:2, :], mod[:, c & 1, 0:2, D:2 * D]))
                    pool.tensor_tensor(tu[:, 0:2, :], tu[:, 0:2, :], mod[:, c & 1, 0:2, 0:D],
                                       ALU.add).then_inc(tok_u, 1)
                    yield from at_ticks(now, base + TOK["clip"])
                    pool.wait_ge(tok_usq, c + 1)
                    clip_factor(st("uclip1", sel), st("usq1", sel)).then_inc(tok_clip, 1)
                    for q in range(2):
                        yield from at_ticks(now, base + TOK["factor"][q])
                        if (c, q) != (NC - 1, 1):
                            pool.wait_ge(factor_bits, 2 * c + q + 1)
                            head_factors(pool, q, settled, False).then_inc(roots, 1)
                    for q in range(2):
                        yield from at_ticks(now, base + TOK["values"][q])
                        pool.wait_ge(factors, 2 * c + q + 1)
                        for j in (2 * q, 2 * q + 1):
                            for slot in range(2):
                                pp = slice(CH * slot, CH * slot + CH)
                                fv = view(hfac[pp, q, 48 * (j % 2) + 32:48 * (j % 2) + 33], [1, NH],
                                          [0, HD])
                                i = times(V[pp, batch_of(c, j, slot), c // 2, :, 0:HD],
                                          y[pp, j, 2 * D:3 * D].rearrange("p (h d) -> p h d", d=HD), fv)
                                if slot == 0:
                                    settled(i)
                            i.then_inc(v_scaled, 1)
                            pool.wait_ge(v_scaled, NJ * c + j + 1)

            def tail(j):
                def work(now):
                    sel, base, T = pair_tiles(j), tail_base(j), tail_of(j)

                    def vector_norms(clip, sq, msq, n, rn):
                        settled(clip_factor(clip, sq))
                        settled(times(n, msq, clip))
                        settled(times(n, n, clip))
                        settled(pool.tensor_scalar(n, n, 1e-14, None, ALU.max))
                        settled(pool.tensor_tensor(rn, n, neg_half[:, :], ALU.pow))
                        return times(n, n, rn)

                    yield from at_ticks(now, base + T["norm"])
                    pool.wait_ge(wo_sq, j + 1)
                    pool.wait_ge(att_sq, j + 1)
                    vector_norms(st("oclip", sel), st("osq", sel), st("asq", sel), st("an", sel),
                                 st("arn", sel)).then_inc(att_n, 1)
                    yield from at_ticks(now, base + T["norm2"])
                    ln_norm(1, sel, "2", v_norm, (v_moments, j + 1))
                    yield from at_ticks(now, base + T["rho2"])
                    ln_rho(1, sel, "2", (v_a, j + 1)).then_inc(v_rho, 1)
                    pool.wait_ge(v_rho, j + 1)
                    yield from at_ticks(now, base + T["xn"])
                    for c in range(2):
                        i = pool_xn(T_O[j][:, c, :], T_X[j][:, c, :], "2", tok_tile(c, j))
                    i.then_inc(v_xn, 1)
                    yield from at_ticks(now, base + T["clip2"])
                    pool.wait_ge(v_usq, j + 1)
                    clip_factor(st("uclip2", sel), st("usq2", sel)).then_inc(v_clip, 1)
                    yield from at_ticks(now, base + T["clip3"])
                    pool.wait_ge(f1_sum, j + 1)
                    clip_factor(st("fc1", sel), st("fsq1", sel)).then_inc(f1_clip, 1)
                    yield from at_ticks(now, base + T["norm3"])
                    pool.wait_ge(f2_sq, j + 1)
                    pool.wait_ge(ff_sq, j + 1)
                    vector_norms(st("fclip", sel), st("fsq2", sel), st("fsq3", sel), st("fn", sel),
                                 st("frn", sel)).then_inc(ff_n, 1)
                    if j == NJ - 1:
                        return
                    yield from at_ticks(now, base + T["add"])
                    pool.wait_ge(block_out, NC * j + NC)
                    pool.tensor_tensor(T_R[j], T_R[j], view(resid[:, j, 0:1], [NJ * D, NC], [1, D]),
                                       ALU.add).then_inc(res_ready, 1)
                return work

            tails = [tail(j) for j in range(NJ)]
            run(lambda t: None, [tokens, *tails])

        @block.tensor
        def _(pe):
            def transpose(dst, src, ident):
                k = src.ap[0][1]
                return pe.transpose(dst, src, ident[0:k, 0:k])

            def x_transposes(c):
                if c == 0:
                    pe.wait_ge(load_x0, 32)
                else:
                    pe.wait_ge(load_x, 32 * (NC - 1))
                    pe.wait_ge(xT_sb, c)
                for j in range(NJ):
                    i = transpose(xT_bank(c)[:, D * j:D * j + D], resid[:, NJ * c + j, :], identf)
                i.then_inc(xT_ps, 1)

            def first_x_part():
                n = NB * FIRST
                for k in range(2):
                    pe.matmul(z_bank(0, k)[:, 0:n], w0s[:, k, :], xT[:, 0:n], start=True, stop=False,
                              skip_group_check=True)
                    for half in range(2):
                        pe.matmul(z_bank(0, k)[:, 0:n], b0h[:, half, k, :], onesh[:, 0:n],
                                  start=False, stop=False, skip_group_check=True)

            def x_part(c):
                for k in range(2):
                    for q in range(1 if c == 0 else 0, 4):
                        if k == 0 and c and q == 0:
                            pe.wait_ge(xT_sb, c + 1)
                        pe.matmul(zb[:, c % 2, k, 128 * q:128 * q + 128], w0s[:, k, :],
                                  xT[:, 512 * c + 128 * q:512 * c + 128 * q + 128],
                                  start=(q == (1 if c == 0 else 0)), stop=False,
                                  skip_group_check=True)
                        yield
                    for half in range(2):
                        pe.matmul(zb[:, c % 2, k, :], b0h[:, half, k, :], onesh[:, :],
                                  start=False, stop=False, skip_group_check=True)
                        yield

            pe.wait_ge(load_scan, 64)
            pe.wait_ge(consts, 1)
            transpose(tb[:, 0, 0:NB], condr[:, :], identf).then_inc(condT_ps, 1)
            x_transposes(0)
            pe.wait_ge(x_split, 1)
            pe.wait_ge(xT_sb, 1)
            first_x_part()

            def z_part(src, half, k, t):
                for p in range(2):
                    i = pe.matmul(z_bank(t, k)[:, NB * (t % CH):NB * (t % CH) + NB],
                                  whh[:, half, p, k, :], src[:, NB * p:NB * p + NB],
                                  start=False, stop=False, skip_group_check=True)
                return i

            def step(t):
                pe.wait_ge(hi_ready, t + 1)
                for k in (1, 0):
                    for half in range(2):
                        z_part(prod_hi, half, k, t)
                pe.wait_ge(lo_ready, t + 1)
                z_part(prod_lo, 0, 1, t).then_inc(gate_z, 1)
                z_part(prod_lo, 0, 0, t).then_inc(cand_z, 1)

            def prepare(now):
                yield from at_ticks(now, 1)
                yield from x_part(0)
                yield from at_ticks(now, 12)
                pe.wait_ge(load_rest, LOADS_REST)
                for h in range(2):
                    for q in range(3):
                        cols = slice(384 * h + 128 * q, 384 * h + 128 * q + 128)
                        pe.matmul(tb[0:NB, h, 128 * q:128 * q + 128], condT[:, :], wada_s[:, cols],
                                  start=(q == 0), stop=False, skip_group_check=True)
                        i = pe.matmul(tb[0:NB, h, 128 * q:128 * q + 128], ones[:, 0:NB],
                                      badar[:, cols], start=False, stop=True,
                                      skip_group_check=True)
                        yield
                i.then_inc(ada_ps, 1)
                for c in range(1, NC):
                    yield from at_ticks(now, 16 + 3 * c)
                    x_transposes(c)
                yield from at_ticks(now, 27)
                yield from x_part(1)
                for k in range(4):
                    i = transpose(ob[:, D * k:D * k + D], w1[:, D * k:D * k + D], identf)
                    yield
                i.then_inc(w1T_ps, 1)
                yield from at_ticks(now, 45)
                pe.wait_ge(w1T_sb, 1)
                for k in range(4):
                    for cols in (slice(0, D), slice(D, 2 * D + 1)):
                        pe.matmul(sbk[:, cols], ffw[:, k, 0:D], ffw[:, k, cols],
                                  start=(k == 0 and cols.start == 0), stop=(k == 3),
                                  skip_group_check=True)
                        yield
                for k in range(4):
                    i = pe.matmul(ob[0:1, 0:2 * D + 1], ffw[:, k, 2 * D:2 * D + 1], ffw[:, k, :],
                                  start=(k == 0), stop=(k == 3))
                    yield
                i.then_inc(gw_ps, 1)
                yield from at_ticks(now, 59)
                pe.wait_ge(gw_sb, 1)
                pe.matmul(sbk[:, 0:D + 1], ones[:, :], gwrow[:, :], start=True, stop=True)\
                    .then_inc(beta_ps, 1)
                for c in range(2, NC):
                    yield from at_ticks(now, CH * (c - 1) + 4)
                    yield from x_part(c)

            def tokens(now):
                pe.wait_ge(consts16, 1)
                for c in range(NC):
                    base = tok_base(c)
                    yield from at_ticks(now, base + TOK["transpose"])
                    if c == 0:
                        pe.wait_ge(ada_sb, 1)
                    else:
                        pe.wait_ge(q_stack, NT // NC * c)
                        pe.wait_ge(k_stack, NT // NC * c)
                    pe.wait_ge(h_copied, c + 1)
                    for j in range(NJ):
                        i = transpose(tb[:, 0, D * j:D * j + D], tus[:, j, :], identf)
                        if j == 1:
                            yield
                    i.then_inc(h_transposed, 1)
                    yield from at_ticks(now, base + TOK["utrans"])
                    pe.wait_ge(tok_u2, c + 1)
                    for j in (2, 3, 0, 1):
                        i = transpose(tb[:, 1, D * j:D * j + D], tu[:, j, :], identf)
                        if j == 3:
                            yield
                            pe.wait_ge(tok_u, c + 1)
                    i.then_inc(tok_uT_ps, 1)
                    for j in range(NJ):
                        for n in range(2):
                            yield from at_ticks(now, base + TOK["qkv"] + 2 * j + n)
                            if n == 0:
                                pe.wait_ge(tok_uT, c + 1)
                                if j >= 2:
                                    pe.wait_ge(qkv_copied, NJ * c + j - 1)
                            i = pe.matmul(tb[:, j % 2, 192 * n:192 * n + 192], tuT[:, j, :],
                                          wqkv[:, 192 * n:192 * n + 192], start=(n == 0), stop=(n == 1),
                                          skip_group_check=True)
                        i.then_inc(qkv_ps, 1)
                    for j in range(NJ):
                        yield from at_ticks(now, base + TOK["stack"][j])
                        n = NJ * c + j
                        pe.wait_ge(split_low, n + 1)
                        if j < 2:
                            pe.wait_ge(qkv_copied, NJ * c + NJ)
                        else:
                            pe.wait_ge(k_stack, n - 1)
                        bank = tb[:, j % 2, :].bitcast(F16)
                        for k in range(2):
                            src = qs[:, n % 2, k].rearrange("p h s d -> p (h s d)")
                            for g in range(4):
                                i = transpose(bank[:, 512 * k + 128 * g:512 * k + 128 * g + 128],
                                              src[:, 128 * g:128 * g + 128], identh)
                            if k == 0:
                                yield
                        i.then_inc(stack_ps, 1)

            def attention(now):
                last = {}
                started = set()

                def values(gs):
                    pe.wait_ge(probs_ready, gs[-1] + 1)
                    part, b, i, _, kb, chunks, _ = GROUPS[gs[0]]
                    nq = CH * len(chunks)
                    if i == 0 and (b, part) not in started:
                        started.add((b, part))
                        if part < 2:
                            if NB * part + b:
                                pe.wait_ge(o_saved, NB * part + b)
                            else:
                                pe.wait_ge(beta_sb, 1)
                        elif b >= 2:
                            pe.wait_ge(o_saved, 2 * NB + b - 1)
                        else:
                            pe.wait_ge(step_in, 2 * STEPS)
                        if part != 1:
                            pe.wait_ge(v_scaled, NJ * (3 if part == 2 else 1) + b // 2 + 1)
                    bank = o_bank(part, b)
                    c0 = 256 * (i // 2) if part == 2 else 128 * (i // 2)
                    if part == 2 and kb == 0:
                        c0 += 192
                    for g in gs:
                        for n, hg in enumerate(GROUPS[g][3]):
                            hd = NI * hg + i
                            window = view(V[:, b, kb, hd, 0:1], [1, VP])
                            if i % 2:
                                window = view(V[:, b, kb, hd - 1, VC:VC + 1], [1, VP])
                            ins = pe.matmul(bank[VW * hg:VW * hg + VP, c0:c0 + nq], window,
                                            pr[:, g % 4, nq * n:nq * n + nq],
                                            start=(i == 0 and kb == 0), stop=False,
                                            skip_group_check=True)
                    ins.then_inc(pv_done, len(gs))

                def scores(g):
                    part, b, i, hgs, kb, chunks, _ = GROUPS[g]
                    nq = CH * len(chunks)
                    c_need = {0: 1, 1: 2, 2: 3}[part]
                    pe.wait_ge(q_stack, NJ * c_need + b // 2 + 1)
                    pe.wait_ge(k_stack, NJ * c_need + b // 2 + 1)
                    k, bank = score_bank(g)
                    if k in last:
                        pe.wait_ge(probs_ready, last[k] + 1)
                    elif part == 0:
                        pe.wait_ge(beta_sb, 1)
                    last[k] = g
                    for n, hg in enumerate(hgs):
                        rows = slice(STACK * i, STACK * i + STACK)
                        q = q_cols(QT[rows, b // 2, hg, :], b, chunks)
                        ins = pe.matmul(bank[:, nq * n:nq * n + nq], KT[rows, hg, b, kb, :], q,
                                        start=(n == 0), stop=(n == len(hgs) - 1),
                                        skip_group_check=True)
                    ins.then_inc(scores_ready, 1)

                pe.wait_ge(pool_init, 1)
                waiting = []

                def oldest():
                    n = 2 if GROUPS[waiting[0]][4] == 1 else 1
                    return n

                for g in range(len(GROUPS)):
                    yield from at_ticks(now, GROUPS[g][6])
                    scores(g)
                    waiting.append(g)
                    if GROUPS[g][0] == 0:
                        yield
                    while len(waiting) >= oldest() + (1 if GROUPS[g][0] == 0 else 2):
                        n = oldest()
                        values(waiting[:n])
                        del waiting[:n]
                yield from at_ticks(now, GROUPS[-1][6] + 2)
                while waiting:
                    n = oldest()
                    values(waiting[:n])
                    del waiting[:n]

            def tail(j):
                def work(now):
                    base, T = tail_base(j), tail_of(j)

                    def bank(user):
                        n = TURN[j, user] - 3
                        if n >= 0:
                            _, i, before = USES[n]
                            pe.wait_ge(*{"ot0": (o_ready, NC * i + 2), "ot1": (o_ready, NC * i + 4),
                                         "oT": (oT_sb, i + 1), "wo": (wo_sq, i + 1),
                                         "uT": (v_uT, i + 1), "g": (f1_dot, i + 1),
                                         "t2": (f1_sum, i + 1), "gy": (gy_saved, i + 1)}[before])
                        return tail_bank(j, user)

                    def products(user, left, right):
                        b = bank(user)
                        for c in range(NC):
                            ins = pe.matmul(b[:, D * c:D * c + D], left[:, c, :], right,
                                            start=(c == 0), stop=True, skip_group_check=True)
                        return ins

                    def transposes(user, src):
                        b = bank(user)
                        for c in range(NC):
                            ins = transpose(b[:, D * c:D * c + D], src[:, c, :], identf)
                        return ins

                    for q in range(2):
                        yield from at_ticks(now, base + T["ot"][q])
                        if q == 0:
                            pe.wait_ge(o_saved, 2 * NB + 2 * (j + 1))
                            if j == 0:
                                pe.wait_ge(k_stack, NT)
                        b = bank(f"ot{q}")
                        for c in (2 * q, 2 * q + 1):
                            for i in range(2):
                                c0 = 2 * P * (c % 2) + P * i
                                ins = transpose(b[:, c0:c0 + P], O[:, j, i, P * c:P * c + P], identf)
                        ins.then_inc(ot_ps, 1)
                    yield from at_ticks(now, base + T["oT"])
                    pe.wait_ge(o_ready, NC * j + NC)
                    transposes("oT", T_O[j]).then_inc(oT_ps, 1)
                    yield from at_ticks(now, base + T["wo"])
                    pe.wait_ge(oT_sb, j + 1)
                    pe.wait_ge(bo_split, 1)
                    b = bank("wo")
                    for half in range(2):
                        pe.matmul(b, onesh[:, 0:P], boh[:, half].rearrange("p c d -> p (c d)"),
                                  start=(half == 0), stop=False, skip_group_check=True)
                    for c in range(NC):
                        ins = pe.matmul(b[:, D * c:D * c + D], T_OT[j][:, c, :], wo_s[:, :], start=False,
                                        stop=True, skip_group_check=True)
                    ins.then_inc(wo_ps, 1)
                    yield from at_ticks(now, base + T["utrans"])
                    pe.wait_ge(v_u, j + 1)
                    transposes("uT", T_O[j]).then_inc(v_uT_ps, 1)
                    yield from at_ticks(now, base + T["g"])
                    pe.wait_ge(v_uT, j + 1)
                    products("g", T_OT[j], gw[:, 0:D]).then_inc(g_ps, 1)
                    yield from at_ticks(now, base + T["t2"])
                    b = bank("t2")
                    for c in range(NC):
                        ins = pe.matmul(b[:, c:c + 1], T_OT[j][:, c, :], gw[:, 2 * D:2 * D + 1],
                                        start=(c == 0), stop=True, skip_group_check=True)
                    ins.then_inc(t2_ps, 1)
                    yield from at_ticks(now, base + T["gy"])
                    products("gy", T_OT[j], gw[:, D:2 * D]).then_inc(gy_ps, 1)
                return work

            tails = [tail(j) for j in range(NJ)]
            run(step, [prepare, tokens, attention, *tails])

        @block.scalar
        def _(act):
            done = [0]

            def settled(ins):
                done[0] += 1
                ins.then_inc(act_done, 1)
                act.wait_ge(act_done, done[0])

            act.wait_ge(condT_ps, 1)
            act.activation(state[:, 0:NB], tb[:, 0, 0:NB], ACT.Copy, scale=2.0).then_inc(condT_sb, 1)
            act.activation(condT[:, :], tb[:, 0, 0:NB], ACT.Copy).then_inc(condT_sb, 1)

            def copy_xT(c):
                act.wait_ge(xT_ps, c + 1)
                first = xT[:, STEPS // NC * NB * c + batch_of(c, 0, 0):][:, 0:1]
                s = batch_of(c, 0, 1) - batch_of(c, 0, 0)
                act.activation(view(first, [2, NJ], [s, 2], [NB, CH]),
                               xT_bank(c).rearrange("p (j s t) -> p j s t", j=NJ, s=2),
                               ACT.Copy).then_inc(xT_sb, 1)

            copy_xT(0)

            def step(t):
                r = state[:, SW * t:SW * t + 32]
                k = NB * (t % CH)
                act.wait_ge(gate_z, t + 1)
                act.activation(r[:, 24:32], z_bank(t, 1)[:, k:k + NB], ACT.Tanh, scale=-1.0 / ZS)
                act.wait_ge(cand_z, t + 1)
                z = firsts[:, :, k:k + NB] if t < FIRST else zb[:, t // CH % 2, :, k:k + NB]
                act.activation(r[:, 8:24].rearrange("p (a b) -> p a b", a=2), z, ACT.Tanh,
                               scale=1.0 / ZS).then_inc(step_in, 1)

            def prepare(now):
                yield from at_ticks(now, 18)
                act.wait_ge(ada_ps, 1)
                act.activation(ada[:, 0:384], tb[0:NB, 0, 0:384], ACT.Copy)
                settled(act.activation(ada[:, 384:768], tb[0:NB, 1, 0:384], ACT.Copy))
                act.activation(ada[:, D:2 * D], ada[:, D:2 * D], ACT.Copy, bias=1.0)
                act.activation(ada[:, 4 * D:5 * D], ada[:, 4 * D:5 * D], ACT.Copy, bias=1.0)\
                    .then_inc(ada_sb, 1)
                for c in range(1, NC):
                    yield from at_ticks(now, 17 + 3 * c)
                    copy_xT(c)
                yield from at_ticks(now, 43)
                act.wait_ge(w1T_ps, 1)
                act.activation(ffw[:, :, 0:D], ob[:, :].rearrange("p (k n) -> p k n", k=4), ACT.Copy)\
                    .then_inc(w1T_sb, 1)
                yield from at_ticks(now, 58)
                act.wait_ge(gw_ps, 1)
                act.activation(gw[:, 0:2 * D], sbk[:, 0:2 * D], ACT.Copy)
                act.activation(gw[:, 2 * D:2 * D + 1], sbk[:, 2 * D:2 * D + 1], ACT.Copy, scale=2.0)
                act.activation(gwrow[:, :], ob[0:1, D:2 * D + 1], ACT.Copy).then_inc(gw_sb, 1)
                yield from at_ticks(now, 61)
                act.wait_ge(beta_ps, 1)
                act.activation(b12[:, :], sbk[:, 0:D + 1], ACT.Copy).then_inc(beta_sb, 1)

            def tokens(now):
                for c in range(NC):
                    base, sel = tok_base(c), tok_tiles(c)
                    tiles = range(NJ * c, NJ * c + NJ)
                    yield from at_ticks(now, base + TOK["hcopy"])
                    act.wait_ge(step_in, 2 * CH * (c + 1) + (1 if c < NC - 1 else 0))
                    first = state[:, SW * (CH * c + 1) + batch_of(c, 0, 0):][:, 0:1]
                    act.activation(tus[:, :, :].rearrange("p j (s t) -> p j s t", s=2),
                                   view(first, [2, NJ], [batch_of(c, 0, 1) - batch_of(c, 0, 0), 2],
                                        [SW, CH]), ACT.Copy).then_inc(h_copied, 1)
                    yield from at_ticks(now, base + TOK["xn"])
                    act.wait_ge(tok_rho, c + 1)
                    act.wait_ge(tok_moments, c + 1)
                    if c:
                        act.wait_ge(tok_uT_ps, c)
                    for j in (2, 3):
                        i = act.activation(tu[:, j, :], resid[:, NJ * c + j, :], ACT.Identity,
                                           scale=st("rho1", tok_tile(c, j)),
                                           bias=st("off1", tok_tile(c, j)))
                    i.then_inc(tok_xn, 1)
                    def squares_of(tiles):
                        for j in tiles:
                            i = act.activation(scr_a[:, j, :], tu[:, j, :], ACT.Square,
                                               accum_out=st("usq1", tok_tile(c, j)))
                        return i

                    yield from at_ticks(now, base + TOK["usq"][0])
                    act.wait_ge(tok_u2, c + 1)
                    squares_of((2, 3))
                    yield from at_ticks(now, base + TOK["usq"][1])
                    act.wait_ge(tok_u, c + 1)
                    squares_of((0, 1)).then_inc(tok_usq, 1)
                    yield from at_ticks(now, base + TOK["uevac"])
                    act.wait_ge(tok_uT_ps, c + 1)
                    act.activation(tuT[:, :, :], tb[:, 1, :].rearrange("p (j t) -> p j t", j=NJ),
                                   ACT.Copy).then_inc(tok_uT, 1)
                    for j in range(NJ):
                        n = NJ * c + j
                        yield from at_ticks(now, base + TOK["qsq"] + 2 * j)
                        act.wait_ge(qkv_copied, n + 1)
                        if n >= 2:
                            act.wait_ge(qkv_reduced, n - 1)
                        act.activation(ysq[:, n % 2, :], y[:, j, :], ACT.Square)\
                            .then_inc(qkv_squared, 1)

                    def high(j):
                        n = NJ * c + j
                        act.wait_ge(qk_scaled, n + 1)
                        if n >= 2:
                            act.wait_ge(stack_ps, n - 1)
                        for k in range(2):
                            src = view(y[:, j, D * k:D * k + 1], [HD, NH], [0, 2], [1, HD])
                            dst = view(qs[:, n % 2, k, 0, 0, 0:1], [4 * HD, NH], [(2, 1)[k] * HD, 2],
                                       [1, HD])
                            i = act.activation(dst, src, ACT.Copy)
                        i.then_inc(split_high, 1)

                    def queries(j):
                        act.wait_ge(stack_ps, NJ * c + j + 1)
                        act.activation(QT[:, j, :, P * c:P * c + P],
                                       tb[:, j % 2, :].bitcast(F16)[:, 0:512]
                                       .rearrange("p (g t) -> p g t", g=4), ACT.Copy)\
                            .then_inc(q_stack, 1)

                    for piece, j in ((high, 0), (high, 1), (queries, 0), (queries, 1), (high, 2), (high, 3),
                                     (queries, 2), (queries, 3)):
                        yield from at_ticks(now, base + TOK[piece.__name__][j])
                        piece(j)

            def attention(now):
                for g, (part, b, i, hgs, kb, chunks, tick) in enumerate(GROUPS):
                    yield from at_ticks(now, tick + 1)
                    n = CH * len(chunks) * len(hgs)
                    act.wait_ge(scores_ready, g + 1)
                    if g >= 4:
                        act.wait_ge(pv_done, g - 3)
                    act.activation(pr[:, g % 4, 0:n], score_bank(g)[1][:, 0:n], ACT.Exp, scale=SCALE)\
                        .then_inc(probs_ready, 1)

            def tail(j):
                def work(now):
                    sel, base, T = pair_tiles(j), tail_base(j), tail_of(j)

                    def squares(junk, src, name, ready):
                        for c in range(NC):
                            i = act.activation(junk[:, c, :], src[:, c, :], ACT.Square,
                                               accum_out=st(name, tok_tile(c, j)))
                        i.then_inc(ready, 1)

                    def scaled(dst, src, name, ready):
                        for c in range(NC):
                            act.activation(dst[:, c, :], src[:, c, :], ACT.Copy,
                                           scale=st(name, tok_tile(c, j))).then_inc(ready, 1)

                    def of_bank(user):
                        return tail_bank(j, user).rearrange("p (c d) -> p c d", c=NC)

                    yield from at_ticks(now, base + T["oevac"])
                    act.wait_ge(oT_ps, j + 1)
                    act.activation(T_OT[j], of_bank("oT"), ACT.Copy).then_inc(oT_sb, 1)
                    yield from at_ticks(now, base + T["wosq"])
                    act.wait_ge(att_m, j + 1)
                    squares(T_F[j], of_bank("wo"), "osq", wo_sq)
                    if j < NJ - 1:
                        yield from at_ticks(now, base + T["asq"])
                        squares(T_R[j], T_M[j], "asq", att_sq)
                    yield from at_ticks(now, base + T["tanh"])
                    act.wait_ge(att_n, j + 1)
                    act.activation(st("ath", sel), st("an", sel), ACT.Tanh).then_inc(att_th, 1)
                    yield from at_ticks(now, base + T["ascale"])
                    act.wait_ge(att_co, j + 1)
                    scaled(T_X[j], T_M[j], "aQ", att_scaled)
                    yield from at_ticks(now, base + T["xn"])
                    act.wait_ge(v_rho, j + 1)
                    for c in (2, 3):
                        i = act.activation(T_O[j][:, c, :], T_X[j][:, c, :], ACT.Identity,
                                           scale=st("rho2", tok_tile(c, j)),
                                           bias=st("off2", tok_tile(c, j)))
                    i.then_inc(v_xn2, 1)
                    yield from at_ticks(now, base + T["uevac"])
                    act.wait_ge(v_uT_ps, j + 1)
                    act.activation(T_OT[j], of_bank("uT"), ACT.Copy).then_inc(v_uT, 1)
                    yield from at_ticks(now, base + T["usq"])
                    act.wait_ge(v_u, j + 1)
                    squares(T_F[j], T_O[j], "usq2", v_usq)
                    yield from at_ticks(now, base + T["f2sq"])
                    act.wait_ge(f2_y, j + 1)
                    squares(T_OT[j], T_F[j], "fsq2", f2_sq)
                    if j < NJ - 1:
                        yield from at_ticks(now, base + T["ffsq"])
                        act.wait_ge(ff_m, j + 1)
                        squares(T_O[j], T_M[j], "fsq3", ff_sq)
                    yield from at_ticks(now, base + T["fftanh"])
                    act.wait_ge(ff_n, j + 1)
                    act.activation(st("fth", sel), st("fn", sel), ACT.Tanh).then_inc(ff_th, 1)
                    if j < NJ - 1:
                        yield from at_ticks(now, base + T["ffscale"])
                        act.wait_ge(ff_co, j + 1)
                        scaled(T_R[j], T_M[j], "fQ", ff_scaled)
                return work

            tails = [tail(j) for j in range(NJ)]
            run(step, [prepare, tokens, attention, *tails])

        @block.vector
        def _(dve):
            done = [0]

            def done_(ins):
                done[0] += 1
                ins.then_inc(dve_done, 1)

            def settle():
                dve.wait_ge(dve_done, done[0])

            def settled(ins):
                done_(ins)
                settle()

            dve.memset(ones[:, :], 1.0)
            dve.memset(onesh[:, :], 1.0)
            dve.wait_ge(load_scan, 64)
            for k, off in ((0, D), (1, 0)):
                s = ZS * (1.0, 0.5)[k]
                dve.tensor_scalar(w0s[:, k, :], w0x[:, off:off + D], s, None, ALU.mult)
                dve.tensor_scalar(whs[:, 0, k, :], w0h[:, off:off + D], s / 4, None, ALU.mult)
                dve.tensor_scalar(whs[:, 1, k, :], w0h[:, off:off + D], s / 2, None, ALU.mult)
                done_(dve.tensor_scalar(b0s[:, k, :], b0row[:, off:off + D], s, (0.0, s)[k],
                                        ALU.mult, ALU.add))
            settle()
            settled(dve.tensor_copy(b0h[:, 0], b0s[:, :, :]))
            dve.tensor_tensor(b0h[:, 1], b0s[:, :, :], b0h[:, 0], ALU.subtract).then_inc(x_split, 1)
            settled(dve.tensor_copy(whh[:, 0], whs[:, :, :, :]))
            dve.tensor_tensor(whh[:, 1], whs[:, :, :, :], whh[:, 0], ALU.subtract).then_inc(w_split, 1)
            done_(dve.memset(prod[:, NB:2 * NB], 0.0))
            dve.wait_ge(condT_sb, 2)
            settled(dve.tensor_scalar(prod[:, 0:NB], state[:, 0:NB], 2.0, None, ALU.mult))
            done_(dve.tensor_copy(prod_hi[:, :], prod[:, :]))
            settle()
            dve.tensor_tensor(prod_lo[:, :], prod[:, :], prod_hi[:, :], ALU.subtract)\
                .then_inc(lo_ready, 1)
            dve.wait_ge(w_split, 1)
            dve.memset(tmp[:, 0, 0, 0:1], 0.0).then_inc(hi_ready, 1)

            def step(t):
                r = state[:, SW * t:SW * t + 32]
                dve.wait_ge(step_in, 2 * t + 1)
                if t < STEPS - 1:
                    dve.scalar_tensor_tensor(prod_hi[:, :], r[:, 16:32], 1.0, r[:, 0:16], ALU.add,
                                             ALU.mult).then_inc(hi_ready, 1)
                dve.scalar_tensor_tensor(prod[:, :], r[:, 16:32], 1.0, r[:, 0:16], ALU.add,
                                         ALU.mult).then_inc(products, 1)
                dve.wait_ge(products, t + 1)
                if t < STEPS - 1:
                    dve.tensor_tensor(prod_lo[:, :], prod[:, :], prod_hi[:, :], ALU.subtract)\
                        .then_inc(lo_ready, 1)
                dve.scalar_tensor_tensor(state[:, SW * (t + 1):SW * (t + 1) + NB], prod[:, 0:NB], 0.5,
                                         prod[:, NB:2 * NB], ALU.mult, ALU.add).then_inc(step_in, 1)

            def prepare(now):
                yield from at_ticks(now, 12)
                dve.wait_ge(load_rest, LOADS_REST)
                rows = view(bor[:, 0:1], [0, NC], [1, D])
                settled(dve.tensor_copy(boh[:, 0], rows))
                dve.tensor_tensor(boh[:, 1], rows, boh[:, 0], ALU.subtract).then_inc(bo_split, 1)
                yield

            def artanh(k, sel, tag, wait, ready, per_piece):
                c = st("cl" + tag, sel)
                size = c.free_size()
                om, op, w, ef, lo, hi_, z, d, zz, l = (tmp[:, k, i, 0:size] for i in range(10))
                eb, mb = itmp[:, k, 0, 0:size], itmp[:, k, 1, 0:size]
                r2, half = math.sqrt(2.0), 0.5 * math.log(2.0)
                n = 0
                dve.wait_ge(*wait)
                chain = (
                    (lambda: dve.tensor_scalar(om, c, -1.0, 1.0, ALU.mult, ALU.add), 0),
                    (lambda: dve.tensor_scalar(op, c, r2, r2, ALU.mult, ALU.add), 1),
                    (lambda: dve.reciprocal(om, om), 1),
                    (lambda: dve.tensor_tensor(w, op, om, ALU.mult), 1),
                    (lambda: dve.tensor_scalar(mb, w.bitcast(I32), 0x7FFFFF, 0x3F800000,
                                               ALU.bitwise_and, ALU.bitwise_or), 0),
                    (lambda: dve.tensor_scalar(eb, w.bitcast(I32), 23, None,
                                               ALU.logical_shift_right), 1),
                    (lambda: dve.tensor_scalar(hi_, mb.bitcast(F32), r2, None, ALU.add), 0),
                    (lambda: dve.tensor_scalar(lo, mb.bitcast(F32), -r2, None, ALU.add), 1),
                    (lambda: dve.reciprocal(hi_, hi_), 0),
                    (lambda: dve.tensor_scalar(ef, eb, -127.0, half, ALU.add, ALU.mult), 1),
                    (lambda: dve.tensor_tensor(z, lo, hi_, ALU.mult), 1),
                    (lambda: dve.tensor_tensor(d, c, z, ALU.subtract), 1),
                    (lambda: dve.scalar_tensor_tensor(d, eb, 127.5, d, ALU.is_lt, ALU.mult), 1),
                    (lambda: dve.tensor_tensor(z, z, d, ALU.add), 1),
                    (lambda: dve.tensor_tensor(zz, z, z, ALU.mult), 1),
                    (lambda: dve.tensor_scalar(l, zz, 1.0 / 9, 1.0 / 7, ALU.mult, ALU.add), 1),
                    (lambda: dve.tensor_tensor(l, l, zz, ALU.mult), 1),
                    (lambda: dve.scalar_tensor_tensor(l, l, 1.0 / 5, zz, ALU.add, ALU.mult), 1),
                    (lambda: dve.scalar_tensor_tensor(l, l, 1.0 / 3, zz, ALU.add, ALU.mult), 1),
                    (lambda: dve.scalar_tensor_tensor(l, l, 1.0, z, ALU.add, ALU.mult), 1),
                    (lambda: dve.tensor_tensor(l, l, ef, ALU.add), 1),
                    (lambda: dve.tensor_tensor(l, l, l, ALU.mult), 1),
                    (lambda: dve.reciprocal(l, l), 1),
                    (lambda: dve.tensor_tensor(l, l, st("ss" + tag, sel), ALU.mult), 1))
                for op_, waits in chain:
                    done_(op_())
                    if waits:
                        settle()
                        n += 1
                        if n % per_piece == 0:
                            yield
                dve.scalar_tensor_tensor(st("va" + tag, sel), l, LN_EPS, mv[:, min(k, 1), sel, 1],
                                         ALU.mult, ALU.add).then_inc(ready, 1)

            def tokens(now):
                for c in range(NC):
                    base, sel = tok_base(c), tok_tiles(c)
                    yield from at_ticks(now, base + TOK["resid"])
                    dve.wait_ge(h_transposed, c + 1)
                    dve.wait_ge(xT_ps, NC)
                    for q in range(2):
                        r = resid[:, NJ * c + 2 * q:NJ * c + 2 * q + 2, :]
                        done_(dve.scalar_tensor_tensor(
                            r, tb[:, 0, 256 * q:256 * q + 256].rearrange("p (j t) -> p j t", j=2), 0.5,
                            r, ALU.mult, ALU.add))
                        yield
                    yield from at_ticks(now, base + TOK["moments"])
                    settle()
                    for j in range(NJ):
                        done_(dve.bn_stats(bnst[:, j, :], resid[:, NJ * c + j, :]))
                        if j % 2:
                            yield
                    settle()
                    for j in range(NJ):
                        i = dve.bn_aggr(mv[:, 0, NC * j + c, :], bnst[:, j, :])
                    i.then_inc(tok_moments, 1)
                    yield from at_ticks(now, base + TOK["artanh"])
                    yield from artanh(0, sel, "1", (tok_norm, c + 1), tok_a, 3 if c < NC - 1 else 99)
                    yield from at_ticks(now, base + TOK["modulate"])
                    if c == 0:
                        dve.wait_ge(mod_in, 64)
                    dve.wait_ge(tok_xn, c + 1)
                    settled(dve.tensor_tensor(tu[:, 2:4, :], tu[:, 2:4, :], mod[:, c & 1, 2:4, D:2 * D],
                                              ALU.mult))
                    yield
                    dve.tensor_tensor(tu[:, 2:4, :], tu[:, 2:4, :], mod[:, c & 1, 2:4, 0:D],
                                      ALU.add).then_inc(tok_u2, 1)
                    for j in range(NJ):
                        n = NJ * c + j
                        yield from at_ticks(now, base + TOK["yevac"] + 2 * j)
                        dve.wait_ge(qkv_ps, n + 1)
                        if j == 0:
                            dve.wait_ge(tok_clip, c + 1)
                            if c:
                                dve.wait_ge(v_scaled, NJ * c)
                        dve.scalar_tensor_tensor(y[:, j, :], tb[:, j % 2, 0:3 * D],
                                                 st("uclip1", tok_tile(c, j)), bqkvb[:, :], ALU.mult,
                                                 ALU.add).then_inc(qkv_copied, 1)
                        if j:
                            yield from at_ticks(now, base + TOK["qreduce"] + 2 * (j - 1))
                            yield from head_sums(c, j - 1)
                    yield from at_ticks(now, base + TOK["qreduce"] + 2 * (NJ - 1))
                    yield from head_sums(c, NJ - 1)

                    def scale(j, _):
                        if j % 2 == 0:
                            q = j // 2
                            if (c, q) == (NC - 1, 1):
                                settle()
                            else:
                                dve.wait_ge(roots, 2 * c + q + 1)
                            dve.scalar_tensor_tensor(
                                hfac[:, q, :].rearrange("p (a h) -> p a h", h=NH),
                                hy[:, q, 0:NH2].rearrange("p (a h) -> p a h", h=NH), M_CLIP,
                                view(ht[:, q, NH2:NH2 + 1], [1, 6], [0, NH]), ALU.mult, ALU.min)\
                                .then_inc(factors, 1)
                            dve.wait_ge(factors, 2 * c + q + 1)
                        yh = y[:, j, 0:2 * D].rearrange("p (h d) -> p h d", d=HD)
                        f = view(hfac[:, j // 2, 48 * (j % 2):48 * (j % 2) + 1], [1, 2 * NH], [0, HD])
                        dve.tensor_tensor(yh, yh, f, ALU.mult).then_inc(qk_scaled, 1)

                    def low(j, k):
                        n = NJ * c + j
                        dve.wait_ge(split_high, n + 1)
                        src = view(y[:, j, D * k:D * k + 1], [HD, NH], [0, 2], [1, HD])
                        q0 = view(qs[:, n % 2, k, 0, 0, 0:1], [4 * HD, NH], [(2, 1)[k] * HD, 2], [1, HD])
                        q1 = view(qs[:, n % 2, k, 0, (1, 2)[k], 0:1], [4 * HD, NH],
                                  [(2, 1)[k] * HD, 2], [1, HD])
                        ins = dve.tensor_tensor(q1, src, q0, ALU.subtract)
                        if k:
                            ins.then_inc(split_low, 1)

                    def keys(j, _):
                        dve.wait_ge(q_stack, NJ * c + j + 1)
                        other = 2 * P * (batch_of(c, j, 1) - batch_of(c, j, 0)) + CH
                        dst = view(KT[:, 0, batch_of(c, j, 0), c // 2, 0:1], [NB * 2 * P, 4],
                                   [other, 2], [1, CH])
                        dve.tensor_copy(dst, tb[:, j % 2, :].bitcast(F16)[:, 512:1024]
                                        .rearrange("p (g s t) -> p g s t", g=4, s=2))\
                            .then_inc(k_stack, 1)

                    for piece, j in ((scale, 0), (scale, 1), (low, 0), (low, 1), (scale, 2), (scale, 3),
                                     (keys, 0), (keys, 1), (low, 2), (low, 3), (keys, 2), (keys, 3)):
                        yield from at_ticks(now, base + TOK[piece.__name__][j])
                        piece(j, 0)
                        if piece is low:
                            yield
                            piece(j, 1)

            def head_sums(c, j):
                n, q = NJ * c + j, j // 2
                dve.wait_ge(qkv_squared, n + 1)
                dve.tensor_reduce(hsum[:, q, 48 * (j % 2):48 * (j % 2) + 48],
                                  ysq[:, n % 2, :].rearrange("p (h d) -> p h d", d=HD), AX.X,
                                  ALU.add).then_inc(qkv_reduced, 1)
                if j % 2 == 0:
                    return
                yield
                dve.wait_ge(qkv_reduced, n + 1)
                done_(dve.tensor_reduce(hsum[:, q, NH2:NA2],
                                        hsum[:, q, 0:NH2].rearrange("p (a h) -> p a h", h=NH), AX.X,
                                        ALU.add))
                settle()
                dve.tensor_scalar(hi32[:, q, :], hsum[:, q, :].bitcast(I32), 1, None,
                                  ALU.logical_shift_right).then_inc(factor_bits, 1)
                if (c, q) == (NC - 1, 1):
                    dve.wait_ge(factor_bits, 2 * c + q + 1)
                    done_(head_factors(dve, q, settled, True))

            def attention(now):
                for g, (part, b, i, hgs, *_rest) in enumerate(GROUPS):
                    if i < NI - 1 or part == 2 and hgs != (2, 3):
                        continue
                    nxt = g + 1 if part < 2 else min(g + 3, len(GROUPS) - 1)
                    tick = GROUPS[nxt][6] if g + 1 < len(GROUPS) else GROUPS[g][6] + 2
                    yield from at_ticks(now, tick + 1)
                    dve.wait_ge(pv_done, g + 1)
                    s, j = b % 2, b // 2
                    bank = o_bank(part, b)
                    if part < 2:
                        chunks = (0, 1) if part == 0 else (2,)
                        n = CH * len(chunks)
                        first = q_cols(O[:, j, 0, :], b, chunks)
                        dst = view(first, [NC * P, 2], *[list(d) for d in list(first.ap)[1:]])
                        src = view(bank[:, 0:1], [P, 2], [CH, len(chunks)], [1, CH])
                        if part == 1:
                            src = view(bank[:, 0:1], [P, 2], [1, CH])
                        dve.tensor_copy(dst, src).then_inc(o_saved, 1)
                    else:
                        if b == 0:
                            dve.wait_ge(o_saved, 2 * NB)
                        dst = view(O[:, j, 0, CH * s:CH * s + 1], [2 * P, 4], [CH * (3 - 2 * s), 2],
                                   [1, CH])
                        dve.tensor_tensor(dst, bank.rearrange("p (a c q) -> p a c q", a=4, c=2),
                                          dst, ALU.add).then_inc(o_saved, 1)

            def mobius(j, sel, pre, dots, x2s, clip):
                tau, xy, y2, al, den, w = (tmp[:, 1 + j, i, :] for i in range(12, 18))
                th = st(pre + "th", sel)
                done_(dve.tensor_tensor(tau, th, st(pre + "rn", sel), ALU.mult))
                done_(dve.tensor_tensor(y2, th, th, ALU.mult))
                settle()
                done_(dve.tensor_tensor(tau, tau, clip, ALU.mult))
                done_(dve.tensor_tensor(den, x2s, y2, ALU.mult))
                settle()
                done_(dve.tensor_tensor(xy, dots, tau, ALU.mult))
                done_(dve.tensor_scalar(w, x2s, -1.0, 1.0, ALU.mult, ALU.add))
                settle()
                done_(dve.tensor_scalar(xy, xy, 2.0, 1.0, ALU.mult, ALU.add))
                done_(dve.tensor_tensor(w, w, tau, ALU.mult))
                settle()
                done_(dve.tensor_tensor(den, den, xy, ALU.add))
                done_(dve.tensor_tensor(al, xy, y2, ALU.add))
                settle()
                settled(dve.tensor_scalar(den, den, EPS, None, ALU.max))
                settled(dve.reciprocal(den, den))
                done_(dve.tensor_tensor(st(pre + "P", sel), al, den, ALU.mult))
                return dve.tensor_tensor(st(pre + "Q", sel), w, den, ALU.mult)

            def tail(j):
                def work(now):
                    sel, base, T = pair_tiles(j), tail_base(j), tail_of(j)

                    def sec(s):
                        return view(mod[:, 0, j, D * s:D * s + 1], [0, 2], [NJ * 6 * D, 2], [1, D])

                    def by_parity(ap):
                        return ap.rearrange("p (a b) d -> p a b d", a=2)

                    def of_bank(user):
                        return tail_bank(j, user).rearrange("p (c d) -> p c d", c=NC)

                    def dots(name, junk, a, b, ready):
                        for c in range(NC):
                            ins = dve.tensor_tensor_reduce(junk[:, c, :], a[:, c, :], b[:, c, :], 1.0,
                                                           0.0, ALU.mult, ALU.add,
                                                           st(name, tok_tile(c, j)))
                        ins.then_inc(ready, 1)

                    x1 = view(resid[:, j, 0:1], [NJ * D, NC], [1, D])
                    for q in range(2):
                        yield from at_ticks(now, base + T["o"][q])
                        dve.wait_ge(ot_ps, 2 * j + q + 1)
                        r, b = rec[:, j, q, :], tail_bank(j, f"ot{q}")
                        settled(dve.reciprocal(view(r[:, 0:1], [8, 4], [2, 4], [1, 2]),
                                               view(b[:, HD:HD + 1], [P, 4], [VW, 4], [VC, 2])))
                        for c in (2 * q, 2 * q + 1):
                            dst = view(T_O[j][:, c, 0:1], [2 * HD, 2], [4 * HD, 4], [HD, 2], [1, HD])
                            src = view(b[:, 2 * P * (c % 2):2 * P * (c % 2) + 1], [P, 2], [VW, 4],
                                       [VC, 2], [1, HD])
                            f = view(r[:, 16 * (c % 2):16 * (c % 2) + 1], [8, 2], [2, 4], [1, 2],
                                     [0, HD])
                            dve.tensor_tensor(dst, src, f, ALU.mult).then_inc(o_ready, 1)
                    yield from at_ticks(now, base + T["m"])
                    dve.wait_ge(wo_ps, j + 1)
                    dve.tensor_tensor(by_parity(T_M[j]), by_parity(of_bank("wo")), sec(2), ALU.mult)\
                        .then_inc(att_m, 1)
                    yield from at_ticks(now, base + T["adot"])
                    dve.wait_ge(att_m, j + 1)
                    if j == NJ - 1:
                        dots("asq", T_R[j], T_M[j], T_M[j], att_sq)
                    dots("adot", T_X[j], T_M[j], x1, att_dot)
                    yield from at_ticks(now, base + T["mob"])
                    dve.wait_ge(att_dot, j + 1)
                    dve.wait_ge(att_th, j + 1)
                    mobius(j, sel, "a", st("adot", sel), st("ss1", sel), st("oclip", sel))\
                        .then_inc(att_co, 1)
                    yield from at_ticks(now, base + T["x2"])
                    dve.wait_ge(att_co, j + 1)
                    for c in range(NC):
                        x = T_X[j][:, c, :]
                        dve.wait_ge(att_scaled, NC * j + c + 1)
                        done_(dve.scalar_tensor_tensor(x, x1[:, c, :], st("aP", tok_tile(c, j)), x,
                                                       ALU.mult, ALU.add))
                    settle()
                    for c in range(NC):
                        done_(dve.bn_stats(bnst2[:, j, c, :], T_X[j][:, c, :]))
                    settle()
                    for c in range(NC):
                        ins = dve.bn_aggr(mv[:, 1, NC * j + c, :], bnst2[:, j, c, :])
                    ins.then_inc(v_moments, 1)
                    yield from at_ticks(now, base + T["artanh"])
                    yield from artanh(1 + j, sel, "2", (v_norm, j + 1), v_a, 2 if j < NJ - 1 else 99)
                    yield from at_ticks(now, base + T["modulate"])
                    dve.wait_ge(v_xn, j + 1)
                    dve.wait_ge(v_xn2, j + 1)
                    u = by_parity(T_O[j])
                    settled(dve.tensor_tensor(u, u, sec(4), ALU.mult))
                    dve.tensor_tensor(u, u, sec(3), ALU.add).then_inc(v_u, 1)
                    yield from at_ticks(now, base + T["gdot"])
                    dve.wait_ge(g_ps, j + 1)
                    dve.wait_ge(v_u, j + 1)
                    dots("gdot", T_R[j], of_bank("g"), T_O[j], f1_dot)
                    yield from at_ticks(now, base + T["f1"])
                    dve.wait_ge(f1_dot, j + 1)
                    dve.wait_ge(t2_ps, j + 1)
                    dve.wait_ge(v_clip, j + 1)
                    f = st("fsq1", sel)
                    settled(dve.tensor_tensor(f, st("gdot", sel), st("uclip2", sel), ALU.mult))
                    settled(dve.tensor_tensor(f, tail_bank(j, "t2")[:, 0:NC], f, ALU.add))
                    settled(dve.tensor_tensor(f, f, st("uclip2", sel), ALU.mult))
                    dve.tensor_scalar(f, f, b12[:, D:D + 1], None, ALU.add).then_inc(f1_sum, 1)
                    yield from at_ticks(now, base + T["gyevac"])
                    dve.wait_ge(gy_ps, j + 1)
                    for c in range(NC):
                        ins = dve.scalar_tensor_tensor(T_F[j][:, c, :], of_bank("gy")[:, c, :],
                                                       st("uclip2", tok_tile(c, j)), b12[:, 0:D],
                                                       ALU.mult, ALU.add)
                    ins.then_inc(gy_saved, 1)
                    yield from at_ticks(now, base + T["f2"])
                    dve.wait_ge(gy_saved, j + 1)
                    dve.wait_ge(f1_clip, j + 1)
                    for c in range(NC):
                        ins = dve.scalar_tensor_tensor(T_F[j][:, c, :], T_F[j][:, c, :],
                                                       st("fc1", tok_tile(c, j)), b2b[:, :],
                                                       ALU.mult, ALU.add)
                    ins.then_inc(f2_y, 1)
                    dve.wait_ge(f2_y, j + 1)
                    dve.tensor_tensor(by_parity(T_M[j]), by_parity(T_F[j]), sec(5), ALU.mult)\
                        .then_inc(ff_m, 1)
                    yield from at_ticks(now, base + T["fdot"])
                    dve.wait_ge(ff_m, j + 1)
                    if j == NJ - 1:
                        dots("fsq3", T_O[j], T_M[j], T_M[j], ff_sq)
                    dots("fdot", T_R[j], T_M[j], T_X[j], ff_dot)
                    yield from at_ticks(now, base + T["mob2"])
                    dve.wait_ge(ff_dot, j + 1)
                    dve.wait_ge(ff_th, j + 1)
                    mobius(j, sel, "f", st("fdot", sel), st("ss2", sel), st("fclip", sel))\
                        .then_inc(ff_co, 1)
                    yield from at_ticks(now, base + T["out"])
                    dve.wait_ge(ff_co, j + 1)
                    if j == NJ - 1:
                        for q in range(2):
                            for c in (q, q + 2):
                                done_(dve.scalar_tensor_tensor(T_R[j][:, c, :], T_M[j][:, c, :],
                                                               st("fQ", tok_tile(c, j)), x1[:, c, :],
                                                               ALU.mult, ALU.add))
                            settle()
                            for c in (q, q + 2):
                                i = dve.scalar_tensor_tensor(T_R[j][:, c, :], T_X[j][:, c, :],
                                                             st("fP", tok_tile(c, j)), T_R[j][:, c, :],
                                                             ALU.mult, ALU.add)
                            i.then_inc(last_out, 1)
                        return
                    for c in range(NC):
                        dve.wait_ge(ff_scaled, NC * j + c + 1)
                        dve.scalar_tensor_tensor(T_R[j][:, c, :], T_X[j][:, c, :],
                                                 st("fP", tok_tile(c, j)), T_R[j][:, c, :], ALU.mult,
                                                 ALU.add).then_inc(block_out, 1)
                return work

            tails = [tail(j) for j in range(NJ)]
            run(step, [prepare, tokens, attention, *tails])


_INS = ['x', 'cond_1024', 'L0_cond_weight', 'L0_cond_bias', 'L1_cond_w_q', 'L1_cond_b_q', 'L1_cond_w_k',
        'L1_cond_b_k', 'L1_cond_w_v', 'L1_cond_b_v', 'L1_cond_w_o', 'L1_cond_b_o', 'L1_cond_w_f1',
        'L1_cond_b_f1', 'L1_cond_w_f2', 'L1_cond_b_f2', 'L1_cond_w_ada', 'L1_cond_b_ada']


def kernel(**inputs):
    import concourse.bacc as _bacc
    from concourse.bass_utils import run_bass_kernel_spmd as _run

    nc = _bacc.Bacc("TRN2", target_bir_lowering=False, num_devices=1)
    arrays, args = {}, []
    for name in _INS:
        a = np.ascontiguousarray(inputs[name])
        arrays[f"in_{name}_dram"] = a
        args.append(nc.dram_tensor(f"in_{name}_dram", a.shape, mybir.dt.from_np(a.dtype),
                                   kind="ExternalInput").ap())
    args.append(nc.dram_tensor("out_0_dram", (NB, STEPS, D), F32, kind="ExternalOutput").ap())
    ugrnn_block_kernel(nc, *args)
    r = _run(nc, [arrays], core_ids=[0])
    return r.results[0]["out_0_dram"]
```
